# Optimizing a Trainium2 kernel written in Bass

```python
import numpy as np
import jax
import jax.numpy as jnp

def _softmax(x, axis=-1):
    return jax.nn.softmax(x, axis=axis)

def _gelu(x):
    return jax.nn.gelu(x, approximate=True)

def _silu(x):
    return jax.nn.silu(x)

def _sigmoid(x):
    return jax.nn.sigmoid(x)

def _layernorm(x, axis=-1, eps=1e-05):
    m = jnp.mean(x, axis=axis, keepdims=True)
    v = jnp.var(x, axis=axis, keepdims=True)
    return (x - m) / jnp.sqrt(v + eps)

def _scatter_add(tgt, idx, src, axis=0):
    return tgt.at[idx].add(src)

def _segment_sum(src, seg, n):
    return jax.ops.segment_sum(src, seg, n)
kernel_name = 'mk_macaron_d2_jaxref_r8_aebe3e'

def setup_inputs(seed: int=0):
    np.random.seed(seed)
    _w = jnp.asarray

    def _L0_attn_setup():
        import jax, jax.numpy as jnp
        import numpy as np
        D_MODEL = 256
        N_HEADS = 16
        SEQ_LEN = 256
        BATCH = 2
        BIAS_MAX = 8.0

        def alibi_bias(n_heads, seq_len, dtype):
            pos = jnp.arange(1 - seq_len, 1, dtype=dtype)
            m = jnp.arange(1, n_heads + 1, dtype=dtype) * (BIAS_MAX / n_heads)
            slopes = 1.0 / 2.0 ** m
            return pos[None, :] * slopes[:, None]
        key = jax.random.key(seed)
        k1, k2, k3 = jax.random.split(key, 3)
        s = 1.0 / np.sqrt(D_MODEL)
        x = jax.random.normal(k1, (BATCH, SEQ_LEN, D_MODEL), dtype=jnp.float32)
        Wqkv = jax.random.normal(k2, (3 * D_MODEL, D_MODEL), dtype=jnp.float32) * s
        b_qkv = jnp.zeros((3 * D_MODEL,), dtype=jnp.float32)
        Wout = jax.random.normal(k3, (D_MODEL, D_MODEL), dtype=jnp.float32) * s
        b_out = jnp.zeros((D_MODEL,), dtype=jnp.float32)
        return {'x': x, 'Wqkv': Wqkv, 'b_qkv': b_qkv, 'Wout': Wout, 'b_out': b_out}
    _L0_attn_in = _L0_attn_setup()

    def _L0_ffn_setup():
        import jax, jax.numpy as jnp
        import numpy as np
        HIDDEN = 256
        INTER = 688
        LUT_SIZE = 16

        def _ghost_linear(x, idx, lut):
            w = lut[idx]
            return jnp.einsum('bsh,oh->bso', x, w)
        key = jax.random.key(seed)
        k_x, k_lut, k_g, k_u, k_d = jax.random.split(key, 5)
        x = jax.random.normal(k_x, (2, 512, HIDDEN), dtype=jnp.float32)
        lut = jax.random.normal(k_lut, (LUT_SIZE,), dtype=jnp.float32) * 0.02
        gate_idx = jax.random.randint(k_g, (INTER, HIDDEN), 0, LUT_SIZE, dtype=jnp.int32)
        up_idx = jax.random.randint(k_u, (INTER, HIDDEN), 0, LUT_SIZE, dtype=jnp.int32)
        down_idx = jax.random.randint(k_d, (HIDDEN, INTER), 0, LUT_SIZE, dtype=jnp.int32)
        return {'x': x, 'lut': lut, 'gate_idx': gate_idx, 'up_idx': up_idx, 'down_idx': down_idx}
    _L0_ffn_in = _L0_ffn_setup()

    def _L1_attn_setup():
        import jax, jax.numpy as jnp
        import numpy as np
        B, T, C = (2, 256, 256)
        NH, NKV = (16, 4)
        HD = C // NH

        def _rope(x):
            D = x.shape[-1]
            t = x.shape[-2]
            inv_freq = 1.0 / 10000.0 ** (jnp.arange(0, D, 2, dtype=jnp.float32) / D)
            freqs = jnp.arange(t, dtype=jnp.float32)[:, None] * inv_freq[None, :]
            emb = jnp.concatenate([freqs, freqs], axis=-1)
            cos, sin = (jnp.cos(emb), jnp.sin(emb))
            x1, x2 = (x[..., :D // 2], x[..., D // 2:])
            rotated = jnp.concatenate([-x2, x1], axis=-1)
            return x * cos + rotated * sin
        key = jax.random.key(seed)
        ks = jax.random.split(key, 5)
        w = lambda k, shape: jax.random.normal(k, shape, jnp.float32) * 0.02
        return {'x': jax.random.normal(ks[0], (B, T, C), jnp.float32), 'Wq': w(ks[1], (C, C)), 'Wk': w(ks[2], (C, NKV * HD)), 'Wv': w(ks[3], (C, NKV * HD)), 'Wproj': w(ks[4], (C, C))}
    _L1_attn_in = _L1_attn_setup()

    def _L1_ffn_setup():
        import jax, jax.numpy as jnp
        import numpy as np
        D_MODEL, D_FF, NS, NR, KR = (256, 176, 2, 16, 4)
        B, S = (4, 256)

        def _moe_forward(u, shared_w1, shared_b1, shared_w2, shared_b2, routed_w1, routed_b1, routed_w2, routed_b2, centroids, bias):
            b, s, d = u.shape
            flat = u.reshape(-1, d)
            T = flat.shape[0]
            h = jax.nn.relu(jnp.einsum('td,ndf->ntf', flat, shared_w1) + shared_b1[:, None, :])
            shared_out = jnp.einsum('ntf,nfd->td', h, shared_w2) + shared_b2.sum(0)
            out = flat + shared_out
            scores = jax.nn.sigmoid(flat @ centroids.T) + bias
            vals, idx = jax.lax.top_k(scores, KR)
            gating = jnp.zeros_like(scores).at[jnp.arange(T)[:, None], idx].set(vals)
            gating = gating / jnp.clip(gating.sum(-1, keepdims=True), 1e-08)

            def step(acc, ew):
                w1, b1, w2, b2, g = ew
                hj = jax.nn.relu(flat @ w1 + b1)
                yj = hj @ w2 + b2
                return (acc + yj * g[:, None], None)
            rout0 = jnp.zeros_like(flat)
            rout, _ = jax.lax.scan(step, rout0, (routed_w1, routed_b1, routed_w2, routed_b2, gating.T))
            return (out + rout).reshape(b, s, d)
        key = jax.random.key(seed)
        ks = jax.random.split(key, 10)
        s1 = 1.0 / np.sqrt(D_MODEL)
        s2 = 1.0 / np.sqrt(D_FF)
        return {'u': jax.random.normal(ks[0], (B, S, D_MODEL), dtype=jnp.float32), 'shared_w1': jax.random.normal(ks[1], (NS, D_MODEL, D_FF), dtype=jnp.float32) * s1, 'shared_b1': jnp.zeros((NS, D_FF), dtype=jnp.float32), 'shared_w2': jax.random.normal(ks[2], (NS, D_FF, D_MODEL), dtype=jnp.float32) * s2, 'shared_b2': jnp.zeros((NS, D_MODEL), dtype=jnp.float32), 'routed_w1': jax.random.normal(ks[3], (NR, D_MODEL, D_FF), dtype=jnp.float32) * s1, 'routed_b1': jnp.zeros((NR, D_FF), dtype=jnp.float32), 'routed_w2': jax.random.normal(ks[4], (NR, D_FF, D_MODEL), dtype=jnp.float32) * s2, 'routed_b2': jnp.zeros((NR, D_MODEL), dtype=jnp.float32), 'centroids': jax.random.normal(ks[5], (NR, D_MODEL), dtype=jnp.float32) * s1, 'bias': jnp.zeros((NR,), dtype=jnp.float32)}
    _L1_ffn_in = _L1_ffn_setup()
    _d = {'L0_attn_x': _L0_attn_in['x'], 'L0_attn_Wqkv': _L0_attn_in['Wqkv'], 'L0_attn_b_qkv': _L0_attn_in['b_qkv'], 'L0_attn_Wout': _L0_attn_in['Wout'], 'L0_attn_b_out': _L0_attn_in['b_out'], 'L0_ffn_lut': _L0_ffn_in['lut'], 'L0_ffn_gate_idx': _L0_ffn_in['gate_idx'], 'L0_ffn_up_idx': _L0_ffn_in['up_idx'], 'L0_ffn_down_idx': _L0_ffn_in['down_idx'], 'L1_attn_Wq': _L1_attn_in['Wq'], 'L1_attn_Wk': _L1_attn_in['Wk'], 'L1_attn_Wv': _L1_attn_in['Wv'], 'L1_attn_Wproj': _L1_attn_in['Wproj'], 'L1_ffn_shared_w1': _L1_ffn_in['shared_w1'], 'L1_ffn_shared_b1': _L1_ffn_in['shared_b1'], 'L1_ffn_shared_w2': _L1_ffn_in['shared_w2'], 'L1_ffn_shared_b2': _L1_ffn_in['shared_b2'], 'L1_ffn_routed_w1': _L1_ffn_in['routed_w1'], 'L1_ffn_routed_b1': _L1_ffn_in['routed_b1'], 'L1_ffn_routed_w2': _L1_ffn_in['routed_w2'], 'L1_ffn_routed_b2': _L1_ffn_in['routed_b2'], 'L1_ffn_centroids': _L1_ffn_in['centroids'], 'L1_ffn_bias': _L1_ffn_in['bias']}
    _x0 = _d['L0_attn_x']
    _d['L0_attn_x'] = jax.random.normal(jax.random.fold_in(jax.random.key(seed), 1), (4, 512, 256), dtype=_x0.dtype)
    del _x0
    return _d

def reference(L0_attn_x, L0_attn_Wqkv, L0_attn_b_qkv, L0_attn_Wout, L0_attn_b_out, L0_ffn_lut, L0_ffn_gate_idx, L0_ffn_up_idx, L0_ffn_down_idx, L1_attn_Wq, L1_attn_Wk, L1_attn_Wv, L1_attn_Wproj, L1_ffn_shared_w1, L1_ffn_shared_b1, L1_ffn_shared_w2, L1_ffn_shared_b2, L1_ffn_routed_w1, L1_ffn_routed_b1, L1_ffn_routed_w2, L1_ffn_routed_b2, L1_ffn_centroids, L1_ffn_bias):

    def _L0_attn_ref(x, Wqkv, b_qkv, Wout, b_out):
        import jax, jax.numpy as jnp
        import numpy as np
        D_MODEL = 256
        N_HEADS = 16
        SEQ_LEN = 256
        BATCH = 2
        BIAS_MAX = 8.0

        def alibi_bias(n_heads, seq_len, dtype):
            pos = jnp.arange(1 - seq_len, 1, dtype=dtype)
            m = jnp.arange(1, n_heads + 1, dtype=dtype) * (BIAS_MAX / n_heads)
            slopes = 1.0 / 2.0 ** m
            return pos[None, :] * slopes[:, None]
        B, S, D = x.shape
        H = N_HEADS
        hd = D // H
        scale = 1.0 / jnp.sqrt(jnp.asarray(hd, dtype=x.dtype))
        qkv = x @ Wqkv.T + b_qkv
        q, k, v = jnp.split(qkv, 3, axis=-1)
        q = q.reshape(B, S, H, hd)
        k = k.reshape(B, S, H, hd)
        v = v.reshape(B, S, H, hd)
        scores = jnp.einsum('bqhd,bkhd->bhqk', q, k) * scale
        bias = alibi_bias(H, S, x.dtype)
        scores = scores + bias[None, :, None, :]
        causal = jnp.tril(jnp.ones((S, S), dtype=bool))
        scores = jnp.where(causal[None, None, :, :], scores, jnp.asarray(-1000000000.0, dtype=x.dtype))
        p = jax.nn.softmax(scores, axis=-1)
        ctx = jnp.einsum('bhqk,bkhd->bqhd', p, v).reshape(B, S, D)
        return ctx @ Wout.T + b_out

    def _L0_ffn_ref(x, lut, gate_idx, up_idx, down_idx):
        import jax, jax.numpy as jnp
        import numpy as np
        HIDDEN = 256
        INTER = 688
        LUT_SIZE = 16

        def _ghost_linear(x, idx, lut):
            w = lut[idx]
            return jnp.einsum('bsh,oh->bso', x, w)
        gate = _ghost_linear(x, gate_idx, lut)
        up = _ghost_linear(x, up_idx, lut)
        h = jax.nn.silu(gate) * up
        return _ghost_linear(h, down_idx, lut)

    def _L1_attn_ref(x, Wq, Wk, Wv, Wproj):
        import jax, jax.numpy as jnp
        import numpy as np
        B, T, C = (2, 256, 256)
        NH, NKV = (16, 4)
        HD = C // NH

        def _rope(x):
            D = x.shape[-1]
            t = x.shape[-2]
            inv_freq = 1.0 / 10000.0 ** (jnp.arange(0, D, 2, dtype=jnp.float32) / D)
            freqs = jnp.arange(t, dtype=jnp.float32)[:, None] * inv_freq[None, :]
            emb = jnp.concatenate([freqs, freqs], axis=-1)
            cos, sin = (jnp.cos(emb), jnp.sin(emb))
            x1, x2 = (x[..., :D // 2], x[..., D // 2:])
            rotated = jnp.concatenate([-x2, x1], axis=-1)
            return x * cos + rotated * sin
        b, t, c = x.shape
        q = (x @ Wq).reshape(b, t, NH, HD).transpose(0, 2, 1, 3)
        k = (x @ Wk).reshape(b, t, NKV, HD).transpose(0, 2, 1, 3)
        v = (x @ Wv).reshape(b, t, NKV, HD).transpose(0, 2, 1, 3)
        q = _rope(q)
        k = _rope(k)
        rep = NH // NKV
        k = jnp.repeat(k, rep, axis=1)
        v = jnp.repeat(v, rep, axis=1)
        scale = 1.0 / jnp.sqrt(jnp.float32(HD))
        scores = jnp.einsum('bhqd,bhkd->bhqk', q, k) * scale
        causal = jnp.tril(jnp.ones((t, t), dtype=bool))
        scores = jnp.where(causal, scores, jnp.finfo(scores.dtype).min)
        attn = jax.nn.softmax(scores, axis=-1)
        y = jnp.einsum('bhqk,bhkd->bhqd', attn, v)
        y = y.transpose(0, 2, 1, 3).reshape(b, t, c)
        return y @ Wproj

    def _L1_ffn_ref(u, shared_w1, shared_b1, shared_w2, shared_b2, routed_w1, routed_b1, routed_w2, routed_b2, centroids, bias):
        import jax, jax.numpy as jnp
        import numpy as np
        D_MODEL, D_FF, NS, NR, KR = (256, 176, 2, 16, 4)
        B, S = (4, 256)

        def _moe_forward(u, shared_w1, shared_b1, shared_w2, shared_b2, routed_w1, routed_b1, routed_w2, routed_b2, centroids, bias):
            b, s, d = u.shape
            flat = u.reshape(-1, d)
            T = flat.shape[0]
            h = jax.nn.relu(jnp.einsum('td,ndf->ntf', flat, shared_w1) + shared_b1[:, None, :])
            shared_out = jnp.einsum('ntf,nfd->td', h, shared_w2) + shared_b2.sum(0)
            out = flat + shared_out
            scores = jax.nn.sigmoid(flat @ centroids.T) + bias
            vals, idx = jax.lax.top_k(scores, KR)
            gating = jnp.zeros_like(scores).at[jnp.arange(T)[:, None], idx].set(vals)
            gating = gating / jnp.clip(gating.sum(-1, keepdims=True), 1e-08)

            def step(acc, ew):
                w1, b1, w2, b2, g = ew
                hj = jax.nn.relu(flat @ w1 + b1)
                yj = hj @ w2 + b2
                return (acc + yj * g[:, None], None)
            rout0 = jnp.zeros_like(flat)
            rout, _ = jax.lax.scan(step, rout0, (routed_w1, routed_b1, routed_w2, routed_b2, gating.T))
            return (out + rout).reshape(b, s, d)
        return _moe_forward(u, shared_w1, shared_b1, shared_w2, shared_b2, routed_w1, routed_b1, routed_w2, routed_b2, centroids, bias)
    x = L0_attn_x
    x = x + 0.5 * _L0_ffn_ref(_layernorm(x, axis=-1), L0_ffn_lut, L0_ffn_gate_idx, L0_ffn_up_idx, L0_ffn_down_idx)
    x = x + _L0_attn_ref(_layernorm(x, axis=-1), L0_attn_Wqkv, L0_attn_b_qkv, L0_attn_Wout, L0_attn_b_out)
    x = x + 0.5 * _L0_ffn_ref(_layernorm(x, axis=-1), L0_ffn_lut, L0_ffn_gate_idx, L0_ffn_up_idx, L0_ffn_down_idx)
    x = x + 0.5 * _L1_ffn_ref(_layernorm(x, axis=-1), L1_ffn_shared_w1, L1_ffn_shared_b1, L1_ffn_shared_w2, L1_ffn_shared_b2, L1_ffn_routed_w1, L1_ffn_routed_b1, L1_ffn_routed_w2, L1_ffn_routed_b2, L1_ffn_centroids, L1_ffn_bias)
    x = x + _L1_attn_ref(_layernorm(x, axis=-1), L1_attn_Wq, L1_attn_Wk, L1_attn_Wv, L1_attn_Wproj)
    x = x + 0.5 * _L1_ffn_ref(_layernorm(x, axis=-1), L1_ffn_shared_w1, L1_ffn_shared_b1, L1_ffn_shared_w2, L1_ffn_shared_b2, L1_ffn_routed_w1, L1_ffn_routed_b1, L1_ffn_routed_w2, L1_ffn_routed_b2, L1_ffn_centroids, L1_ffn_bias)
    return x

_drawn_inputs = setup_inputs


def setup_inputs(seed=0):
    import zlib

    import numpy as np

    out = dict(_drawn_inputs(seed))
    spreads = {'L0_attn_b_qkv': (0.0, 0.1),
     'L0_attn_b_out': (0.0, 0.1),
     'L1_ffn_shared_b1': (0.0, 0.1),
     'L1_ffn_shared_b2': (0.0, 0.1),
     'L1_ffn_routed_b1': (0.0, 0.451),
     'L1_ffn_routed_b2': (0.0, 0.303),
     'L1_ffn_bias': (0.0, 0.1)}
    factors = {'L1_attn_Wq': 8.0, 'L1_attn_Wk': 8.0, 'L1_attn_Wv': 3.449, 'L1_attn_Wproj': 3.58}
    for name, (base, spread) in spreads.items():
        noise = np.random.default_rng([zlib.crc32(name.encode()), seed]).standard_normal(out[name].shape)
        drawn = base * np.exp(spread * noise) if base else spread * noise
        out[name] = jnp.asarray(drawn.astype(out[name].dtype))
    for name, factor in factors.items():
        out[name] = (out[name] * factor).astype(out[name].dtype)
    return out
```

```python
from contextlib import ExitStack

import numpy as np

import concourse.bass as bass
from concourse import mybir


F32 = mybir.dt.float32
F32R = mybir.dt.float32r
BF16 = mybir.dt.bfloat16
I32 = mybir.dt.int32
ACT = mybir.ActivationFunctionType
ALU = mybir.AluOpType
AX = mybir.AxisListType

P = 128
BATCHES = 4
SEQ = 512
D = 256
DH = D // P
TT = SEQ // P
TILES = BATCHES * TT
EPS = 1e-5
HEADS = 16
HD = D // HEADS
KV = 4

FF = 688
FT = -(-FF // P)
FW = [min(P, FF - P * m) for m in range(FT)]
LUT = 16

NS, NR, EF, TOPK = 2, 16, 176, 4
RT = NR * EF // P
ST = -(-NS * EF // P)
MT = RT + ST
MW = [P] * RT + [min(P, NS * EF - P * m) for m in range(ST)]
MORDER = list(range(RT, MT)) + list(range(RT))
PAD = -1.0e30

ONE = 1

PHASES = ["ffn", "attn0", "ffn", "moe", "attn1", "moe"]
ATT_SEMS = ("load", "w_hi", "w_lo", "const", "cast", "zero", "proj", "rope", "sum", "hi", "lo", "v", "v_ready",
            "place_q", "qz", "place_k", "kz", "s", "smax", "mt", "mrow", "row", "st", "exp", "pv", "ctx_recip", "ctx",
            "ct", "ct_hi", "ct_lo", "o", "x", "bias")


def hi_lo(x):
    u = np.asarray(x, np.float32)
    m, e = np.frexp(u.astype(np.float64))
    hi = np.ldexp(np.round(m * 4096) / 4096, e).astype(np.float32)
    return hi, (u - hi).astype(np.float32)


def constants():
    c = {}
    c["c_ident"] = np.eye(P, dtype=np.float32)
    q = np.arange(P)
    c["c_mask"] = np.where(q[None, :] > q[:, None], np.float32(PAD), np.float32(0))
    c["c_maskT"] = c["c_mask"].T.copy()
    unit = np.arange(NR * EF) // EF
    sel = np.zeros((P, NR * EF), np.float32)
    sel[:NR] = unit[None, :] == np.arange(NR)[:, None]
    sel[NR:2 * NR] = sel[:NR]
    c["c_sel"] = sel
    place = np.zeros((P, 4, HEADS // 4, P), np.float32)
    for cc in range(4):
        for half in range(2):
            for d in range(HD):
                src, dst = HD * (2 * cc + half) + d, 64 * half + d
                place[src, 0, cc, dst] = place[src, 0, cc, dst + 2 * HD] = 1
                place[src, 1, cc, dst + HD] = 1
                place[src, 2, cc, dst] = place[src, 2, cc, dst + HD] = 1
                place[src, 3, cc, dst + 2 * HD] = 1
    c["c_place"] = place.reshape(P, 16 * P)
    m = np.arange(1, HEADS + 1, dtype=np.float32) * np.float32(8.0 / HEADS)
    slopes = (np.float32(1.0) / np.float32(2.0) ** m).astype(np.float32)
    s_hi, s_lo = hi_lo(slopes * np.float32(4.0))
    qx = np.zeros((P, HEADS), np.float32)
    kx = np.zeros((P, SEQ), np.float32)
    for half in range(2):
        qx[64 * half + 48], qx[64 * half + 49] = s_hi, s_lo
        kx[64 * half + 48] = kx[64 * half + 49] = np.arange(1 - SEQ, 1)
        kx[64 * half + 50] = 1
    c["c_qx"], c["c_kx"] = qx, kx
    inv = (1.0 / np.float32(10000.0) ** (np.arange(0, HD, 2, dtype=np.float32) / np.float32(HD))).astype(np.float32)
    ang = np.arange(SEQ, dtype=np.float32)[:, None] * inv[None, :]
    ang = np.concatenate([ang, ang], -1).T
    c["c_cos"] = np.tile(np.cos(ang), (P // HD, 1)).astype(np.float32)
    sign = np.where(np.arange(HD) < HD // 2, np.float32(-1), np.float32(1))[:, None]
    c["c_sin"] = np.tile(sign * np.sin(ang), (P // HD, 1)).astype(np.float32)
    return c


def kernel_program(nc, t, out):
    with ExitStack() as top:
        def sb(ctx, name, shape, dt=F32):
            return ctx.enter_context(nc.sbuf_tensor(name, shape, dt))

        def sem(name):
            return top.enter_context(nc.semaphore(name))

        PS = top.enter_context(nc.psum_tensor("PS", [P, 8, 512], F32))

        X = sb(top, "X", [P, TILES, D])
        XN = sb(top, "XN", [P, 2, TT, D])
        XH = sb(top, "XH", [P, 2, DH, SEQ], F32R)
        XL = sb(top, "XL", [P, 2, DH, SEQ], F32R)
        LST = sb(top, "LST", [P, TT, 6])
        LTMP = sb(top, "LTMP", [P, 5, TT])
        LMEAN = sb(top, "LMEAN", [P, TT])
        LVE = sb(top, "LVE", [P, TT])
        LRS = sb(top, "LRS", [P, TT])
        MHALF = sb(top, "MHALF", [P, TT])
        IDENT = sb(top, "IDENT", [P, P])
        YS = sb(top, "YS", [P, DH, SEQ])

        ln_stats = sem("ln_stats")
        ln_parts = sem("ln_parts")
        ln_var = sem("ln_var")
        ln_rstd = sem("ln_rstd")
        xn_ready = sem("xn_ready")
        xt_done = sem("xt_done")
        xh_ready = sem("xh_ready")
        xl_ready = sem("xl_ready")
        ins = sem("ins")
        ready = sem("ready")
        stored = sem("stored")
        y_done = sem("y_done")
        y_copied = sem("y_copied")
        yt_done = sem("yt_done")
        x_updated = sem("x_updated")

        def ln_stats_dve(dve, b, g):
            for j in range(TT):
                dve.bn_stats(LST[:, j, :], X[:, bass.ds(b * TT + j, 1), :]).then_inc(ln_stats, 1)
            m_even, v_even, m_odd, v_odd = (LST[:, :, k] for k in (1, 2, 4, 5))
            dve.wait_ge(ln_stats, g * TT + TT)
            dve.tensor_tensor(LTMP[:, 0, :], m_even, m_odd, ALU.subtract).then_inc(ln_parts, 1)
            dve.tensor_tensor(LTMP[:, 1, :], v_even, v_odd, ALU.add).then_inc(ln_parts, 1)
            dve.tensor_tensor(LTMP[:, 2, :], m_even, m_odd, ALU.add).then_inc(ln_parts, 1)
            dve.wait_ge(ln_parts, g * 6 + 3)
            dve.tensor_tensor(LTMP[:, 3, :], LTMP[:, 0, :], LTMP[:, 0, :], ALU.mult).then_inc(ln_parts, 1)
            dve.tensor_scalar(LMEAN[:], LTMP[:, 2, :], 0.5, None, ALU.mult).then_inc(ln_parts, 1)
            dve.wait_ge(ln_parts, g * 6 + 5)
            dve.scalar_tensor_tensor(out=LTMP[:, 4, :], in0=LTMP[:, 3, :], scalar=float(D // 4), in1=LTMP[:, 1, :],
                                     op0=ALU.mult, op1=ALU.add).then_inc(ln_parts, 1)
            dve.wait_ge(ln_parts, g * 6 + 6)
            dve.tensor_scalar(LVE[:], LTMP[:, 4, :], 1.0 / D, EPS, ALU.mult, ALU.add).then_inc(ln_var, 1)

        def ln_rstd_pool(pool, g):
            pool.wait_ge(ln_var, g + 1)
            pool.tensor_tensor(LRS[:], LVE[:], MHALF[:], ALU.pow).then_inc(ln_rstd, 1)

        def ln_norm_dve(dve, b, g, par):
            dve.wait_ge(ln_rstd, g + 1)
            for j in range(TT):
                dve.tensor_scalar(XN[:, par, j, :], X[:, bass.ds(b * TT + j, 1), :], LMEAN[:, j:j + 1],
                                  LRS[:, j:j + 1], ALU.subtract, ALU.mult).then_inc(xn_ready, 1)

        def ln_transpose_pe(pe, g, par, banks):
            pe.wait_ge(xn_ready, g * TT + TT)
            for f in range(DH):
                for j in range(TT):
                    mm = pe.transpose(PS[:, banks[f], j * P:(j + 1) * P],
                                      XN[:, par, j, f * P:(f + 1) * P], IDENT[:])
                mm.then_inc(xt_done, 1)

        def ln_hi_act(act, g, par, banks):
            for f in range(DH):
                act.wait_ge(xt_done, g * DH + f + 1)
                act.activation(XH[:, par, f, :], PS[:, banks[f], :], ACT.Copy).then_inc(xh_ready, 1)

        def ln_lo_dve(dve, g, par, banks):
            for f in range(DH):
                dve.wait_ge(xh_ready, g * DH + f + 1)
                dve.tensor_tensor(XL[:, par, f, :], PS[:, banks[f], :], XH[:, par, f, :].bitcast(F32),
                                  ALU.subtract).then_inc(xl_ready, 1)

        def three_passes(pe, psum, w_hi, w_lo, x_hi, x_lo, start, stop):
            pe.matmul(psum, w_hi, x_hi, start=start, stop=False)
            pe.matmul(psum, w_lo, x_hi, start=False, stop=False)
            return pe.matmul(psum, w_hi, x_lo, start=False, stop=stop)

        fs = {n: sem("f_" + n) for n in (
            "idx", "masks", "sums", "sums_used", "diag", "diag_hi", "diag_lo",
            "gate", "up", "silu", "h", "hh", "hl", "h_used")}
        ms = {n: sem("m_" + n) for n in (
            "raw0", "raw1", "raw2", "raw3", "w_hi", "w_lo", "const", "bs_sum", "sel", "zero", "ct_hi", "ct_lo",
            "b2_hi", "b2_lo", "logits", "scores", "gate_steps", "g2", "gt", "gt_ready",
            "hid", "gbc", "relu", "h", "hh", "hl", "h_used", "xn_added")}
        a0 = {n: sem("a0_" + n) for n in ATT_SEMS}
        a1 = {n: sem("a1_" + n) for n in ATT_SEMS}

        with nc.Block() as block:
            @block.sync
            def _(sp):
                for q in (a0["row"], a1["row"]):
                    sp.sem_inc(q, ONE)
                sp.dma_start(IDENT[:], t["c_ident"]).then_inc(ins, 16)
                for b in range(BATCHES):
                    sp.dma_start(X[:, b * TT:(b + 1) * TT, :],
                                 t["L0_attn_x"][b].rearrange("(j p) d -> p j d", p=P)).then_inc(ins, 16)

            @block.gpsimd
            def _(pool):
                for q in (fs["hl"], ms["hl"]):
                    pool.sem_inc(q, ONE)
                pool.memset(MHALF[:], -0.5).then_inc(ready, 1)
                pool.wait_ge(ready, 1)
                ln_rstd_pool(pool, 0)

            @block.vector
            def _(dve):
                for q in (x_updated, fs["h"], ms["h"], a0["smax"], a0["x"], a1["smax"], a1["x"], a0["ctx"], a1["ctx"]):
                    dve.sem_inc(q, ONE)
                dve.wait_ge(ins, 16 * (1 + BATCHES))
                ln_stats_dve(dve, 0, 0)
                ln_norm_dve(dve, 0, 0, 0)
                ln_lo_dve(dve, 0, 0, (0, 1))

            @block.tensor
            def _(pe):
                for q in (y_done, fs["h_used"], ms["h_used"], a0["pv"], a1["pv"]):
                    pe.sem_inc(q, ONE)
                pe.wait_ge(ins, 16 * (1 + BATCHES))
                ln_transpose_pe(pe, 0, 0, (0, 1))

            @block.scalar
            def _(act):
                for q in (y_copied, fs["silu"], ms["relu"], a0["exp"], a1["exp"]):
                    act.sem_inc(q, ONE)
                ln_hi_act(act, 0, 0, (0, 1))


        def ring(s, n, k, depth):
            return ONE + s * n + max(k - depth + 1, 0)

        def next_batch(i, u):
            return 2 * i + 1 if u == 0 else 2 - 2 * i

        def epilogue_copy_act(act, e, bias):
            for f in range(DH):
                act.wait_ge(y_done, ONE + e * DH + f + 1)
                if bias is None:
                    act.activation(YS[:, f, :], PS[:, 6 + f, :], ACT.Copy).then_inc(y_copied, 1)
                else:
                    act.activation(YS[:, f, :], PS[:, 6 + f, :], ACT.Identity,
                                   bias=bias[:, f:f + 1]).then_inc(y_copied, 1)

        def epilogue_transpose_pe(pe, e, g, follows=True):
            pe.wait_ge(y_copied, ONE + e * DH + DH)
            if follows:
                pe.wait_ge(xl_ready, (g + 1) * DH + DH)
            for jj in range(2):
                for j in range(2):
                    for f in range(DH):
                        mm = pe.transpose(PS[:, jj, j * D + f * P:j * D + (f + 1) * P],
                                          YS[:, f, (2 * jj + j) * P:(2 * jj + j + 1) * P], IDENT[:])
                mm.then_inc(yt_done, 1)

        def epilogue_add_dve(dve, e, b, follows=True):
            for jj in range(2):
                dve.wait_ge(yt_done, e * 2 + jj + 1)
                xs = X[:, bass.ds(b * TT + 2 * jj, 2), :]
                dve.scalar_tensor_tensor(out=xs, in0=PS[:, jj, :].rearrange("p (j d) -> p j d", j=2), scalar=0.5,
                                         in1=xs, op0=ALU.mult, op1=ALU.add).then_inc(x_updated, 1)

        def ffn_weights(keep):
            WG = sb(keep, "WGU", [P, 2, 2, DH, FF], F32R)
            WD = sb(keep, "WD", [P, 2, FT, D], F32R)
            with ExitStack() as ctx:
                LB = sb(ctx, "LUTB", [P, LUT])
                DG = sb(ctx, "DIAG", [P, LUT, P])
                DHL = sb(ctx, "DIAGHL", [P, LUT, 2, P], F32R)
                IX = sb(ctx, "IDX", [P, 2, FT, D], I32)
                IXD = sb(ctx, "IDXD", [P, DH, FF], I32)
                MK = sb(ctx, "MASKS", [P, 2, LUT, D], F32R)
                units = [("gu", gu, o) for gu in range(2) for o in range(FT)]
                units += [("d", dh, m0) for dh in range(DH) for m0 in range(0, FT, 2)]

                def sums(n):
                    kind, a, c = units[n]
                    if kind == "gu":
                        return [(slice(f * P, (f + 1) * P), FW[c], P, WG[:, a, :, f, c * P:c * P + FW[c]])
                                for f in range(DH)]
                    return [(slice(i * P, i * P + FW[c + i]), P, FW[c + i],
                             WD[0:FW[c + i], :, c + i, a * P:(a + 1) * P]) for i in range(2)]

                with nc.Block() as block:
                    @block.sync
                    def _(sp):
                        sp.dma_start(LB[:], t["L0_ffn_lut"].partition_broadcast(P)).then_inc(fs["idx"], 16)
                        full = (FT - 1) * P
                        for gu, name in enumerate(("L0_ffn_gate_idx", "L0_ffn_up_idx")):
                            sp.dma_start(IX[:, gu, 0:FT - 1, :],
                                         t[name][0:full, :].rearrange("(o p) d -> p o d", p=P)).then_inc(fs["idx"], 16)
                            sp.dma_start(IX[0:FF - full, gu, FT - 1, :], t[name][full:FF, :]).then_inc(fs["idx"], 16)
                        sp.dma_start(IXD[:], t["L0_ffn_down_idx"].rearrange("(h p) f -> p h f", p=P)).then_inc(fs["idx"], 16)

                    @block.vector
                    def _(dve):
                        dve.wait_ge(fs["idx"], 96)
                        for k in range(LUT):
                            dve.tensor_scalar(DG[:, k, :], IDENT[:], LB[:, k:k + 1], None,
                                              ALU.mult).then_inc(fs["diag"], 1)
                        dve.wait_ge(fs["diag"], LUT)
                        dve.tensor_copy(DHL[:, :, 0, :], DG[:]).then_inc(fs["diag_hi"], 1)
                        dve.wait_ge(fs["diag_hi"], 1)
                        dve.tensor_tensor(DHL[:, :, 1, :], DG[:], DHL[:, :, 0, :].bitcast(F32),
                                          ALU.subtract).then_inc(fs["diag_lo"], 1)
                        for n, (kind, a, c) in enumerate(units):
                            if n >= 2:
                                dve.wait_ge(fs["sums"], 2 * (n - 1))
                            if kind == "gu":
                                rows, w = FW[c], D
                                src = IX[0:rows, a, c, :]
                            else:
                                rows, w = P, min(2 * P, FF - c * P)
                                src = IXD[:, a, c * P:c * P + w]
                            for k in range(LUT):
                                last = dve.tensor_scalar(MK[0:rows, n % 2, k, 0:w], src, float(k), None, ALU.is_equal)
                            last.then_inc(fs["masks"], 1)

                    @block.tensor
                    def _(pe):
                        pe.wait_ge(fs["diag_lo"], 1)
                        for n, (kind, a, c) in enumerate(units):
                            rows = FW[c] if kind == "gu" else P
                            pe.wait_ge(fs["masks"], n + 1)
                            for i, (cols, w, orows, _) in enumerate(sums(n)):
                                q = 2 * n + i
                                if q >= 4:
                                    pe.wait_ge(fs["sums_used"], q - 3)
                                dst = PS[0:orows, 2 + q % 4, 0:2 * w].rearrange("p (a n) -> p a n", a=2)
                                for k in range(LUT):
                                    mm = pe.matmul(dst, MK[0:rows, n % 2, k, cols], DHL[0:rows, k, :, 0:w],
                                                   start=k == 0, stop=k == LUT - 1)
                                mm.then_inc(fs["sums"], 1)

                    @block.scalar
                    def _(act):
                        for n in range(len(units)):
                            for i, (cols, w, orows, dst) in enumerate(sums(n)):
                                q = 2 * n + i
                                act.wait_ge(fs["sums"], q + 1)
                                act.activation(dst, PS[0:orows, 2 + q % 4, 0:2 * w].rearrange("p (a n) -> p a n", a=2),
                                               ACT.Copy).then_inc(fs["sums_used"], 1)
            return WG, WD

        def ffn_phase(phase, occ, WG, WD, e0):
            with ExitStack() as ctx:
                SG = sb(ctx, f"SG{phase}", [P, 2, SEQ])
                HF = sb(ctx, f"HF{phase}", [P, 2, SEQ])
                HH = sb(ctx, f"HH{phase}", [P, 2, SEQ], F32R)
                HL = sb(ctx, f"HL{phase}", [P, 2, SEQ], F32R)
                block = ctx.enter_context(nc.Block())

                def steps(eng):
                    with eng.Fori(0, BATCHES // 2) as i:
                        for u in range(2):
                            b = 2 * i + u
                            yield i, u, b, 4 * occ + b, e0 + b, 4 * phase + b

                @block.tensor
                def _(pe):
                    for i, u, b, s, e, g in steps(pe):
                        def up(m):
                            w = FW[m]
                            for gu, (done, freed) in enumerate((("gate", "silu"), ("up", "h"))):
                                pe.wait_ge(fs[freed], ring(s, FT, m, 2))
                                dst = PS[0:w, 2 + 2 * gu + m % 2, :]
                                cols = slice(m * P, m * P + w)
                                for f in range(DH):
                                    mm = three_passes(pe, dst, WG[:, gu, 0, f, cols], WG[:, gu, 1, f, cols],
                                                      XH[:, u, f, :], XL[:, u, f, :], f == 0, f == DH - 1)
                                mm.then_inc(fs[done], 1)

                        def down(m):
                            w = FW[m]
                            pe.wait_ge(fs["hl"], ONE + s * FT + m + 1)
                            for f in range(DH):
                                cols = slice(f * P, (f + 1) * P)
                                mm = three_passes(pe, PS[:, 6 + f, :], WD[0:w, 0, m, cols], WD[0:w, 1, m, cols],
                                                  HH[0:w, m % 2, :], HL[0:w, m % 2, :], m == 0, m == FT - 1)
                                if m == FT - 1:
                                    mm.then_inc(y_done, 1)
                            mm.then_inc(fs["h_used"], 1) if m < FT - 1 else None

                        pe.wait_ge(xl_ready, g * DH + DH)
                        pe.wait_ge(y_copied, ONE + e * DH)
                        for m in range(FT):
                            up(m)
                            if m == 3:
                                pe.wait_ge(x_updated, ONE + e * 2)
                                ln_transpose_pe(pe, g + 1, 1 - u, (0, 1))
                            if m >= 1:
                                down(m - 1)
                        down(FT - 1)
                        epilogue_transpose_pe(pe, e, g)

                @block.scalar
                def _(act):
                    for i, u, b, s, e, g in steps(act):
                        def silu(m):
                            act.wait_ge(fs["gate"], s * FT + m + 1)
                            act.wait_ge(fs["h"], ring(s, FT, m, 2))
                            act.activation(SG[0:FW[m], m % 2, :], PS[0:FW[m], 2 + m % 2, :],
                                           ACT.Silu).then_inc(fs["silu"], 1)

                        def hi(m):
                            act.wait_ge(fs["h"], ONE + s * FT + m + 1)
                            if m >= 2:
                                act.wait_ge(fs["h_used"], ONE + s * (FT - 1) + m - 1)
                            else:
                                act.wait_ge(y_done, ONE + e * DH)
                            act.activation(HH[0:FW[m], m % 2, :], HF[0:FW[m], m % 2, :], ACT.Copy).then_inc(fs["hh"], 1)

                        for m in range(FT):
                            silu(m)
                            if m >= 1:
                                hi(m - 1)
                            if m == 4:
                                ln_hi_act(act, g + 1, 1 - u, (0, 1))
                        hi(FT - 1)
                        epilogue_copy_act(act, e, None)

                @block.vector
                def _(dve):
                    for i, u, b, s, e, g in steps(dve):
                        nb = next_batch(i, u)
                        for m in range(FT):
                            w = FW[m]
                            dve.wait_ge(fs["silu"], ONE + s * FT + m + 1)
                            dve.wait_ge(fs["up"], s * FT + m + 1)
                            dve.wait_ge(fs["hl"], ring(s, FT, m, 2))
                            dve.tensor_tensor(HF[0:w, m % 2, :], SG[0:w, m % 2, :], PS[0:w, 4 + m % 2, :],
                                              ALU.mult).then_inc(fs["h"], 1)
                            if m == 0:
                                ln_stats_dve(dve, nb, g + 1)
                            if m == 1:
                                ln_norm_dve(dve, nb, g + 1, 1 - u)
                            if m == 4:
                                ln_lo_dve(dve, g + 1, 1 - u, (0, 1))
                        epilogue_add_dve(dve, e, b)

                @block.gpsimd
                def _(pool):
                    for i, u, b, s, e, g in steps(pool):
                        for m in range(FT):
                            w = FW[m]
                            pool.wait_ge(fs["hh"], s * FT + m + 1)
                            pool.tensor_tensor(HL[0:w, m % 2, :], HF[0:w, m % 2, :], HH[0:w, m % 2, :].bitcast(F32),
                                               ALU.subtract).then_inc(fs["hl"], 1)
                            if m == 0:
                                ln_rstd_pool(pool, g + 1)


        def moe_phase(phase, occ, e0):
            with ExitStack() as ctx:
                def mb(name, shape, dt=F32):
                    return sb(ctx, f"{name}_{phase}", shape, dt)

                RING = 4
                WRAW = mb("WRAW", [P, RING, DH * P + D])
                W = mb("W", [P, MT, 2, DH * P + D], F32R)
                B1 = mb("B1", [P, MT])
                SEL = mb("SEL", [P, RT, P], F32R)
                B2R = mb("B2R", [P, D])
                B2 = mb("B2", [P, 2, D], F32R)
                BS2 = mb("BS2", [P, NS, DH])
                BS = mb("BS", [P, DH])
                CR = mb("CR", [P, DH, NR])
                CT = mb("CT", [P, 2, DH, NR], F32R)
                RB = mb("RB", [P, NR])
                SC = mb("SC", [P, TT, NR + 8])
                V8 = mb("V8", [P, TT, 8])
                MR = mb("MR", [P, TT, NR + 8])
                GK = mb("GK", [P, TT, NR])
                GS = mb("GS", [P, 3, TT])
                G2 = mb("G2", [P, TT, P], F32R)
                GT = mb("GT", [P, SEQ], F32R)
                HR = mb("HR", [P, 2, SEQ])
                HF = mb("HFM", [P, 2, SEQ])
                HH = mb("HHM", [P, 2, SEQ], F32R)
                HL = mb("HLM", [P, 2, SEQ], F32R)
                block = ctx.enter_context(nc.Block())
                LAG = 2

                STEPS = [(b, b % 2, 4 * occ + b, e0 + b, 4 * phase + b) for b in range(BATCHES)]
                LAST = 4 * len(PHASES) - 1
                CONST = 5 * 16

                @block.sync
                def _(sp):
                    for k in range(MT):
                        if k >= RING:
                            sp.wait_ge(ms["w_lo"], occ * MT + k - RING + 1)
                        sp.dma_start(WRAW[:, k % RING, :], t["m_w"][k]).then_inc(ms[f"raw{k % RING}"], 16)

                def raw_loads(k):
                    before = occ * len(range(k % RING, MT, RING))
                    return 16 * (before + k // RING + 1)

                @block.scalar
                def _(act):
                    for dst, name in ((CR, "m_centroids"), (B1, "m_b1"), (B2R, "m_b2"), (BS2, "m_bs2")):
                        act.dma_start(dst[:], t[name]).then_inc(ms["const"], 16)
                    act.dma_start(RB[:], t["L1_ffn_bias"].partition_broadcast(P)).then_inc(ms["const"], 16)
                    act.wait_ge(ms["const"], occ * CONST + CONST)
                    act.activation(CT[:, 0, :, :], CR[:], ACT.Copy).then_inc(ms["ct_hi"], 1)
                    act.activation(B2[:, 0, :], B2R[:], ACT.Copy).then_inc(ms["b2_hi"], 1)

                    def split_hi(k):
                        m = MORDER[k]
                        act.wait_ge(ms[f"raw{k % RING}"], raw_loads(k))
                        act.activation(W[:, m, 0, :], WRAW[:, k % RING, :], ACT.Copy).then_inc(ms["w_hi"], 1)

                    for b, par, s, e, g in STEPS:
                        def relu(k):
                            m, w = MORDER[k], MW[MORDER[k]]
                            act.wait_ge(ms["hid"], s * MT + k + 1)
                            if m >= RT:
                                act.wait_ge(ms["hl"], ring(s, MT, k, 2))
                                dst = HF
                            else:
                                act.wait_ge(ms["h"], ring(s, RT, k - ST, 2))
                                dst = HR
                            act.activation(dst[0:w, k % 2, :], PS[0:w, 2 + k % 2, :], ACT.Relu,
                                           bias=B1[0:w, m:m + 1]).then_inc(ms["relu"], 1)

                        def hi(k):
                            m, w = MORDER[k], MW[MORDER[k]]
                            if m >= RT:
                                act.wait_ge(ms["relu"], ONE + s * MT + k + 1)
                            else:
                                act.wait_ge(ms["h"], ONE + s * RT + k - ST + 1)
                            act.wait_ge(ms["h_used"], ring(s, MT, k, 2))
                            act.activation(HH[0:w, k % 2, :], HF[0:w, k % 2, :], ACT.Copy).then_inc(ms["hh"], 1)

                        if b == 0:
                            split_hi(0)
                            split_hi(1)
                        act.wait_ge(ms["logits"], s + 1)
                        act.activation(SC[:, :, 0:NR], PS[:, 0, 0:TT * NR].rearrange("p (j n) -> p j n", j=TT),
                                       ACT.Sigmoid).then_inc(ms["scores"], 1)
                        for k in range(MT):
                            if b == 0 and k + 2 < MT:
                                split_hi(k + 2)
                            relu(k)
                            if k >= 1:
                                hi(k - 1)
                            if k == ST:
                                act.wait_ge(ms["gt"], s + 1)
                                act.activation(GT[:], PS[:, 1, :], ACT.Copy).then_inc(ms["gt_ready"], 1)
                            if k == 13 and g < LAST:
                                ln_hi_act(act, g + 1, 1 - par, (0, 1))
                        hi(MT - 1)
                        epilogue_copy_act(act, e, BS)

                @block.gpsimd
                def _(pool):
                    pool.dma_start(SEL[:].rearrange("p m c -> p (m c)"), t["c_sel"]).then_inc(ms["sel"], 16)
                    for b, par, s, e, g in STEPS:
                        def split_lo(k):
                            m = MORDER[k]
                            pool.wait_ge(ms["w_hi"], occ * MT + k + 1)
                            pool.tensor_tensor(W[:, m, 1, :], WRAW[:, k % RING, :], W[:, m, 0, :].bitcast(F32),
                                               ALU.subtract).then_inc(ms["w_lo"], 1)

                        if b == 0:
                            split_lo(0)
                            split_lo(1)
                        for k in range(MT):
                            w = MW[MORDER[k]]
                            if b == 0 and k + 2 < MT:
                                split_lo(k + 2)
                            pool.wait_ge(ms["hh"], s * MT + k + 1)
                            pool.tensor_tensor(HL[0:w, k % 2, :], HF[0:w, k % 2, :], HH[0:w, k % 2, :].bitcast(F32),
                                               ALU.subtract).then_inc(ms["hl"], 1)
                            if k == 5 and g < LAST:
                                ln_rstd_pool(pool, g + 1)

                @block.vector
                def _(dve):
                    for n, (dst, v) in enumerate(((SC[:, :, NR:], PAD), (G2[:].bitcast(F32), 0.0))):
                        dve.memset(dst, v).then_inc(ms["zero"], 1)
                    dve.wait_ge(ms["const"], CONST * (occ + 1))
                    dve.tensor_tensor(BS[:], BS2[:, 0, :], BS2[:, 1, :], ALU.add).then_inc(ms["bs_sum"], 1)
                    dve.wait_ge(ms["ct_hi"], occ + 1)
                    dve.tensor_tensor(CT[:, 1, :, :], CR[:], CT[:, 0, :, :].bitcast(F32), ALU.subtract).then_inc(ms["ct_lo"], 1)
                    dve.wait_ge(ms["b2_hi"], occ + 1)
                    dve.tensor_tensor(B2[:, 1, :], B2R[:], B2[:, 0, :].bitcast(F32), ALU.subtract).then_inc(ms["b2_lo"], 1)
                    dve.wait_ge(ms["zero"], 2 * occ + 2)
                    for b, par, s, e, g in STEPS:
                        steps_done = [s * 11]

                        def link(ins_):
                            steps_done[0] += 1
                            ins_.then_inc(ms["gate_steps"], 1)
                            dve.wait_ge(ms["gate_steps"], steps_done[0])

                        dve.wait_ge(ms["scores"], s + 1)
                        best = SC[:, :, 0:NR]
                        link(dve.tensor_tensor(best, best, RB[:].unsqueeze(1).broadcast_to([P, TT, NR]), ALU.add))
                        for j in range(TT):
                            last = dve.max(V8[:, j, :], SC[:, j, :])
                        link(last)
                        link(dve.memset(V8[:, :, TOPK:], PAD))
                        for j in range(TT):
                            last = dve.match_replace(MR[:, j, :], V8[:, j, :], SC[:, j, :], 2 * PAD)
                        link(last)
                        link(dve.tensor_tensor(GK[:], best, MR[:, :, 0:NR], ALU.not_equal))
                        link(dve.tensor_tensor(GK[:], GK[:], best, ALU.mult))
                        link(dve.tensor_reduce(GS[:, 0, :], GK[:], AX.X, ALU.add))
                        link(dve.tensor_scalar(GS[:, 1, :], GS[:, 0, :], 1e-8, None, ALU.max))
                        link(dve.reciprocal(GS[:, 2, :], GS[:, 1, :]))
                        link(dve.tensor_tensor(GK[:], GK[:], GS[:, 2, :].unsqueeze(2).broadcast_to([P, TT, NR]), ALU.mult))
                        link(dve.tensor_copy(G2[:, :, 0:NR], GK[:]))
                        dve.tensor_tensor(G2[:, :, NR:2 * NR], GK[:], G2[:, :, 0:NR].bitcast(F32),
                                          ALU.subtract).then_inc(ms["g2"], 1)
                        xs = X[:, b * TT:(b + 1) * TT, :]
                        dve.scalar_tensor_tensor(out=xs, in0=XN[:, par, :, :], scalar=0.5, in1=xs, op0=ALU.mult,
                                                 op1=ALU.add).then_inc(ms["xn_added"], 1)
                        for r in range(RT):
                            k = ST + r
                            dve.wait_ge(ms["relu"], ONE + s * MT + k + 1)
                            dve.wait_ge(ms["gbc"], s * RT + r + 1)
                            dve.wait_ge(ms["hl"], ring(s, MT, k, 2))
                            dve.tensor_tensor(HF[:, k % 2, :], HR[:, k % 2, :], PS[:, 4 + r % 2, :],
                                              ALU.mult).then_inc(ms["h"], 1)
                            if g < LAST:
                                if r == 2:
                                    ln_stats_dve(dve, (b + 1) % BATCHES, g + 1)
                                if r == 4:
                                    ln_norm_dve(dve, (b + 1) % BATCHES, g + 1, 1 - par)
                                if r == 11:
                                    ln_lo_dve(dve, g + 1, 1 - par, (0, 1))
                        dve.wait_ge(ms["xn_added"], s + 1)
                        epilogue_add_dve(dve, e, b, g < LAST)

                @block.tensor
                def _(pe):
                    for b, par, s, e, g in STEPS:
                        def gates(k):
                            r = k - ST
                            pe.wait_ge(ms["h"], ring(s, RT, r, 2))
                            pe.matmul(PS[:, 4 + r % 2, :], SEL[:, r, :], GT[:], start=True, stop=True).then_inc(ms["gbc"], 1)

                        def up(k):
                            m, w = MORDER[k], MW[MORDER[k]]
                            if b == 0:
                                pe.wait_ge(ms["w_lo"], occ * MT + k + 1)
                            pe.wait_ge(ms["relu"], ring(s, MT, k, 2))
                            for f in range(DH):
                                cols = slice(f * P, f * P + w)
                                mm = three_passes(pe, PS[0:w, 2 + k % 2, :], W[:, m, 0, cols], W[:, m, 1, cols],
                                                  XH[:, par, f, :], XL[:, par, f, :], f == 0, f == DH - 1)
                            mm.then_inc(ms["hid"], 1)

                        def down(k):
                            m, w = MORDER[k], MW[MORDER[k]]
                            pe.wait_ge(ms["hl"], ONE + s * MT + k + 1)
                            for f in range(DH):
                                cols = slice(DH * P + f * P, DH * P + (f + 1) * P)
                                mm = three_passes(pe, PS[:, 6 + f, :], W[0:w, m, 0, cols], W[0:w, m, 1, cols],
                                                  HH[0:w, k % 2, :], HL[0:w, k % 2, :], k == 0, False)
                            mm.then_inc(ms["h_used"], 1)

                        pe.wait_ge(xl_ready, g * DH + DH)
                        if b == 0:
                            pe.wait_ge(ms["ct_lo"], occ + 1)
                            pe.wait_ge(ms["sel"], 16 * (occ + 1))
                            pe.wait_ge(ms["b2_lo"], occ + 1)
                        pe.wait_ge(x_updated, ONE + e * 2)
                        for j in range(TT):
                            tok = slice(j * P, (j + 1) * P)
                            for f in range(DH):
                                dst = PS[:, 0, j * NR:(j + 1) * NR]
                                for n, (x_, c_) in enumerate(((XH, 0), (XL, 0), (XH, 1))):
                                    mm = pe.matmul(dst, x_[:, par, f, tok], CT[:, c_, f, :], start=f == 0 and n == 0,
                                                   stop=f == DH - 1 and n == 2)
                        mm.then_inc(ms["logits"], 1)
                        pe.wait_ge(y_copied, ONE + e * DH)
                        for k in range(MT):
                            if k == ST:
                                pe.wait_ge(ms["g2"], s + 1)
                                for j in range(TT):
                                    mm = pe.transpose(PS[:, 1, j * P:(j + 1) * P], G2[:, j, :].bitcast(F32), IDENT[:])
                                mm.then_inc(ms["gt"], 1)
                            up(k)
                            if k == ST:
                                pe.wait_ge(ms["gt_ready"], s + 1)
                            if k >= ST:
                                gates(k)
                            if k == 12 and g < LAST:
                                pe.wait_ge(ms["scores"], s + 1)
                                ln_transpose_pe(pe, g + 1, 1 - par, (0, 1))
                            if k >= LAG:
                                down(k - LAG)
                        for k in range(MT - LAG, MT):
                            down(k)
                        for f in range(DH):
                            cols = slice(f * P, (f + 1) * P)
                            pe.matmul(PS[:, 6 + f, :], B2[:, 0, cols], GT[:], start=False, stop=False)
                            pe.matmul(PS[:, 6 + f, :], B2[:, 1, cols], GT[:], start=False, stop=True).then_inc(y_done, 1)
                        epilogue_transpose_pe(pe, e, g, g < LAST)


        def attn_phase(phase, first_layer):
            A = a0 if first_layer else a1
            NI = 4 if first_layer else 3
            NK = 8 if first_layer else 2
            NV = 2 if first_layer else 1
            VH = HEADS if first_layer else KV
            COLS = 4 * D if first_layer else 3 * D + 3 * KV * HD
            with ExitStack() as ctx:
                def ab(name, shape, dt=F32):
                    return sb(ctx, f"{name}_{phase}", shape, dt)

                W = ab("W", [P, 2, DH, COLS], F32R)
                PLACE = ab("PLACE", [P, 4, 4, P], F32R)
                QX = ab("QX", [P, HEADS])
                KX = ab("KX", [P, SEQ])
                IDB = ab("IDB", [P, P], BF16)
                MKB = ab("MKB", [P, P], BF16)
                MTB = ab("MTB", [P, P], BF16)
                QZ = ab("QZ", [P, HEADS, SEQ], F32R)
                KS = ab("KS", [P, NK, SEQ], F32R)
                QKH = ab("QKH", [P, NI, SEQ], F32R)
                QKL = ab("QKL", [P, NI, SEQ], F32R)
                V = ab("V", [P, TT, VH, HD + 1])
                NM = ab("NM", [P, TT, HEADS])
                MROW = ab("MROW", [4, 2, SEQ], F32R)
                TRI = [sum(SEQ - P * x for x in range(kt)) for kt in range(TT + 1)]
                PT = ab("PT", [P, 2, 2, TRI[TT]])
                WR = PT[:].rearrange("p a b n -> p (a b n)")[:, 0:DH * COLS].rearrange("p (h n) -> p h n", h=DH)
                RCP = ab("RCP", [P, 2, TT])
                CTX = ab("CTX", [P, TT, D])
                if first_layer:
                    BQK = ab("BQK", [P, 4])
                    BVB = ab("BVB", [P, D])
                    BOB = ab("BOB", [P, D])
                    V0 = 2 * D
                    O0 = 3 * D
                else:
                    COS = ab("COS", [P, SEQ])
                    SIN = ab("SIN", [P, SEQ])
                    RA = ab("RA", [P, 2, SEQ])
                    RB_ = ab("RB", [P, 2, SEQ])
                    RC = ab("RC", [P, 3, SEQ])
                    K0 = 2 * D
                    V0 = K0 + 2 * KV * HD
                    O0 = V0 + KV * HD
                block = ctx.enter_context(nc.Block())

                def steps(eng):
                    with eng.Fori(0, BATCHES // 2) as i:
                        for u in range(2):
                            b = 2 * i + u
                            yield i, u, b, b, 4 * phase + b

                core = []
                for k in range(4 * HEADS + 24 + 16):
                    if k < 4 * HEADS:
                        core.append(("S", k))
                    if k >= 17 and (k - 17) % 16 == 0 and (k - 17) // 16 < 4:
                        core.append(("NMT", (k - 17) // 16))
                    if k >= 24 and k % 2 == 0 and (k - 24) // 2 < 2 * HEADS:
                        x = (k - 24) // 2
                        core.append(("ST", x))
                        if x >= 5 and x % 4 == 1:
                            core.append(("PV", (x - 5) // 4))
                core.append(("PV", HEADS // 2 - 1))
                assert [x for x in core if x[0] == "NMT"] == [("NMT", y) for y in range(4)]
                assert sum(x[0] == "PV" for x in core) == HEADS // 2

                def kidx(z):
                    return z // 2 if first_layer else z // 8

                @block.sync
                def _(sp):
                    sp.dma_start(WR, t["a0_w" if first_layer else "a1_w"]).then_inc(A["load"], 16)
                    if first_layer:
                        consts = [(BQK[:], t["a0_bqk"]), (BVB[:], t["a0_bv"].partition_broadcast(P)),
                                  (BOB[:], t["a0_bo"].partition_broadcast(P)), (QX[:], t["c_qx"]), (KX[:], t["c_kx"])]
                    else:
                        consts = [(COS[:], t["c_cos"]), (SIN[:], t["c_sin"]), (KX[:], t["c_kx"])]
                    for dst, src in consts:
                        sp.dma_start(dst, src).then_inc(A["const"], 16)
                    for i, u, b, a, g in steps(sp):
                        for y in range(4):
                            sp.wait_ge(A["mrow"], 4 * a + y + 1)
                            for zi in range(4):
                                z = 4 * y + zi
                                row = 64 * (z % 2) + 50
                                sp.dma_start(QZ[row:row + 1, z, :].bitcast(F32),
                                             MROW[zi:zi + 1, y % 2, :].bitcast(F32)).then_inc(A["row"], 16)

                N_CONST = 16 * (5 if first_layer else 3)

                @block.gpsimd
                def _(pool):
                    pool.dma_start(PLACE[:].rearrange("p a b c -> p (a b c)"), t["c_place"]).then_inc(A["cast"], 16)
                    pool.dma_start(IDB[:], t["c_ident"]).then_inc(A["cast"], 16)
                    pool.dma_start(MKB[:], t["c_mask"]).then_inc(A["cast"], 16)
                    pool.dma_start(MTB[:], t["c_maskT"]).then_inc(A["cast"], 16)
                    if first_layer:
                        pool.wait_ge(A["const"], N_CONST)
                    for i, u, b, a, g in steps(pool):
                        if first_layer:
                            pool.wait_ge(xn_ready, g * TT + TT)
                            xs = X[:, bass.ds(b * TT, TT), :]
                            pool.tensor_tensor(xs, xs, BOB[:].unsqueeze(1).broadcast_to([P, TT, D]),
                                               ALU.add).then_inc(A["bias"], 1)
                        else:
                            for n in range(NI):
                                w = P if n < 2 else KV * HD
                                pool.wait_ge(A["rope"], 6 * a + 2 * n + 2)
                                pool.tensor_tensor(RC[0:w, n, :], RA[0:w, n % 2, :], RB_[0:w, n % 2, :],
                                                   ALU.add).then_inc(A["sum"], 1)
                                pool.wait_ge(A["hi"], NI * a + n + 1)
                                pool.tensor_tensor(QKL[0:w, n, :], RC[0:w, n, :], QKH[0:w, n, :].bitcast(F32),
                                                   ALU.subtract).then_inc(A["lo"], 1)
                        ln_rstd_pool(pool, g + 1)

                @block.scalar
                def _(act):
                    act.wait_ge(A["load"], 16)
                    act.activation(W[:, 0, :, :], WR, ACT.Copy).then_inc(A["w_hi"], 1)
                    act.wait_ge(A["const"], N_CONST)
                    for i, u, b, a, g in steps(act):
                        for n in range(NI):
                            if first_layer:
                                act.wait_ge(A["proj"], NI * a + n + 1)
                                act.activation(QKH[:, n, :], PS[:, n, :], ACT.Identity,
                                               bias=BQK[:, n:n + 1]).then_inc(A["hi"], 1)
                            else:
                                w = P if n < 2 else KV * HD
                                act.wait_ge(A["sum"], NI * a + n + 1)
                                act.activation(QKH[0:w, n, :], RC[0:w, n, :], ACT.Copy).then_inc(A["hi"], 1)
                        for n in range(8):
                            act.wait_ge(A["place_q"], 8 * a + n + 1)
                            for half in range(2):
                                rows = slice(64 * half, 64 * half + 64)
                                z = 2 * n + half
                                if first_layer:
                                    act.activation(QZ[rows, z, :], PS[rows, n % 2, :], ACT.Identity,
                                                   bias=QX[rows, z:z + 1]).then_inc(A["qz"], 1)
                                else:
                                    act.activation(QZ[rows, z, :], PS[rows, n % 2, :], ACT.Copy).then_inc(A["qz"], 1)
                        ln_hi_act(act, g + 1, 1 - u, (6, 7))
                        for kind, k in core:
                            if kind == "NMT":
                                act.wait_ge(A["mt"], 4 * a + k + 1)
                                act.wait_ge(A["row"], ONE + 256 * a + 64 * max(k - 1, 0))
                                act.activation(MROW[:, k % 2, :], PS[0:4, 7, :], ACT.Copy).then_inc(A["mrow"], 1)
                            if kind == "ST":
                                p, kt = divmod(k, TT)
                                n = SEQ - P * kt
                                act.wait_ge(A["st"], 32 * a + k + 1)
                                if kt == 0:
                                    act.wait_ge(A["pv"], ring(a, 8, p, 2))
                                act.activation(PT[:, p % 2, :, TRI[kt]:TRI[kt] + n],
                                               PS[:, 2 + 2 * (k % 2):4 + 2 * (k % 2), 0:n], ACT.Exp,
                                               scale=0.25).then_inc(A["exp"], 1)
                        for f in range(DH):
                            act.wait_ge(A["ct"], DH * a + f + 1)
                            act.activation(QKH[:, f, :], PS[:, f, :], ACT.Copy).then_inc(A["ct_hi"], 1)

                @block.vector
                def _(dve):
                    dve.memset(QZ[:].bitcast(F32), 0.0).then_inc(A["zero"], 1)
                    dve.memset(V[:, :, :, HD:HD + 1], 1.0).then_inc(A["zero"], 1)
                    dve.wait_ge(A["w_hi"], 1)
                    dve.tensor_tensor(W[:, 1, :, :], WR, W[:, 0, :, :].bitcast(F32), ALU.subtract).then_inc(A["w_lo"], 1)
                    dve.wait_ge(A["const"], N_CONST)
                    for i, u, b, a, g in steps(dve):
                        nb = next_batch(i, u)
                        for n in range(NI):
                            if first_layer:
                                dve.wait_ge(A["hi"], NI * a + n + 1)
                                dve.scalar_tensor_tensor(out=QKL[:, n, :], in0=PS[:, n, :], scalar=BQK[:, n:n + 1],
                                                         in1=QKH[:, n, :].bitcast(F32), op0=ALU.add,
                                                         op1=ALU.subtract).then_inc(A["lo"], 1)
                            else:
                                w = P if n < 2 else KV * HD
                                dve.wait_ge(A["proj"], NI * a + n + 1)
                                if n == 2:
                                    dve.wait_ge(A["sum"], NI * a + 1)
                                dve.tensor_tensor(RA[0:w, n % 2, :], PS[0:w, 2 * n, :], COS[0:w, :], ALU.mult).then_inc(A["rope"], 1)
                                dve.tensor_tensor(RB_[0:w, n % 2, :], PS[0:w, 2 * n + 1, :], SIN[0:w, :], ALU.mult).then_inc(A["rope"], 1)
                        for jj in range(NV):
                            dve.wait_ge(A["v"], NV * a + jj + 1)
                            if first_layer:
                                dve.tensor_tensor(V[:, 2 * jj:2 * jj + 2, :, 0:HD],
                                                  PS[:, 4 + jj, :].rearrange("p (j h d) -> p j h d", j=2, h=HEADS),
                                                  BVB[:].rearrange("p (h d) -> p h d", d=HD).unsqueeze(1).broadcast_to([P, 2, HEADS, HD]),
                                                  ALU.add).then_inc(A["v_ready"], 1)
                            else:
                                dve.tensor_copy(V[:, :, :, 0:HD],
                                                PS[:, 6, 0:TT * KV * HD].rearrange("p (j h d) -> p j h d", j=TT, h=KV)).then_inc(A["v_ready"], 1)
                        ln_stats_dve(dve, nb, g + 1)
                        for n in range(NK):
                            dve.wait_ge(A["place_k"], NK * a + n + 1)
                            dve.tensor_tensor(KS[:, n, :], PS[:, 2 + n % 2, :], KX[:], ALU.add).then_inc(A["kz"], 1)
                        ln_norm_dve(dve, nb, g + 1, 1 - u)
                        for kind, k in core:
                            if kind == "S":
                                z, qt = divmod(k, TT)
                                dve.wait_ge(A["s"], 64 * a + k + 1)
                                dve.tensor_reduce(NM[:, qt, z:z + 1], PS[:, k % 2, 0:P * (qt + 1)], AX.X, ALU.max,
                                                  negate=True).then_inc(A["smax"], 1)
                                if k == 1:
                                    ln_lo_dve(dve, g + 1, 1 - u, (6, 7))
                            if kind == "PV":
                                dve.wait_ge(A["pv"], ONE + 8 * a + k + 1)
                                o = PS[:, 6, 0:2 * TT * (HD + 1)].rearrange("p (z q d) -> p z q d", z=2, q=TT)
                                dve.reciprocal(RCP[:], o[:, :, :, HD]).then_inc(A["ctx_recip"], 1)
                                dve.wait_ge(A["ctx_recip"], 8 * a + k + 1)
                                if first_layer:
                                    dst = CTX[:, :, 2 * HD * k:2 * HD * (k + 1)].rearrange("p q (z d) -> p z q d", z=2)
                                else:
                                    tl, cc = divmod(k, 4)
                                    dst = CTX[:, :, tl * P:(tl + 1) * P].rearrange("p q (z c d) -> p z q c d", z=2, c=4)[:, :, :, cc, :]
                                dve.tensor_tensor(dst, o[:, :, :, 0:HD], RCP[:].unsqueeze(3).broadcast_to([P, 2, TT, HD]),
                                                  ALU.mult).then_inc(A["ctx"], 1)
                        for f in range(DH):
                            dve.wait_ge(A["ct_hi"], DH * a + f + 1)
                            dve.tensor_tensor(QKL[:, f, :], PS[:, f, :], QKH[:, f, :].bitcast(F32),
                                              ALU.subtract).then_inc(A["ct_lo"], 1)
                        if first_layer:
                            dve.wait_ge(A["bias"], a + 1)
                        for jj in range(2):
                            dve.wait_ge(A["o"], 2 * a + jj + 1)
                            xs = X[:, bass.ds(b * TT + 2 * jj, 2), :]
                            dve.tensor_tensor(xs, PS[:, 2 + jj, :].rearrange("p (j d) -> p j d", j=2), xs,
                                              ALU.add).then_inc(A["x"], 1)

                @block.tensor
                def _(pe):
                    pe.wait_ge(A["w_lo"], 1)
                    pe.wait_ge(A["cast"], 64)
                    pe.wait_ge(A["zero"], 2)
                    for i, u, b, a, g in steps(pe):
                        xh, xl = XH[:, u, :, :], XL[:, u, :, :]

                        def project(dst, cols):
                            for f in range(DH):
                                mm = three_passes(pe, dst, W[:, 0, f, cols], W[:, 1, f, cols], xh[:, f, :], xl[:, f, :],
                                                  f == 0, f == DH - 1)
                            return mm

                        pe.wait_ge(xl_ready, g * DH + DH)
                        pe.wait_ge(A["x"], ONE + 2 * a)
                        for n in range(NI):
                            if first_layer:
                                project(PS[:, n, :], slice(n * P, (n + 1) * P)).then_inc(A["proj"], 1)
                            else:
                                for sw in range(2):
                                    c0, w = (sw * D + n * P, P) if n < 2 else (K0 + sw * KV * HD, KV * HD)
                                    mm = project(PS[0:w, 2 * n + sw, :], slice(c0, c0 + w))
                                mm.then_inc(A["proj"], 1)
                        pe.wait_ge(A["ctx"], ONE + 8 * a)
                        w = VH * HD
                        for j in range(TT):
                            tok = slice(j * P, (j + 1) * P)
                            dst = PS[:, 4 + j // 2, (j % 2) * w:(j % 2 + 1) * w] if first_layer else PS[:, 6, j * w:(j + 1) * w]
                            for f in range(DH):
                                mm = three_passes(pe, dst, xh[:, f, tok], xl[:, f, tok], W[:, 0, f, V0:V0 + w],
                                                  W[:, 1, f, V0:V0 + w], f == 0, f == DH - 1)
                            if not first_layer and j == TT - 1 or first_layer and j % 2:
                                mm.then_inc(A["v"], 1)
                        pe.wait_ge(A["lo"], NI * a + NI)
                        for n in range(8):
                            tl, cc = divmod(n, 4)
                            if n >= 2:
                                pe.wait_ge(A["qz"], 16 * a + 2 * (n - 1))
                            pe.matmul(PS[:, n % 2, :], PLACE[:, 0, cc, :], QKH[:, tl, :], start=True, stop=False)
                            pe.matmul(PS[:, n % 2, :], PLACE[:, 1, cc, :], QKL[:, tl, :], start=False,
                                      stop=True).then_inc(A["place_q"], 1)
                            if n < NK:
                                if n >= 2:
                                    pe.wait_ge(A["kz"], NK * a + n - 1)
                                r, src = (P, 2 + tl) if first_layer else (KV * HD, 2)
                                pe.matmul(PS[:, 2 + n % 2, :], PLACE[0:r, 2, cc, :], QKH[0:r, src, :], start=True, stop=False)
                                pe.matmul(PS[:, 2 + n % 2, :], PLACE[0:r, 3, cc, :], QKL[0:r, src, :], start=False,
                                          stop=True).then_inc(A["place_k"], 1)
                        pe.wait_ge(A["v_ready"], NV * a + NV)
                        ln_transpose_pe(pe, g + 1, 1 - u, (6, 7))
                        pe.wait_ge(A["qz"], 16 * a + 16)
                        pe.wait_ge(A["kz"], NK * a + NK)
                        for kind, k in core:
                            if kind == "S":
                                z, qt = divmod(k, TT)
                                if k >= 2:
                                    pe.wait_ge(A["smax"], ring(a, 64, k, 2))
                                tok = slice(qt * P, (qt + 1) * P)
                                pe.matmul(PS[:, k % 2, 0:P * (qt + 1)], QZ[:, z, tok], KS[:, kidx(z), 0:P * (qt + 1)],
                                          start=True, stop=False)
                                pe.matmul(PS[:, k % 2, tok], IDB[:], MKB[:], start=False, stop=True).then_inc(A["s"], 1)
                            if kind == "NMT":
                                pe.wait_ge(A["smax"], ONE + 64 * a + 16 * (k + 1))
                                if k == 0:
                                    pe.wait_ge(xl_ready, (g + 1) * DH + DH)
                                else:
                                    pe.wait_ge(A["mrow"], 4 * a + k)
                                for qt in range(TT):
                                    mm = pe.transpose(PS[0:4, 7, qt * P:(qt + 1) * P], NM[:, qt, 4 * k:4 * k + 4], IDENT[:])
                                mm.then_inc(A["mt"], 1)
                            if kind == "ST":
                                n, kt = divmod(k, TT)
                                if k % 8 == 0:
                                    pe.wait_ge(A["row"], ONE + 256 * a + 64 * (k // 8 + 1))
                                if k >= 2:
                                    pe.wait_ge(A["exp"], ring(a, 32, k, 2))
                                for zi in range(2):
                                    z, bank = 2 * n + zi, 2 + 2 * (k % 2) + zi
                                    pe.matmul(PS[:, bank, 0:SEQ - P * kt], KS[:, kidx(z), kt * P:(kt + 1) * P],
                                              QZ[:, z, kt * P:SEQ], start=True, stop=False)
                                    mm = pe.matmul(PS[:, bank, 0:P], IDB[:], MTB[:], start=False, stop=True)
                                mm.then_inc(A["st"], 1)
                            if kind == "PV":
                                pe.wait_ge(A["exp"], ONE + 32 * a + 4 * (k + 1))
                                pe.wait_ge(A["ctx"], ONE + 8 * a + k)
                                for zi in range(2):
                                    z = 2 * k + zi
                                    vh = z if first_layer else (z // 8) * 2 + z % 2
                                    for qt in range(TT):
                                        c0 = (zi * TT + qt) * (HD + 1)
                                        for kt in range(qt + 1):
                                            at = TRI[kt] + (qt - kt) * P
                                            mm = pe.matmul(PS[:, 6, c0:c0 + HD + 1], PT[:, k % 2, zi, at:at + P],
                                                           V[:, kt, vh, :], start=kt == 0, stop=kt == qt)
                                mm.then_inc(A["pv"], 1)
                        pe.wait_ge(A["ctx"], ONE + 8 * a + 8)
                        for f in range(DH):
                            for j in range(TT):
                                mm = pe.transpose(PS[:, f, j * P:(j + 1) * P], CTX[:, j, f * P:(f + 1) * P], IDENT[:])
                            mm.then_inc(A["ct"], 1)
                        pe.wait_ge(A["ct_lo"], DH * a + DH)
                        for j in range(TT):
                            tok = slice(j * P, (j + 1) * P)
                            for f in range(DH):
                                mm = three_passes(pe, PS[:, 2 + j // 2, (j % 2) * D:(j % 2 + 1) * D], QKH[:, f, tok],
                                                  QKL[:, f, tok], W[:, 0, f, O0:O0 + D], W[:, 1, f, O0:O0 + D],
                                                  f == 0, f == DH - 1)
                            if j % 2:
                                mm.then_inc(A["o"], 1)


        def run(kinds, first_phase, WG=None, WD=None):
            for phase, kind in enumerate(kinds, first_phase):
                seen = PHASES[:phase].count(kind)
                e0 = BATCHES * sum(x in ("ffn", "moe") for x in PHASES[:phase])
                if kind == "ffn":
                    ffn_phase(phase, seen, WG, WD, e0)
                elif kind == "moe":
                    moe_phase(phase, seen, e0)
                else:
                    attn_phase(phase, kind == "attn0")

        lut_phases = max([n + 1 for n, x in enumerate(PHASES) if x == "ffn"], default=0)
        with ExitStack() as keep:
            if lut_phases:
                WG, WD = ffn_weights(keep)
                run(PHASES[:lut_phases], 0, WG, WD)
        run(PHASES[lut_phases:], lut_phases)

        with nc.Block() as block:
            @block.sync
            def _(sp):
                for b in range(BATCHES):
                    sp.dma_start(out[b].rearrange("(j p) d -> p j d", p=P),
                                 X[:, b * TT:(b + 1) * TT, :]).then_inc(stored, 16)
                sp.wait_ge(stored, 16 * BATCHES)


_INS = ["L0_attn_x", "L0_attn_Wqkv", "L0_attn_b_qkv", "L0_attn_Wout", "L0_attn_b_out", "L0_ffn_lut",
        "L0_ffn_gate_idx", "L0_ffn_up_idx", "L0_ffn_down_idx", "L1_attn_Wq", "L1_attn_Wk", "L1_attn_Wv",
        "L1_attn_Wproj", "L1_ffn_shared_w1", "L1_ffn_shared_b1", "L1_ffn_shared_w2", "L1_ffn_shared_b2",
        "L1_ffn_routed_w1", "L1_ffn_routed_b1", "L1_ffn_routed_w2", "L1_ffn_routed_b2", "L1_ffn_centroids",
        "L1_ffn_bias"]


def layouts(x):
    a = {}
    w1 = np.zeros((D, MT * P), np.float32)
    w2 = np.zeros((MT * P, D), np.float32)
    b1 = np.zeros(MT * P, np.float32)
    n_routed, n_shared = NR * EF, NS * EF
    w1[:, :n_routed] = x["L1_ffn_routed_w1"].transpose(1, 0, 2).reshape(D, -1)
    w1[:, n_routed:n_routed + n_shared] = x["L1_ffn_shared_w1"].transpose(1, 0, 2).reshape(D, -1)
    w2[:n_routed] = x["L1_ffn_routed_w2"].reshape(-1, D)
    w2[n_routed:n_routed + n_shared] = x["L1_ffn_shared_w2"].reshape(-1, D)
    b1[:n_routed] = x["L1_ffn_routed_b1"].reshape(-1)
    b1[n_routed:n_routed + n_shared] = x["L1_ffn_shared_b1"].reshape(-1)
    up = w1.reshape(DH, P, MT, P).transpose(2, 1, 0, 3).reshape(MT, P, DH * P)
    down = w2.reshape(MT, P, D)
    a["m_w"] = np.concatenate([up, down], -1)[MORDER]
    a["m_b1"] = b1.reshape(MT, P).T
    a["m_centroids"] = x["L1_ffn_centroids"].T.reshape(DH, P, NR).transpose(1, 0, 2)
    b2 = np.zeros((P, D), np.float32)
    b2[:NR] = b2[NR:2 * NR] = x["L1_ffn_routed_b2"]
    a["m_b2"] = b2
    a["m_bs2"] = x["L1_ffn_shared_b2"].reshape(NS, DH, P).transpose(2, 0, 1)
    a["L1_ffn_bias"] = x["L1_ffn_bias"]
    w = np.concatenate([x["L0_attn_Wqkv"].T, x["L0_attn_Wout"].T], 1)
    a["a0_w"] = w.reshape(DH, P, 4 * D).transpose(1, 0, 2)
    a["a0_bqk"] = x["L0_attn_b_qkv"][:2 * D].reshape(4, P).T
    a["a0_bv"], a["a0_bo"] = x["L0_attn_b_qkv"][2 * D:], x["L0_attn_b_out"]
    wq = x["L1_attn_Wq"].reshape(D, 2, 2, 4, 2, HD // 2).transpose(0, 1, 3, 2, 4, 5)
    wk = x["L1_attn_Wk"].reshape(D, KV, 2, HD // 2)
    w = np.concatenate([wq.reshape(D, D), wq[..., ::-1, :].reshape(D, D), wk.reshape(D, -1),
                        wk[..., ::-1, :].reshape(D, -1), x["L1_attn_Wv"], x["L1_attn_Wproj"]], 1)
    a["a1_w"] = w.reshape(DH, P, -1).transpose(1, 0, 2)
    for n in ("L0_attn_x", "L0_ffn_lut", "L0_ffn_gate_idx", "L0_ffn_up_idx", "L0_ffn_down_idx"):
        a[n] = x[n]
    return {n: np.ascontiguousarray(v) for n, v in a.items()}


def kernel(**inputs):
    import concourse.bacc as bacc
    from concourse.bass_utils import run_bass_kernel_spmd

    nc = bacc.Bacc("TRN2", target_bir_lowering=False, num_devices=1)
    arrays = layouts({n: np.asarray(inputs[n]) for n in _INS})
    arrays.update(constants())
    t = {n: nc.dram_tensor("in_" + n, a.shape, mybir.dt.from_np(a.dtype), kind="ExternalInput").ap()
         for n, a in arrays.items()}
    shape = (BATCHES, SEQ, D)
    out = nc.dram_tensor("out_x", shape, F32, kind="ExternalOutput").ap()
    kernel_program(nc, t, out)
    r = run_bass_kernel_spmd(nc, [{"in_" + n: a for n, a in arrays.items()}], core_ids=[0])
    return r.results[0]["out_x"]
```

```python
from contextlib import ExitStack

import numpy as np

import concourse.bass as bass
from concourse import mybir


F32 = mybir.dt.float32
F32R = mybir.dt.float32r
BF16 = mybir.dt.bfloat16
I32 = mybir.dt.int32
ACT = mybir.ActivationFunctionType
ALU = mybir.AluOpType
AX = mybir.AxisListType

P = 128
BATCHES = 4
SEQ = 512
D = 256
DH = D // P
TT = SEQ // P
TILES = BATCHES * TT
EPS = 1e-5
HEADS = 16
HD = D // HEADS
KV = 4

FF = 688
FT = -(-FF // P)
FW = [min(P, FF - P * m) for m in range(FT)]
LUT = 16

NS, NR, EF, TOPK = 2, 16, 176, 4
RT = NR * EF // P
ST = -(-NS * EF // P)
MT = RT + ST
MW = [P] * RT + [min(P, NS * EF - P * m) for m in range(ST)]
MORDER = list(range(RT, MT)) + list(range(RT))
PAD = -1.0e30

ONE = 1

PHASES = ["ffn", "attn0", "ffn", "moe", "attn1", "moe"]
ATT_SEMS = ("load", "w_hi", "w_lo", "const", "cast", "zero", "proj", "rope", "sum", "hi", "lo", "v", "v_ready",
            "place_q", "qz", "place_k", "kz", "s", "smax", "mt", "mrow", "row", "st", "exp", "pv", "pv_copied",
            "sums", "recip", "recip_wide", "spread",
            "ctx", "ctx_hi", "ctx_lo", "o", "x", "bias")


def hi_lo(x):
    u = np.asarray(x, np.float32)
    m, e = np.frexp(u.astype(np.float64))
    hi = np.ldexp(np.round(m * 4096) / 4096, e).astype(np.float32)
    return hi, (u - hi).astype(np.float32)


def constants():
    c = {}
    c["c_ident"] = np.eye(P, dtype=np.float32)
    q = np.arange(P)
    c["c_mask"] = np.where(q[None, :] > q[:, None], np.float32(PAD), np.float32(0))
    c["c_maskT"] = c["c_mask"].T.copy()
    unit = np.arange(NR * EF) // EF
    sel = np.zeros((P, NR * EF), np.float32)
    sel[:NR] = unit[None, :] == np.arange(NR)[:, None]
    sel[NR:2 * NR] = sel[:NR]
    c["c_sel"] = sel
    place = np.zeros((P, 4, HEADS // 4, P), np.float32)
    for cc in range(4):
        for half in range(2):
            for d in range(HD):
                src, dst = HD * (2 * cc + half) + d, 64 * half + d
                place[src, 0, cc, dst] = place[src, 0, cc, dst + 2 * HD] = 1
                place[src, 1, cc, dst + HD] = 1
                place[src, 2, cc, dst] = place[src, 2, cc, dst + HD] = 1
                place[src, 3, cc, dst + 2 * HD] = 1
    c["c_place"] = place.reshape(P, 16 * P)
    c["c_pick"] = np.kron(np.eye(4), np.eye(2 * HD)[:, HD:HD + 1]).astype(np.float32)
    m = np.arange(1, HEADS + 1, dtype=np.float32) * np.float32(8.0 / HEADS)
    slopes = (np.float32(1.0) / np.float32(2.0) ** m).astype(np.float32)
    s_hi, s_lo = hi_lo(slopes * np.float32(4.0))
    qx = np.zeros((P, HEADS), np.float32)
    kx = np.zeros((P, SEQ), np.float32)
    for half in range(2):
        qx[64 * half + 48], qx[64 * half + 49] = s_hi, s_lo
        kx[64 * half + 48] = kx[64 * half + 49] = np.arange(1 - SEQ, 1)
        kx[64 * half + 50] = 1
    c["c_qx"], c["c_kx"] = qx, kx
    inv = (1.0 / np.float32(10000.0) ** (np.arange(0, HD, 2, dtype=np.float32) / np.float32(HD))).astype(np.float32)
    ang = np.arange(SEQ, dtype=np.float32)[:, None] * inv[None, :]
    ang = np.concatenate([ang, ang], -1).T
    c["c_cos"] = np.tile(np.cos(ang), (P // HD, 1)).astype(np.float32)
    sign = np.where(np.arange(HD) < HD // 2, np.float32(-1), np.float32(1))[:, None]
    c["c_sin"] = np.tile(sign * np.sin(ang), (P // HD, 1)).astype(np.float32)
    return c


def kernel_program(nc, t, out):
    with ExitStack() as top:
        def sb(ctx, name, shape, dt=F32):
            return ctx.enter_context(nc.sbuf_tensor(name, shape, dt))

        def sem(name):
            return top.enter_context(nc.semaphore(name))

        PS = top.enter_context(nc.psum_tensor("PS", [P, 8, 512], F32))

        X = sb(top, "X", [P, TILES, D])
        XN = sb(top, "XN", [P, 2, TT, D])
        XH = sb(top, "XH", [P, 2, DH, SEQ], F32R)
        XL = sb(top, "XL", [P, 2, DH, SEQ], F32R)
        LST = sb(top, "LST", [P, TT, 6])
        LTMP = sb(top, "LTMP", [P, 5, TT])
        LMEAN = sb(top, "LMEAN", [P, TT])
        LVE = sb(top, "LVE", [P, TT])
        LRS = sb(top, "LRS", [P, TT])
        MHALF = sb(top, "MHALF", [P, TT])
        IDENT = sb(top, "IDENT", [P, P])
        YS = sb(top, "YS", [P, DH, SEQ])

        ln_stats = sem("ln_stats")
        ln_parts = sem("ln_parts")
        ln_var = sem("ln_var")
        ln_rstd = sem("ln_rstd")
        xn_ready = sem("xn_ready")
        xt_done = sem("xt_done")
        xh_ready = sem("xh_ready")
        xl_ready = sem("xl_ready")
        ins = sem("ins")
        ready = sem("ready")
        stored = sem("stored")
        y_done = sem("y_done")
        y_copied = sem("y_copied")
        yt_done = sem("yt_done")
        x_updated = sem("x_updated")

        def ln_stats_dve(dve, b, g):
            for j in range(TT):
                dve.bn_stats(LST[:, j, :], X[:, bass.ds(b * TT + j, 1), :]).then_inc(ln_stats, 1)
            m_even, v_even, m_odd, v_odd = (LST[:, :, k] for k in (1, 2, 4, 5))
            dve.wait_ge(ln_stats, g * TT + TT)
            dve.tensor_tensor(LTMP[:, 0, :], m_even, m_odd, ALU.subtract).then_inc(ln_parts, 1)
            dve.tensor_tensor(LTMP[:, 1, :], v_even, v_odd, ALU.add).then_inc(ln_parts, 1)
            dve.tensor_tensor(LTMP[:, 2, :], m_even, m_odd, ALU.add).then_inc(ln_parts, 1)
            dve.wait_ge(ln_parts, g * 6 + 3)
            dve.tensor_tensor(LTMP[:, 3, :], LTMP[:, 0, :], LTMP[:, 0, :], ALU.mult).then_inc(ln_parts, 1)
            dve.tensor_scalar(LMEAN[:], LTMP[:, 2, :], 0.5, None, ALU.mult).then_inc(ln_parts, 1)
            dve.wait_ge(ln_parts, g * 6 + 5)
            dve.scalar_tensor_tensor(out=LTMP[:, 4, :], in0=LTMP[:, 3, :], scalar=float(D // 4), in1=LTMP[:, 1, :],
                                     op0=ALU.mult, op1=ALU.add).then_inc(ln_parts, 1)
            dve.wait_ge(ln_parts, g * 6 + 6)
            dve.tensor_scalar(LVE[:], LTMP[:, 4, :], 1.0 / D, EPS, ALU.mult, ALU.add).then_inc(ln_var, 1)

        def ln_rstd_pool(pool, g):
            pool.wait_ge(ln_var, g + 1)
            pool.tensor_tensor(LRS[:], LVE[:], MHALF[:], ALU.pow).then_inc(ln_rstd, 1)

        def ln_norm_dve(dve, b, g, par):
            dve.wait_ge(ln_rstd, g + 1)
            for j in range(TT):
                dve.tensor_scalar(XN[:, par, j, :], X[:, bass.ds(b * TT + j, 1), :], LMEAN[:, j:j + 1],
                                  LRS[:, j:j + 1], ALU.subtract, ALU.mult).then_inc(xn_ready, 1)

        def ln_transpose_pe(pe, g, par, banks):
            pe.wait_ge(xn_ready, g * TT + TT)
            for f in range(DH):
                for j in range(TT):
                    mm = pe.transpose(PS[:, banks[f], j * P:(j + 1) * P],
                                      XN[:, par, j, f * P:(f + 1) * P], IDENT[:])
                mm.then_inc(xt_done, 1)

        def ln_hi_act(act, g, par, banks):
            for f in range(DH):
                act.wait_ge(xt_done, g * DH + f + 1)
                act.activation(XH[:, par, f, :], PS[:, banks[f], :], ACT.Copy).then_inc(xh_ready, 1)

        def ln_lo_dve(dve, g, par, banks):
            for f in range(DH):
                dve.wait_ge(xh_ready, g * DH + f + 1)
                dve.tensor_tensor(XL[:, par, f, :], PS[:, banks[f], :], XH[:, par, f, :].bitcast(F32),
                                  ALU.subtract).then_inc(xl_ready, 1)

        def three_passes(pe, psum, w_hi, w_lo, x_hi, x_lo, start, stop):
            pe.matmul(psum, w_hi, x_hi, start=start, stop=False)
            pe.matmul(psum, w_lo, x_hi, start=False, stop=False)
            return pe.matmul(psum, w_hi, x_lo, start=False, stop=stop)

        fs = {n: sem("f_" + n) for n in (
            "idx", "masks", "sums", "sums_used", "diag", "diag_hi", "diag_lo",
            "gate", "up", "silu", "h", "hh", "hl", "h_used")}
        ms = {n: sem("m_" + n) for n in (
            "raw0", "raw1", "raw2", "raw3", "w_hi", "w_lo", "const", "bs_sum", "sel", "zero", "ct_hi", "ct_lo",
            "b2_hi", "b2_lo", "logits", "scores", "gate_steps", "g2", "gt", "gt_ready",
            "hid", "gbc", "relu", "h", "hh", "hl", "h_used", "xn_added")}
        a0 = {n: sem("a0_" + n) for n in ATT_SEMS}
        a1 = {n: sem("a1_" + n) for n in ATT_SEMS}

        with nc.Block() as block:
            @block.sync
            def _(sp):
                for q in (a0["row"], a1["row"]):
                    sp.sem_inc(q, ONE)
                sp.dma_start(IDENT[:], t["c_ident"]).then_inc(ins, 16)
                for b in range(BATCHES):
                    sp.dma_start(X[:, b * TT:(b + 1) * TT, :],
                                 t["L0_attn_x"][b].rearrange("(j p) d -> p j d", p=P)).then_inc(ins, 16)

            @block.gpsimd
            def _(pool):
                for q in (fs["hl"], ms["hl"], a0["ctx_lo"], a1["ctx_lo"]):
                    pool.sem_inc(q, ONE)
                pool.memset(MHALF[:], -0.5).then_inc(ready, 1)
                pool.wait_ge(ready, 1)
                ln_rstd_pool(pool, 0)

            @block.vector
            def _(dve):
                for q in (x_updated, fs["h"], ms["h"], a0["smax"], a0["x"], a1["smax"], a1["x"]):
                    dve.sem_inc(q, ONE)
                dve.wait_ge(ins, 16 * (1 + BATCHES))
                ln_stats_dve(dve, 0, 0)
                ln_norm_dve(dve, 0, 0, 0)
                ln_lo_dve(dve, 0, 0, (0, 1))

            @block.tensor
            def _(pe):
                for q in (y_done, fs["h_used"], ms["h_used"], a0["pv"], a1["pv"]):
                    pe.sem_inc(q, ONE)
                pe.wait_ge(ins, 16 * (1 + BATCHES))
                ln_transpose_pe(pe, 0, 0, (0, 1))

            @block.scalar
            def _(act):
                for q in (y_copied, fs["silu"], ms["relu"], a0["exp"], a1["exp"], a0["pv_copied"], a1["pv_copied"]):
                    act.sem_inc(q, ONE)
                ln_hi_act(act, 0, 0, (0, 1))


        def ring(s, n, k, depth):
            return ONE + s * n + max(k - depth + 1, 0)

        def next_batch(i, u):
            return 2 * i + 1 if u == 0 else 2 - 2 * i

        def epilogue_copy_act(act, e, bias):
            for f in range(DH):
                act.wait_ge(y_done, ONE + e * DH + f + 1)
                if bias is None:
                    act.activation(YS[:, f, :], PS[:, 6 + f, :], ACT.Copy).then_inc(y_copied, 1)
                else:
                    act.activation(YS[:, f, :], PS[:, 6 + f, :], ACT.Identity,
                                   bias=bias[:, f:f + 1]).then_inc(y_copied, 1)

        def epilogue_transpose_pe(pe, e, g, follows=True):
            pe.wait_ge(y_copied, ONE + e * DH + DH)
            if follows:
                pe.wait_ge(xl_ready, (g + 1) * DH + DH)
            for jj in range(2):
                for j in range(2):
                    for f in range(DH):
                        mm = pe.transpose(PS[:, jj, j * D + f * P:j * D + (f + 1) * P],
                                          YS[:, f, (2 * jj + j) * P:(2 * jj + j + 1) * P], IDENT[:])
                mm.then_inc(yt_done, 1)

        def epilogue_add_dve(dve, e, b, follows=True):
            for jj in range(2):
                dve.wait_ge(yt_done, e * 2 + jj + 1)
                xs = X[:, bass.ds(b * TT + 2 * jj, 2), :]
                dve.scalar_tensor_tensor(out=xs, in0=PS[:, jj, :].rearrange("p (j d) -> p j d", j=2), scalar=0.5,
                                         in1=xs, op0=ALU.mult, op1=ALU.add).then_inc(x_updated, 1)

        def ffn_weights(keep):
            WG = sb(keep, "WGU", [P, 2, 2, DH, FF], F32R)
            WD = sb(keep, "WD", [P, 2, FT, D], F32R)
            with ExitStack() as ctx:
                LB = sb(ctx, "LUTB", [P, LUT])
                DG = sb(ctx, "DIAG", [P, LUT, P])
                DHL = sb(ctx, "DIAGHL", [P, LUT, 2, P], F32R)
                IX = sb(ctx, "IDX", [P, 2, FT, D], I32)
                IXD = sb(ctx, "IDXD", [P, DH, FF], I32)
                MK = sb(ctx, "MASKS", [P, 2, LUT, D], F32R)
                units = [("gu", gu, o) for gu in range(2) for o in range(FT)]
                units += [("d", dh, m0) for dh in range(DH) for m0 in range(0, FT, 2)]

                def sums(n):
                    kind, a, c = units[n]
                    if kind == "gu":
                        return [(slice(f * P, (f + 1) * P), FW[c], P, WG[:, a, :, f, c * P:c * P + FW[c]])
                                for f in range(DH)]
                    return [(slice(i * P, i * P + FW[c + i]), P, FW[c + i],
                             WD[0:FW[c + i], :, c + i, a * P:(a + 1) * P]) for i in range(2)]

                with nc.Block() as block:
                    @block.sync
                    def _(sp):
                        sp.dma_start(LB[:], t["L0_ffn_lut"].partition_broadcast(P)).then_inc(fs["idx"], 16)
                        full = (FT - 1) * P
                        for gu, name in enumerate(("L0_ffn_gate_idx", "L0_ffn_up_idx")):
                            sp.dma_start(IX[:, gu, 0:FT - 1, :],
                                         t[name][0:full, :].rearrange("(o p) d -> p o d", p=P)).then_inc(fs["idx"], 16)
                            sp.dma_start(IX[0:FF - full, gu, FT - 1, :], t[name][full:FF, :]).then_inc(fs["idx"], 16)
                        sp.dma_start(IXD[:], t["L0_ffn_down_idx"].rearrange("(h p) f -> p h f", p=P)).then_inc(fs["idx"], 16)

                    @block.vector
                    def _(dve):
                        dve.wait_ge(fs["idx"], 96)
                        for k in range(LUT):
                            dve.tensor_scalar(DG[:, k, :], IDENT[:], LB[:, k:k + 1], None,
                                              ALU.mult).then_inc(fs["diag"], 1)
                        dve.wait_ge(fs["diag"], LUT)
                        dve.tensor_copy(DHL[:, :, 0, :], DG[:]).then_inc(fs["diag_hi"], 1)
                        dve.wait_ge(fs["diag_hi"], 1)
                        dve.tensor_tensor(DHL[:, :, 1, :], DG[:], DHL[:, :, 0, :].bitcast(F32),
                                          ALU.subtract).then_inc(fs["diag_lo"], 1)
                        for n, (kind, a, c) in enumerate(units):
                            if n >= 2:
                                dve.wait_ge(fs["sums"], 2 * (n - 1))
                            if kind == "gu":
                                rows, w = FW[c], D
                                src = IX[0:rows, a, c, :]
                            else:
                                rows, w = P, min(2 * P, FF - c * P)
                                src = IXD[:, a, c * P:c * P + w]
                            for k in range(LUT):
                                last = dve.tensor_scalar(MK[0:rows, n % 2, k, 0:w], src, float(k), None, ALU.is_equal)
                            last.then_inc(fs["masks"], 1)

                    @block.tensor
                    def _(pe):
                        pe.wait_ge(fs["diag_lo"], 1)
                        for n, (kind, a, c) in enumerate(units):
                            rows = FW[c] if kind == "gu" else P
                            pe.wait_ge(fs["masks"], n + 1)
                            for i, (cols, w, orows, _) in enumerate(sums(n)):
                                q = 2 * n + i
                                if q >= 4:
                                    pe.wait_ge(fs["sums_used"], q - 3)
                                dst = PS[0:orows, 2 + q % 4, 0:2 * w].rearrange("p (a n) -> p a n", a=2)
                                for k in range(LUT):
                                    mm = pe.matmul(dst, MK[0:rows, n % 2, k, cols], DHL[0:rows, k, :, 0:w],
                                                   start=k == 0, stop=k == LUT - 1)
                                mm.then_inc(fs["sums"], 1)

                    @block.scalar
                    def _(act):
                        for n in range(len(units)):
                            for i, (cols, w, orows, dst) in enumerate(sums(n)):
                                q = 2 * n + i
                                act.wait_ge(fs["sums"], q + 1)
                                act.activation(dst, PS[0:orows, 2 + q % 4, 0:2 * w].rearrange("p (a n) -> p a n", a=2),
                                               ACT.Copy).then_inc(fs["sums_used"], 1)
            return WG, WD

        def ffn_phase(phase, occ, WG, WD, e0):
            with ExitStack() as ctx:
                SG = sb(ctx, f"SG{phase}", [P, 2, SEQ])
                HF = sb(ctx, f"HF{phase}", [P, 2, SEQ])
                HH = sb(ctx, f"HH{phase}", [P, 2, SEQ], F32R)
                HL = sb(ctx, f"HL{phase}", [P, 2, SEQ], F32R)
                block = ctx.enter_context(nc.Block())

                def steps(eng):
                    with eng.Fori(0, BATCHES // 2) as i:
                        for u in range(2):
                            b = 2 * i + u
                            yield i, u, b, 4 * occ + b, e0 + b, 4 * phase + b

                @block.tensor
                def _(pe):
                    for i, u, b, s, e, g in steps(pe):
                        def up(m):
                            w = FW[m]
                            for gu, (done, freed) in enumerate((("gate", "silu"), ("up", "h"))):
                                pe.wait_ge(fs[freed], ring(s, FT, m, 2))
                                dst = PS[0:w, 2 + 2 * gu + m % 2, :]
                                cols = slice(m * P, m * P + w)
                                for f in range(DH):
                                    mm = three_passes(pe, dst, WG[:, gu, 0, f, cols], WG[:, gu, 1, f, cols],
                                                      XH[:, u, f, :], XL[:, u, f, :], f == 0, f == DH - 1)
                                mm.then_inc(fs[done], 1)

                        def down(m):
                            w = FW[m]
                            pe.wait_ge(fs["hl"], ONE + s * FT + m + 1)
                            for f in range(DH):
                                cols = slice(f * P, (f + 1) * P)
                                mm = three_passes(pe, PS[:, 6 + f, :], WD[0:w, 0, m, cols], WD[0:w, 1, m, cols],
                                                  HH[0:w, m % 2, :], HL[0:w, m % 2, :], m == 0, m == FT - 1)
                                if m == FT - 1:
                                    mm.then_inc(y_done, 1)
                            mm.then_inc(fs["h_used"], 1) if m < FT - 1 else None

                        pe.wait_ge(xl_ready, g * DH + DH)
                        pe.wait_ge(y_copied, ONE + e * DH)
                        for m in range(FT):
                            up(m)
                            if m == 3:
                                pe.wait_ge(x_updated, ONE + e * 2)
                                ln_transpose_pe(pe, g + 1, 1 - u, (0, 1))
                            if m >= 1:
                                down(m - 1)
                        down(FT - 1)
                        epilogue_transpose_pe(pe, e, g)

                @block.scalar
                def _(act):
                    for i, u, b, s, e, g in steps(act):
                        def silu(m):
                            act.wait_ge(fs["gate"], s * FT + m + 1)
                            act.wait_ge(fs["h"], ring(s, FT, m, 2))
                            act.activation(SG[0:FW[m], m % 2, :], PS[0:FW[m], 2 + m % 2, :],
                                           ACT.Silu).then_inc(fs["silu"], 1)

                        def hi(m):
                            act.wait_ge(fs["h"], ONE + s * FT + m + 1)
                            if m >= 2:
                                act.wait_ge(fs["h_used"], ONE + s * (FT - 1) + m - 1)
                            else:
                                act.wait_ge(y_done, ONE + e * DH)
                            act.activation(HH[0:FW[m], m % 2, :], HF[0:FW[m], m % 2, :], ACT.Copy).then_inc(fs["hh"], 1)

                        for m in range(FT):
                            silu(m)
                            if m >= 1:
                                hi(m - 1)
                            if m == 4:
                                ln_hi_act(act, g + 1, 1 - u, (0, 1))
                        hi(FT - 1)
                        epilogue_copy_act(act, e, None)

                @block.vector
                def _(dve):
                    for i, u, b, s, e, g in steps(dve):
                        nb = next_batch(i, u)
                        for m in range(FT):
                            w = FW[m]
                            dve.wait_ge(fs["silu"], ONE + s * FT + m + 1)
                            dve.wait_ge(fs["up"], s * FT + m + 1)
                            dve.wait_ge(fs["hl"], ring(s, FT, m, 2))
                            dve.tensor_tensor(HF[0:w, m % 2, :], SG[0:w, m % 2, :], PS[0:w, 4 + m % 2, :],
                                              ALU.mult).then_inc(fs["h"], 1)
                            if m == 0:
                                ln_stats_dve(dve, nb, g + 1)
                            if m == 1:
                                ln_norm_dve(dve, nb, g + 1, 1 - u)
                            if m == 4:
                                ln_lo_dve(dve, g + 1, 1 - u, (0, 1))
                        epilogue_add_dve(dve, e, b)

                @block.gpsimd
                def _(pool):
                    for i, u, b, s, e, g in steps(pool):
                        for m in range(FT):
                            w = FW[m]
                            pool.wait_ge(fs["hh"], s * FT + m + 1)
                            pool.tensor_tensor(HL[0:w, m % 2, :], HF[0:w, m % 2, :], HH[0:w, m % 2, :].bitcast(F32),
                                               ALU.subtract).then_inc(fs["hl"], 1)
                            if m == 0:
                                ln_rstd_pool(pool, g + 1)


        def moe_phase(phase, occ, e0):
            with ExitStack() as ctx:
                def mb(name, shape, dt=F32):
                    return sb(ctx, f"{name}_{phase}", shape, dt)

                RING = 4
                WRAW = mb("WRAW", [P, RING, DH * P + D])
                W = mb("W", [P, MT, 2, DH * P + D], F32R)
                B1 = mb("B1", [P, MT])
                SEL = mb("SEL", [P, RT, P], F32R)
                B2R = mb("B2R", [P, D])
                B2 = mb("B2", [P, 2, D], F32R)
                BS2 = mb("BS2", [P, NS, DH])
                BS = mb("BS", [P, DH])
                CR = mb("CR", [P, DH, NR])
                CT = mb("CT", [P, 2, DH, NR], F32R)
                RB = mb("RB", [P, NR])
                SC = mb("SC", [P, TT, NR + 8])
                V8 = mb("V8", [P, TT, 8])
                MR = mb("MR", [P, TT, NR + 8])
                GK = mb("GK", [P, TT, NR])
                GS = mb("GS", [P, 3, TT])
                G2 = mb("G2", [P, TT, P], F32R)
                GT = mb("GT", [P, SEQ], F32R)
                HR = mb("HR", [P, 2, SEQ])
                HF = mb("HFM", [P, 2, SEQ])
                HH = mb("HHM", [P, 2, SEQ], F32R)
                HL = mb("HLM", [P, 2, SEQ], F32R)
                block = ctx.enter_context(nc.Block())
                LAG = 2

                STEPS = [(b, b % 2, 4 * occ + b, e0 + b, 4 * phase + b) for b in range(BATCHES)]
                LAST = 4 * len(PHASES) - 1
                CONST = 5 * 16

                @block.sync
                def _(sp):
                    for k in range(MT):
                        if k >= RING:
                            sp.wait_ge(ms["w_lo"], occ * MT + k - RING + 1)
                        sp.dma_start(WRAW[:, k % RING, :], t["m_w"][k]).then_inc(ms[f"raw{k % RING}"], 16)

                def raw_loads(k):
                    before = occ * len(range(k % RING, MT, RING))
                    return 16 * (before + k // RING + 1)

                @block.scalar
                def _(act):
                    for dst, name in ((CR, "m_centroids"), (B1, "m_b1"), (B2R, "m_b2"), (BS2, "m_bs2")):
                        act.dma_start(dst[:], t[name]).then_inc(ms["const"], 16)
                    act.dma_start(RB[:], t["L1_ffn_bias"].partition_broadcast(P)).then_inc(ms["const"], 16)
                    act.wait_ge(ms["const"], occ * CONST + CONST)
                    act.activation(CT[:, 0, :, :], CR[:], ACT.Copy).then_inc(ms["ct_hi"], 1)
                    act.activation(B2[:, 0, :], B2R[:], ACT.Copy).then_inc(ms["b2_hi"], 1)

                    def split_hi(k):
                        m = MORDER[k]
                        act.wait_ge(ms[f"raw{k % RING}"], raw_loads(k))
                        act.activation(W[:, m, 0, :], WRAW[:, k % RING, :], ACT.Copy).then_inc(ms["w_hi"], 1)

                    for b, par, s, e, g in STEPS:
                        def relu(k):
                            m, w = MORDER[k], MW[MORDER[k]]
                            act.wait_ge(ms["hid"], s * MT + k + 1)
                            if m >= RT:
                                act.wait_ge(ms["hl"], ring(s, MT, k, 2))
                                dst = HF
                            else:
                                act.wait_ge(ms["h"], ring(s, RT, k - ST, 2))
                                dst = HR
                            act.activation(dst[0:w, k % 2, :], PS[0:w, 2 + k % 2, :], ACT.Relu,
                                           bias=B1[0:w, m:m + 1]).then_inc(ms["relu"], 1)

                        def hi(k):
                            m, w = MORDER[k], MW[MORDER[k]]
                            if m >= RT:
                                act.wait_ge(ms["relu"], ONE + s * MT + k + 1)
                            else:
                                act.wait_ge(ms["h"], ONE + s * RT + k - ST + 1)
                            act.wait_ge(ms["h_used"], ring(s, MT, k, 2))
                            act.activation(HH[0:w, k % 2, :], HF[0:w, k % 2, :], ACT.Copy).then_inc(ms["hh"], 1)

                        if b == 0:
                            split_hi(0)
                            split_hi(1)
                        act.wait_ge(ms["logits"], s + 1)
                        act.activation(SC[:, :, 0:NR], PS[:, 0, 0:TT * NR].rearrange("p (j n) -> p j n", j=TT),
                                       ACT.Sigmoid).then_inc(ms["scores"], 1)
                        for k in range(MT):
                            if b == 0 and k + 2 < MT:
                                split_hi(k + 2)
                            relu(k)
                            if k >= 1:
                                hi(k - 1)
                            if k == ST:
                                act.wait_ge(ms["gt"], s + 1)
                                act.activation(GT[:], PS[:, 1, :], ACT.Copy).then_inc(ms["gt_ready"], 1)
                            if k == 13 and g < LAST:
                                ln_hi_act(act, g + 1, 1 - par, (0, 1))
                        hi(MT - 1)
                        epilogue_copy_act(act, e, BS)

                @block.gpsimd
                def _(pool):
                    pool.dma_start(SEL[:].rearrange("p m c -> p (m c)"), t["c_sel"]).then_inc(ms["sel"], 16)
                    for b, par, s, e, g in STEPS:
                        def split_lo(k):
                            m = MORDER[k]
                            pool.wait_ge(ms["w_hi"], occ * MT + k + 1)
                            pool.tensor_tensor(W[:, m, 1, :], WRAW[:, k % RING, :], W[:, m, 0, :].bitcast(F32),
                                               ALU.subtract).then_inc(ms["w_lo"], 1)

                        if b == 0:
                            split_lo(0)
                            split_lo(1)
                        for k in range(MT):
                            w = MW[MORDER[k]]
                            if b == 0 and k + 2 < MT:
                                split_lo(k + 2)
                            pool.wait_ge(ms["hh"], s * MT + k + 1)
                            pool.tensor_tensor(HL[0:w, k % 2, :], HF[0:w, k % 2, :], HH[0:w, k % 2, :].bitcast(F32),
                                               ALU.subtract).then_inc(ms["hl"], 1)
                            if k == 5 and g < LAST:
                                ln_rstd_pool(pool, g + 1)

                @block.vector
                def _(dve):
                    for n, (dst, v) in enumerate(((SC[:, :, NR:], PAD), (G2[:].bitcast(F32), 0.0))):
                        dve.memset(dst, v).then_inc(ms["zero"], 1)
                    dve.wait_ge(ms["const"], CONST * (occ + 1))
                    dve.tensor_tensor(BS[:], BS2[:, 0, :], BS2[:, 1, :], ALU.add).then_inc(ms["bs_sum"], 1)
                    dve.wait_ge(ms["ct_hi"], occ + 1)
                    dve.tensor_tensor(CT[:, 1, :, :], CR[:], CT[:, 0, :, :].bitcast(F32), ALU.subtract).then_inc(ms["ct_lo"], 1)
                    dve.wait_ge(ms["b2_hi"], occ + 1)
                    dve.tensor_tensor(B2[:, 1, :], B2R[:], B2[:, 0, :].bitcast(F32), ALU.subtract).then_inc(ms["b2_lo"], 1)
                    dve.wait_ge(ms["zero"], 2 * occ + 2)
                    for b, par, s, e, g in STEPS:
                        steps_done = [s * 11]

                        def link(ins_):
                            steps_done[0] += 1
                            ins_.then_inc(ms["gate_steps"], 1)
                            dve.wait_ge(ms["gate_steps"], steps_done[0])

                        dve.wait_ge(ms["scores"], s + 1)
                        best = SC[:, :, 0:NR]
                        link(dve.tensor_tensor(best, best, RB[:].unsqueeze(1).broadcast_to([P, TT, NR]), ALU.add))
                        for j in range(TT):
                            last = dve.max(V8[:, j, :], SC[:, j, :])
                        link(last)
                        link(dve.memset(V8[:, :, TOPK:], PAD))
                        for j in range(TT):
                            last = dve.match_replace(MR[:, j, :], V8[:, j, :], SC[:, j, :], 2 * PAD)
                        link(last)
                        link(dve.tensor_tensor(GK[:], best, MR[:, :, 0:NR], ALU.not_equal))
                        link(dve.tensor_tensor(GK[:], GK[:], best, ALU.mult))
                        link(dve.tensor_reduce(GS[:, 0, :], GK[:], AX.X, ALU.add))
                        link(dve.tensor_scalar(GS[:, 1, :], GS[:, 0, :], 1e-8, None, ALU.max))
                        link(dve.reciprocal(GS[:, 2, :], GS[:, 1, :]))
                        link(dve.tensor_tensor(GK[:], GK[:], GS[:, 2, :].unsqueeze(2).broadcast_to([P, TT, NR]), ALU.mult))
                        link(dve.tensor_copy(G2[:, :, 0:NR], GK[:]))
                        dve.tensor_tensor(G2[:, :, NR:2 * NR], GK[:], G2[:, :, 0:NR].bitcast(F32),
                                          ALU.subtract).then_inc(ms["g2"], 1)
                        xs = X[:, b * TT:(b + 1) * TT, :]
                        dve.scalar_tensor_tensor(out=xs, in0=XN[:, par, :, :], scalar=0.5, in1=xs, op0=ALU.mult,
                                                 op1=ALU.add).then_inc(ms["xn_added"], 1)
                        for r in range(RT):
                            k = ST + r
                            dve.wait_ge(ms["relu"], ONE + s * MT + k + 1)
                            dve.wait_ge(ms["gbc"], s * RT + r + 1)
                            dve.wait_ge(ms["hl"], ring(s, MT, k, 2))
                            dve.tensor_tensor(HF[:, k % 2, :], HR[:, k % 2, :], PS[:, 4 + r % 2, :],
                                              ALU.mult).then_inc(ms["h"], 1)
                            if g < LAST:
                                if r == 2:
                                    ln_stats_dve(dve, (b + 1) % BATCHES, g + 1)
                                if r == 4:
                                    ln_norm_dve(dve, (b + 1) % BATCHES, g + 1, 1 - par)
                                if r == 11:
                                    ln_lo_dve(dve, g + 1, 1 - par, (0, 1))
                        dve.wait_ge(ms["xn_added"], s + 1)
                        epilogue_add_dve(dve, e, b, g < LAST)

                @block.tensor
                def _(pe):
                    for b, par, s, e, g in STEPS:
                        def gates(k):
                            r = k - ST
                            pe.wait_ge(ms["h"], ring(s, RT, r, 2))
                            pe.matmul(PS[:, 4 + r % 2, :], SEL[:, r, :], GT[:], start=True, stop=True).then_inc(ms["gbc"], 1)

                        def up(k):
                            m, w = MORDER[k], MW[MORDER[k]]
                            if b == 0:
                                pe.wait_ge(ms["w_lo"], occ * MT + k + 1)
                            pe.wait_ge(ms["relu"], ring(s, MT, k, 2))
                            for f in range(DH):
                                cols = slice(f * P, f * P + w)
                                mm = three_passes(pe, PS[0:w, 2 + k % 2, :], W[:, m, 0, cols], W[:, m, 1, cols],
                                                  XH[:, par, f, :], XL[:, par, f, :], f == 0, f == DH - 1)
                            mm.then_inc(ms["hid"], 1)

                        def down(k):
                            m, w = MORDER[k], MW[MORDER[k]]
                            pe.wait_ge(ms["hl"], ONE + s * MT + k + 1)
                            for f in range(DH):
                                cols = slice(DH * P + f * P, DH * P + (f + 1) * P)
                                mm = three_passes(pe, PS[:, 6 + f, :], W[0:w, m, 0, cols], W[0:w, m, 1, cols],
                                                  HH[0:w, k % 2, :], HL[0:w, k % 2, :], k == 0, False)
                            mm.then_inc(ms["h_used"], 1)

                        pe.wait_ge(xl_ready, g * DH + DH)
                        if b == 0:
                            pe.wait_ge(ms["ct_lo"], occ + 1)
                            pe.wait_ge(ms["sel"], 16 * (occ + 1))
                            pe.wait_ge(ms["b2_lo"], occ + 1)
                        pe.wait_ge(x_updated, ONE + e * 2)
                        for j in range(TT):
                            tok = slice(j * P, (j + 1) * P)
                            for f in range(DH):
                                dst = PS[:, 0, j * NR:(j + 1) * NR]
                                for n, (x_, c_) in enumerate(((XH, 0), (XL, 0), (XH, 1))):
                                    mm = pe.matmul(dst, x_[:, par, f, tok], CT[:, c_, f, :], start=f == 0 and n == 0,
                                                   stop=f == DH - 1 and n == 2)
                        mm.then_inc(ms["logits"], 1)
                        pe.wait_ge(y_copied, ONE + e * DH)
                        for k in range(MT):
                            if k == ST:
                                pe.wait_ge(ms["g2"], s + 1)
                                for j in range(TT):
                                    mm = pe.transpose(PS[:, 1, j * P:(j + 1) * P], G2[:, j, :].bitcast(F32), IDENT[:])
                                mm.then_inc(ms["gt"], 1)
                            up(k)
                            if k == ST:
                                pe.wait_ge(ms["gt_ready"], s + 1)
                            if k >= ST:
                                gates(k)
                            if k == 12 and g < LAST:
                                pe.wait_ge(ms["scores"], s + 1)
                                ln_transpose_pe(pe, g + 1, 1 - par, (0, 1))
                            if k >= LAG:
                                down(k - LAG)
                        for k in range(MT - LAG, MT):
                            down(k)
                        for f in range(DH):
                            cols = slice(f * P, (f + 1) * P)
                            pe.matmul(PS[:, 6 + f, :], B2[:, 0, cols], GT[:], start=False, stop=False)
                            pe.matmul(PS[:, 6 + f, :], B2[:, 1, cols], GT[:], start=False, stop=True).then_inc(y_done, 1)
                        epilogue_transpose_pe(pe, e, g, g < LAST)


        def attn_phase(phase, first_layer):
            A = a0 if first_layer else a1
            TILE_ORDER = (0, 2, 1, 3) if first_layer else (0, 2, 1)
            NI = len(TILE_ORDER)
            NK = 8 if first_layer else 2
            NV = 2 if first_layer else 1
            VH = HEADS if first_layer else KV
            COLS = 3 * D if first_layer else 2 * D + 3 * KV * HD
            QUADS = HEADS // 4
            O0 = DH * COLS
            K0 = 2 * D
            V0 = 2 * D if first_layer else K0 + 2 * KV * HD
            with ExitStack() as ctx:
                def ab(name, shape, dt=F32):
                    return sb(ctx, f"{name}_{phase}", shape, dt)

                W = ab("W", [P, 2, O0 + QUADS * D], F32R)
                PLACE = ab("PLACE", [P, 4, 4, P], F32R)
                PICK = ab("PICK", [P, 4])
                KX = ab("KX", [P, SEQ])
                IDB = ab("IDB", [P, P], BF16)
                MKB = ab("MKB", [P, P], BF16)
                MTB = ab("MTB", [P, P], BF16)
                QZ = ab("QZ", [P, HEADS, SEQ], F32R)
                KS = ab("KS", [P, NK, SEQ], F32R)
                QKH = ab("QKH", [P, QUADS, SEQ], F32R)
                QKL = ab("QKL", [P, QUADS, SEQ], F32R)
                V = ab("V", [P, TT, VH, 2 * HD])
                NM = ab("NM", [P, TT, HEADS])
                MROW = ab("MROW", [4, 2, SEQ], F32R)
                TRI = [sum(SEQ - P * x for x in range(kt)) for kt in range(TT + 1)]
                PT = ab("PT", [P, 2, 2, TRI[TT]])
                WR = PT[:].rearrange("p a b n -> p (a b n)")[:, 0:O0 + QUADS * D]
                RECIP = ab("RECIP", [P, TT * 4])

                def r_wide(u):
                    return XN[:, u, 0:2, :].rearrange("p j (z r) -> p (j z) r", r=2 * HD)

                if first_layer:
                    QX = ab("QX", [P, HEADS])
                    BQK = ab("BQK", [P, 4])
                    BVB = ab("BVB", [P, D])
                    BOB = ab("BOB", [P, D])
                else:
                    COS = ab("COS", [P, SEQ])
                    SIN = ab("SIN", [P, SEQ])
                    RA = ab("RA", [P, 2, SEQ])
                    RB_ = ab("RB", [P, 2, SEQ])
                    RC = ab("RC", [P, 3, SEQ])
                block = ctx.enter_context(nc.Block())

                def steps(eng):
                    with eng.Fori(0, BATCHES // 2) as i:
                        for u in range(2):
                            b = 2 * i + u
                            yield i, u, b, b, 4 * phase + b

                LEAD = 24
                core = [("PLACE", 0)]
                for k in range(0, 2 * (4 * QUADS * 2 + 8) + LEAD, 2):
                    x = (k - LEAD) // 2
                    if k // 2 + 1 < HEADS // 2:
                        core.append(("PLACE", k // 2 + 1))
                    for kk in (k, k + 1):
                        if kk < 4 * HEADS:
                            core.append(("S", kk))
                        if kk >= 17 and (kk - 17) % 16 == 0 and (kk - 17) // 16 < QUADS:
                            core.append(("NMT", (kk - 17) // 16))
                    if k in (30, 36, 70):
                        core.append(({30: "LN_STATS", 36: "LN_NORM", 70: "LN_T"}[k], 0))
                    if 0 <= x < 2 * HEADS:
                        core.append(("ST", x))
                    if 0 <= x - 2 < 2 * HEADS:
                        core.append(("PV", x - 2))
                    for name, at in (("COPY", 9), ("SUMS", 10), ("SPREAD", 11), ("HI", 12)):
                        if x >= at and (x - at) % 8 == 0 and (x - at) // 8 < QUADS:
                            core.append((name, (x - at) // 8))
                    core += [("OUT", q) for q, at in enumerate((34, 36, 37, 38)) if x == at]
                for name, n in (("PLACE", 8), ("S", 64), ("NMT", 4), ("ST", 32), ("PV", 32), ("COPY", 4),
                                ("SUMS", 4), ("SPREAD", 4), ("HI", 4), ("OUT", 4), ("LN_T", 1)):
                    assert [x for x in core if x[0] == name] == [(name, y) for y in range(n)], name

                def bank7_read(a, event):
                    done = [x for x in core[:core.index(event)] if x[0] in ("NMT", "SUMS", "SPREAD")]
                    if not done:
                        return A["qz"], 16 * a + 16
                    kind, k = done[-1]
                    return A[{"NMT": "mrow", "SUMS": "recip", "SPREAD": "ctx"}[kind]], 4 * a + k + 1

                def kidx(z):
                    return z // 2 if first_layer else z // 8

                @block.sync
                def _(sp):
                    sp.dma_start(WR, t["a0_w" if first_layer else "a1_w"]).then_inc(A["load"], 16)
                    consts = [(PICK[:], t["c_pick"]), (KX[:], t["c_kx"])]
                    if first_layer:
                        consts += [(BQK[:], t["a0_bqk"]), (BVB[:], t["a0_bv"].partition_broadcast(P)),
                                   (BOB[:], t["a0_bo"].partition_broadcast(P)), (QX[:], t["c_qx"])]
                    else:
                        consts += [(COS[:], t["c_cos"]), (SIN[:], t["c_sin"])]
                    for dst, src in consts:
                        sp.dma_start(dst, src).then_inc(A["const"], 16)
                    for i, u, b, a, g in steps(sp):
                        for y in range(QUADS):
                            sp.wait_ge(A["mrow"], 4 * a + y + 1)
                            for zi in range(4):
                                z = 4 * y + zi
                                row = 64 * (z % 2) + 50
                                sp.dma_start(QZ[row:row + 1, z, :].bitcast(F32),
                                             MROW[zi:zi + 1, y % 2, :].bitcast(F32)).then_inc(A["row"], 16)

                N_CONST = 16 * (6 if first_layer else 4)

                @block.gpsimd
                def _(pool):
                    pool.dma_start(PLACE[:].rearrange("p a b c -> p (a b c)"), t["c_place"]).then_inc(A["cast"], 16)
                    pool.dma_start(IDB[:], t["c_ident"]).then_inc(A["cast"], 16)
                    pool.dma_start(MKB[:], t["c_mask"]).then_inc(A["cast"], 16)
                    pool.dma_start(MTB[:], t["c_maskT"]).then_inc(A["cast"], 16)
                    if first_layer:
                        pool.wait_ge(A["const"], N_CONST)
                    for i, u, b, a, g in steps(pool):
                        if first_layer:
                            pool.wait_ge(xn_ready, g * TT + TT)
                            xs = X[:, bass.ds(b * TT, TT), :]
                            pool.tensor_tensor(xs, xs, BOB[:].unsqueeze(1).broadcast_to([P, TT, D]),
                                               ALU.add).then_inc(A["bias"], 1)
                        else:
                            for n, tile in enumerate(TILE_ORDER):
                                w = P if tile < 2 else KV * HD
                                pool.wait_ge(A["rope"], 6 * a + 2 * n + 2)
                                pool.tensor_tensor(RC[0:w, tile, :], RA[0:w, n % 2, :], RB_[0:w, n % 2, :],
                                                   ALU.add).then_inc(A["sum"], 1)
                                pool.wait_ge(A["hi"], NI * a + n + 1)
                                pool.tensor_tensor(QKL[0:w, tile, :], RC[0:w, tile, :], QKH[0:w, tile, :].bitcast(F32),
                                                   ALU.subtract).then_inc(A["lo"], 1)
                        for kind, k in core:
                            if kind == "LN_STATS":
                                ln_rstd_pool(pool, g + 1)
                            if kind == "HI":
                                pool.wait_ge(A["ctx_hi"], 4 * a + k + 1)
                                pool.tensor_tensor(QKL[:, k, :], YS[:, k % 2, :], QKH[:, k, :].bitcast(F32),
                                                   ALU.subtract).then_inc(A["ctx_lo"], 1)

                @block.scalar
                def _(act):
                    act.wait_ge(A["load"], 16)
                    act.activation(W[:, 0, :], WR, ACT.Copy).then_inc(A["w_hi"], 1)
                    act.wait_ge(A["const"], N_CONST)
                    for i, u, b, a, g in steps(act):
                        for n, tile in enumerate(TILE_ORDER):
                            if first_layer:
                                act.wait_ge(A["proj"], NI * a + n + 1)
                                act.activation(QKH[:, tile, :], PS[:, n, :], ACT.Identity,
                                               bias=BQK[:, tile:tile + 1]).then_inc(A["hi"], 1)
                            else:
                                w = P if tile < 2 else KV * HD
                                act.wait_ge(A["sum"], NI * a + n + 1)
                                act.activation(QKH[0:w, tile, :], RC[0:w, tile, :], ACT.Copy).then_inc(A["hi"], 1)
                        for kind, k in core:
                            if kind == "PLACE":
                                act.wait_ge(A["place_q"], 8 * a + k + 1)
                                for half in range(2):
                                    rows = slice(64 * half, 64 * half + 64)
                                    z = 2 * k + half
                                    if first_layer:
                                        act.activation(QZ[rows, z, :], PS[rows, 6 + k % 2, :], ACT.Identity,
                                                       bias=QX[rows, z:z + 1]).then_inc(A["qz"], 1)
                                    else:
                                        act.activation(QZ[rows, z, :], PS[rows, 6 + k % 2, :],
                                                       ACT.Copy).then_inc(A["qz"], 1)
                            if kind == "NMT":
                                act.wait_ge(A["mt"], 4 * a + k + 1)
                                act.wait_ge(A["row"], ONE + 256 * a + 64 * max(k - 1, 0))
                                act.activation(MROW[:, k % 2, :], PS[0:4, 7, :], ACT.Copy).then_inc(A["mrow"], 1)
                            if kind == "ST":
                                p, kt = divmod(k, TT)
                                n = SEQ - P * kt
                                act.wait_ge(A["st"], 32 * a + k + 1)
                                if kt == 0:
                                    act.wait_ge(A["pv"], ring(a, 8, p, 2))
                                act.activation(PT[:, p % 2, :, TRI[kt]:TRI[kt] + n],
                                               PS[:, 2 + 2 * (k % 2):4 + 2 * (k % 2), 0:n], ACT.Exp,
                                               scale=0.25).then_inc(A["exp"], 1)
                            if kind == "COPY":
                                act.wait_ge(A["pv"], ONE + 8 * a + 2 * k + 2)
                                act.wait_ge(A["ctx_lo"], ring(a, 4, k, 2))
                                act.activation(YS[:, k % 2, :], PS[:, 6, :], ACT.Copy).then_inc(A["pv_copied"], 1)
                            if kind == "HI":
                                act.wait_ge(A["ctx"], 4 * a + k + 1)
                                act.activation(QKH[:, k, :], YS[:, k % 2, :], ACT.Copy).then_inc(A["ctx_hi"], 1)
                            if kind == "LN_T":
                                ln_hi_act(act, g + 1, 1 - u, (0, 1))

                @block.vector
                def _(dve):
                    dve.memset(QZ[:].bitcast(F32), 0.0).then_inc(A["zero"], 1)
                    dve.memset(V[:, :, :, HD:], 1.0).then_inc(A["zero"], 1)
                    dve.wait_ge(A["w_hi"], 1)
                    dve.tensor_tensor(W[:, 1, :], WR, W[:, 0, :].bitcast(F32), ALU.subtract).then_inc(A["w_lo"], 1)
                    dve.wait_ge(A["const"], N_CONST)
                    for i, u, b, a, g in steps(dve):
                        nb = next_batch(i, u)
                        for n, tile in enumerate(TILE_ORDER):
                            if first_layer:
                                dve.wait_ge(A["hi"], NI * a + n + 1)
                                dve.scalar_tensor_tensor(out=QKL[:, tile, :], in0=PS[:, n, :],
                                                         scalar=BQK[:, tile:tile + 1],
                                                         in1=QKH[:, tile, :].bitcast(F32), op0=ALU.add,
                                                         op1=ALU.subtract).then_inc(A["lo"], 1)
                            else:
                                w = P if tile < 2 else KV * HD
                                dve.wait_ge(A["proj"], NI * a + n + 1)
                                if n == 2:
                                    dve.wait_ge(A["sum"], NI * a + 1)
                                dve.tensor_tensor(RA[0:w, n % 2, :], PS[0:w, 2 * n, :], COS[0:w, :],
                                                  ALU.mult).then_inc(A["rope"], 1)
                                dve.tensor_tensor(RB_[0:w, n % 2, :], PS[0:w, 2 * n + 1, :], SIN[0:w, :],
                                                  ALU.mult).then_inc(A["rope"], 1)
                        for jj in range(NV):
                            dve.wait_ge(A["v"], NV * a + jj + 1)
                            if first_layer:
                                dve.tensor_tensor(V[:, 2 * jj:2 * jj + 2, :, 0:HD],
                                                  PS[:, 4 + jj, :].rearrange("p (j h d) -> p j h d", j=2, h=HEADS),
                                                  BVB[:].rearrange("p (h d) -> p h d", d=HD).unsqueeze(1).broadcast_to([P, 2, HEADS, HD]),
                                                  ALU.add).then_inc(A["v_ready"], 1)
                            else:
                                dve.tensor_copy(V[:, :, :, 0:HD],
                                                PS[:, 6, 0:TT * KV * HD].rearrange("p (j h d) -> p j h d", j=TT, h=KV)).then_inc(A["v_ready"], 1)
                        for kind, k in core:
                            if kind == "PLACE" and k < NK:
                                dve.wait_ge(A["place_k"], NK * a + k + 1)
                                dve.tensor_tensor(KS[:, k, :], PS[:, 4 + k % 2, :], KX[:], ALU.add).then_inc(A["kz"], 1)
                            if kind == "S":
                                z, qt = divmod(k, TT)
                                dve.wait_ge(A["s"], 64 * a + k + 1)
                                dve.tensor_reduce(NM[:, qt, z:z + 1], PS[:, k % 2, 0:P * (qt + 1)], AX.X, ALU.max,
                                                  negate=True).then_inc(A["smax"], 1)
                            if kind == "LN_STATS":
                                ln_stats_dve(dve, nb, g + 1)
                            if kind == "LN_NORM":
                                ln_norm_dve(dve, nb, g + 1, 1 - u)
                            if kind == "LN_T":
                                ln_lo_dve(dve, g + 1, 1 - u, (0, 1))
                            if kind == "SUMS":
                                dve.wait_ge(A["sums"], 4 * a + k + 1)
                                if k:
                                    dve.wait_ge(A["spread"], 4 * a + k)
                                dve.reciprocal(RECIP[:], PS[:, 7, 0:16]).then_inc(A["recip"], 1)
                                dve.wait_ge(A["recip"], 4 * a + k + 1)
                                dve.tensor_copy(r_wide(u), RECIP[:].unsqueeze(2).broadcast_to([P, TT * 4, 2 * HD])).then_inc(A["recip_wide"], 1)
                            if kind == "SPREAD":
                                dve.wait_ge(A["spread"], 4 * a + k + 1)
                                dve.tensor_tensor(YS[:, k % 2, :], YS[:, k % 2, :], PS[:, 7, :],
                                                  ALU.mult).then_inc(A["ctx"], 1)
                        if first_layer:
                            dve.wait_ge(A["bias"], a + 1)
                        for jj in range(2):
                            dve.wait_ge(A["o"], 2 * a + jj + 1)
                            xs = X[:, bass.ds(b * TT + 2 * jj, 2), :]
                            dve.tensor_tensor(xs, PS[:, 2 + 2 * jj:4 + 2 * jj, 0:D], xs, ALU.add).then_inc(A["x"], 1)

                @block.tensor
                def _(pe):
                    pe.wait_ge(A["w_lo"], 1)
                    pe.wait_ge(A["cast"], 64)
                    pe.wait_ge(A["zero"], 2)
                    pe.wait_ge(A["const"], N_CONST)
                    for i, u, b, a, g in steps(pe):
                        xh, xl = XH[:, u, :, :], XL[:, u, :, :]

                        def w_cols(part, f, c0, n):
                            return W[:, part, f * COLS + c0:f * COLS + c0 + n]

                        def project(dst, c0, n):
                            for f in range(DH):
                                mm = three_passes(pe, dst, w_cols(0, f, c0, n), w_cols(1, f, c0, n), xh[:, f, :],
                                                  xl[:, f, :], f == 0, f == DH - 1)
                            return mm

                        pe.wait_ge(xl_ready, g * DH + DH)
                        pe.wait_ge(A["x"], ONE + 2 * a)
                        for n, tile in enumerate(TILE_ORDER):
                            if first_layer:
                                project(PS[:, n, :], tile * P, P).then_inc(A["proj"], 1)
                            else:
                                for sw in range(2):
                                    c0, w = (sw * D + tile * P, P) if tile < 2 else (K0 + sw * KV * HD, KV * HD)
                                    mm = project(PS[0:w, 2 * n + sw, :], c0, w)
                                mm.then_inc(A["proj"], 1)
                        pe.wait_ge(A["pv_copied"], ONE + 4 * a)
                        w = VH * HD
                        for j in range(TT):
                            tok = slice(j * P, (j + 1) * P)
                            dst = PS[:, 4 + j // 2, (j % 2) * w:(j % 2 + 1) * w] if first_layer else PS[:, 6, j * w:(j + 1) * w]
                            for f in range(DH):
                                mm = three_passes(pe, dst, xh[:, f, tok], xl[:, f, tok], w_cols(0, f, V0, w),
                                                  w_cols(1, f, V0, w), f == 0, f == DH - 1)
                            if not first_layer and j == TT - 1 or first_layer and j % 2:
                                mm.then_inc(A["v"], 1)
                        for kind, k in core:
                            if kind == "PLACE":
                                tl, cc = divmod(k, 4)
                                if cc == 0:
                                    pe.wait_ge(A["lo"], NI * a + (2 if tl == 0 else NI))
                                if k == 0:
                                    pe.wait_ge(A["v_ready"], NV * a + NV)
                                if k >= 2:
                                    pe.wait_ge(A["qz"], 16 * a + 2 * (k - 1))
                                pe.matmul(PS[:, 6 + k % 2, :], PLACE[:, 0, cc, :], QKH[:, tl, :], start=True, stop=False)
                                pe.matmul(PS[:, 6 + k % 2, :], PLACE[:, 1, cc, :], QKL[:, tl, :], start=False,
                                          stop=True).then_inc(A["place_q"], 1)
                                if k < NK:
                                    if k >= 2:
                                        pe.wait_ge(A["kz"], NK * a + k - 1)
                                    r, src = (P, 2 + tl) if first_layer else (KV * HD, 2)
                                    pe.matmul(PS[:, 4 + k % 2, :], PLACE[0:r, 2, cc, :], QKH[0:r, src, :], start=True, stop=False)
                                    pe.matmul(PS[:, 4 + k % 2, :], PLACE[0:r, 3, cc, :], QKL[0:r, src, :], start=False,
                                              stop=True).then_inc(A["place_k"], 1)
                            if kind == "S":
                                z, qt = divmod(k, TT)
                                if qt == 0:
                                    pe.wait_ge(A["qz"], 16 * a + z + 1)
                                    pe.wait_ge(A["kz"], NK * a + kidx(z) + 1)
                                if k >= 2:
                                    pe.wait_ge(A["smax"], ring(a, 64, k, 2))
                                tok = slice(qt * P, (qt + 1) * P)
                                pe.matmul(PS[:, k % 2, 0:P * (qt + 1)], QZ[:, z, tok], KS[:, kidx(z), 0:P * (qt + 1)],
                                          start=True, stop=False)
                                pe.matmul(PS[:, k % 2, tok], IDB[:], MKB[:], start=False, stop=True).then_inc(A["s"], 1)
                            if kind == "NMT":
                                pe.wait_ge(A["smax"], ONE + 64 * a + 16 * (k + 1))
                                pe.wait_ge(*bank7_read(a, (kind, k)))
                                for qt in range(TT):
                                    mm = pe.transpose(PS[0:4, 7, qt * P:(qt + 1) * P], NM[:, qt, 4 * k:4 * k + 4], IDENT[:])
                                mm.then_inc(A["mt"], 1)
                            if kind == "ST":
                                n, kt = divmod(k, TT)
                                if k == 0:
                                    pe.wait_ge(A["kz"], NK * a + NK)
                                if k % 8 == 0:
                                    pe.wait_ge(A["row"], ONE + 256 * a + 64 * (k // 8 + 1))
                                if k >= 2:
                                    pe.wait_ge(A["exp"], ring(a, 32, k, 2))
                                for zi in range(2):
                                    z, bank = 2 * n + zi, 2 + 2 * (k % 2) + zi
                                    pe.matmul(PS[:, bank, 0:SEQ - P * kt], KS[:, kidx(z), kt * P:(kt + 1) * P],
                                              QZ[:, z, kt * P:SEQ], start=True, stop=False)
                                    mm = pe.matmul(PS[:, bank, 0:P], IDB[:], MTB[:], start=False, stop=True)
                                mm.then_inc(A["st"], 1)
                            if kind == "PV":
                                n, kt = divmod(k, TT)
                                pe.wait_ge(A["exp"], ONE + 32 * a + k + 1)
                                if k % 8 == 0:
                                    pe.wait_ge(A["pv_copied"], ONE + 4 * a + k // 8)
                                for zi in range(2):
                                    z = 2 * n + zi
                                    vh = z if first_layer else (z // 8) * 2 + z % 2
                                    rows = slice(32 * (z % 4), 32 * (z % 4) + 32)
                                    mm = pe.matmul(PS[rows, 6, kt * P:SEQ], V[:, kt, vh, :],
                                                   PT[:, n % 2, zi, TRI[kt]:TRI[kt + 1]], start=kt == 0,
                                                   stop=kt == TT - 1, tile_position=(0, rows.start))
                                if kt == TT - 1:
                                    mm.then_inc(A["pv"], 1)
                            if kind == "SUMS":
                                pe.wait_ge(A["pv_copied"], ONE + 4 * a + k + 1)
                                pe.wait_ge(*bank7_read(a, (kind, k)))
                                for j in range(TT):
                                    mm = pe.matmul(PS[:, 7, 4 * j:4 * j + 4], YS[:, k % 2, j * P:(j + 1) * P], PICK[:],
                                                   start=True, stop=True)
                                mm.then_inc(A["sums"], 1)
                            if kind == "SPREAD":
                                pe.wait_ge(*bank7_read(a, (kind, k)))
                                pe.wait_ge(A["recip_wide"], 4 * a + k + 1)
                                for j in range(TT):
                                    mm = pe.matmul(PS[:, 7, j * P:(j + 1) * P],
                                                   r_wide(u)[:, 4 * j:4 * j + 4, :].rearrange("p z r -> p (z r)"), IDENT[:],
                                                   start=True, stop=True)
                                mm.then_inc(A["spread"], 1)
                            if kind == "LN_T":
                                pe.wait_ge(A["smax"], ONE + 64 * a + 64)
                                ln_transpose_pe(pe, g + 1, 1 - u, (0, 1))
                            if kind == "OUT":
                                if k == 0:
                                    pe.wait_ge(A["exp"], ONE + 32 * a + 32)
                                pe.wait_ge(A["ctx_lo"], ONE + 4 * a + k + 1)
                                cols = slice(O0 + k * D, O0 + (k + 1) * D)
                                for j in range(TT):
                                    tok = slice(j * P, (j + 1) * P)
                                    mm = three_passes(pe, PS[:, 2 + j, 0:D], QKH[:, k, tok], QKL[:, k, tok],
                                                      W[:, 0, cols], W[:, 1, cols], k == 0, k == QUADS - 1)
                                    if k == QUADS - 1 and j % 2:
                                        mm.then_inc(A["o"], 1)

        def run(kinds, first_phase, WG=None, WD=None):
            for phase, kind in enumerate(kinds, first_phase):
                seen = PHASES[:phase].count(kind)
                e0 = BATCHES * sum(x in ("ffn", "moe") for x in PHASES[:phase])
                if kind == "ffn":
                    ffn_phase(phase, seen, WG, WD, e0)
                elif kind == "moe":
                    moe_phase(phase, seen, e0)
                else:
                    attn_phase(phase, kind == "attn0")

        lut_phases = max([n + 1 for n, x in enumerate(PHASES) if x == "ffn"], default=0)
        with ExitStack() as keep:
            if lut_phases:
                WG, WD = ffn_weights(keep)
                run(PHASES[:lut_phases], 0, WG, WD)
        run(PHASES[lut_phases:], lut_phases)

        with nc.Block() as block:
            @block.sync
            def _(sp):
                for b in range(BATCHES):
                    sp.dma_start(out[b].rearrange("(j p) d -> p j d", p=P),
                                 X[:, b * TT:(b + 1) * TT, :]).then_inc(stored, 16)
                sp.wait_ge(stored, 16 * BATCHES)


_INS = ["L0_attn_x", "L0_attn_Wqkv", "L0_attn_b_qkv", "L0_attn_Wout", "L0_attn_b_out", "L0_ffn_lut",
        "L0_ffn_gate_idx", "L0_ffn_up_idx", "L0_ffn_down_idx", "L1_attn_Wq", "L1_attn_Wk", "L1_attn_Wv",
        "L1_attn_Wproj", "L1_ffn_shared_w1", "L1_ffn_shared_b1", "L1_ffn_shared_w2", "L1_ffn_shared_b2",
        "L1_ffn_routed_w1", "L1_ffn_routed_b1", "L1_ffn_routed_w2", "L1_ffn_routed_b2", "L1_ffn_centroids",
        "L1_ffn_bias"]


def layouts(x):
    a = {}
    w1 = np.zeros((D, MT * P), np.float32)
    w2 = np.zeros((MT * P, D), np.float32)
    b1 = np.zeros(MT * P, np.float32)
    n_routed, n_shared = NR * EF, NS * EF
    w1[:, :n_routed] = x["L1_ffn_routed_w1"].transpose(1, 0, 2).reshape(D, -1)
    w1[:, n_routed:n_routed + n_shared] = x["L1_ffn_shared_w1"].transpose(1, 0, 2).reshape(D, -1)
    w2[:n_routed] = x["L1_ffn_routed_w2"].reshape(-1, D)
    w2[n_routed:n_routed + n_shared] = x["L1_ffn_shared_w2"].reshape(-1, D)
    b1[:n_routed] = x["L1_ffn_routed_b1"].reshape(-1)
    b1[n_routed:n_routed + n_shared] = x["L1_ffn_shared_b1"].reshape(-1)
    up = w1.reshape(DH, P, MT, P).transpose(2, 1, 0, 3).reshape(MT, P, DH * P)
    down = w2.reshape(MT, P, D)
    a["m_w"] = np.concatenate([up, down], -1)[MORDER]
    a["m_b1"] = b1.reshape(MT, P).T
    a["m_centroids"] = x["L1_ffn_centroids"].T.reshape(DH, P, NR).transpose(1, 0, 2)
    b2 = np.zeros((P, D), np.float32)
    b2[:NR] = b2[NR:2 * NR] = x["L1_ffn_routed_b2"]
    a["m_b2"] = b2
    a["m_bs2"] = x["L1_ffn_shared_b2"].reshape(NS, DH, P).transpose(2, 0, 1)
    a["L1_ffn_bias"] = x["L1_ffn_bias"]
    def out_rows(w_out, head):
        rows = np.zeros((4, 4, 2 * HD, D), np.float32)
        for z in range(HEADS):
            rows[z // 4, z % 4, :HD] = w_out[HD * head(z):HD * (head(z) + 1)]
        return rows.reshape(4, P, D).transpose(1, 0, 2).reshape(P, 4 * D)

    def qkv_columns(w):
        return w.reshape(DH, P, -1).transpose(1, 0, 2).reshape(P, -1)

    a["a0_w"] = np.concatenate([qkv_columns(x["L0_attn_Wqkv"].T), out_rows(x["L0_attn_Wout"].T, lambda z: z)], 1)
    a["a0_bqk"] = x["L0_attn_b_qkv"][:2 * D].reshape(4, P).T
    a["a0_bv"], a["a0_bo"] = x["L0_attn_b_qkv"][2 * D:], x["L0_attn_b_out"]
    wq = x["L1_attn_Wq"].reshape(D, 2, 2, 4, 2, HD // 2).transpose(0, 1, 3, 2, 4, 5)
    wk = x["L1_attn_Wk"].reshape(D, KV, 2, HD // 2)
    w = np.concatenate([wq.reshape(D, D), wq[..., ::-1, :].reshape(D, D), wk.reshape(D, -1),
                        wk[..., ::-1, :].reshape(D, -1), x["L1_attn_Wv"]], 1)
    a["a1_w"] = np.concatenate([qkv_columns(w), out_rows(x["L1_attn_Wproj"],
                                                         lambda z: 8 * (z // 8) + 4 * (z % 2) + z % 8 // 2)], 1)
    for n in ("L0_attn_x", "L0_ffn_lut", "L0_ffn_gate_idx", "L0_ffn_up_idx", "L0_ffn_down_idx"):
        a[n] = x[n]
    return {n: np.ascontiguousarray(v) for n, v in a.items()}


def kernel(**inputs):
    import concourse.bacc as bacc
    from concourse.bass_utils import run_bass_kernel_spmd

    nc = bacc.Bacc("TRN2", target_bir_lowering=False, num_devices=1)
    arrays = layouts({n: np.asarray(inputs[n]) for n in _INS})
    arrays.update(constants())
    t = {n: nc.dram_tensor("in_" + n, a.shape, mybir.dt.from_np(a.dtype), kind="ExternalInput").ap()
         for n, a in arrays.items()}
    shape = (BATCHES, SEQ, D)
    out = nc.dram_tensor("out_x", shape, F32, kind="ExternalOutput").ap()
    kernel_program(nc, t, out)
    r = run_bass_kernel_spmd(nc, [{"in_" + n: a for n, a in arrays.items()}], core_ids=[0])
    return r.results[0]["out_x"]
```

```python
from contextlib import ExitStack

import numpy as np

import concourse.bass as bass
from concourse import mybir


F32 = mybir.dt.float32
F32R = mybir.dt.float32r
BF16 = mybir.dt.bfloat16
I32 = mybir.dt.int32
ACT = mybir.ActivationFunctionType
ALU = mybir.AluOpType
AX = mybir.AxisListType

P = 128
BATCHES = 4
SEQ = 512
D = 256
DH = D // P
TT = SEQ // P
TILES = BATCHES * TT
EPS = 1e-5
HEADS = 16
HD = D // HEADS
KV = 4

FF = 688
FT = -(-FF // P)
FW = [min(P, FF - P * m) for m in range(FT)]
LUT = 16

NS, NR, EF, TOPK = 2, 16, 176, 4
RT = NR * EF // P
ST = -(-NS * EF // P)
MT = RT + ST
MW = [P] * RT + [min(P, NS * EF - P * m) for m in range(ST)]
MORDER = list(range(RT, MT)) + list(range(RT))
PAD = -1.0e30

ONE = 1

PHASES = ["ffn", "attn0", "ffn", "moe", "attn1", "moe"]
ATT_SEMS = ("load", "load_out", "w_hi", "w_lo", "const", "cast", "zero", "proj", "rope", "sum", "hi", "lo", "v", "v_ready",
            "place_q", "qz", "place_k", "kz", "s", "smax", "mt", "mrow", "row", "st", "exp", "pv", "pv_copied",
            "sums", "recip", "recip_wide", "spread",
            "ctx", "ctx_hi", "ctx_lo", "o", "x", "bias")


def hi_lo(x):
    u = np.asarray(x, np.float32)
    m, e = np.frexp(u.astype(np.float64))
    hi = np.ldexp(np.round(m * 4096) / 4096, e).astype(np.float32)
    return hi, (u - hi).astype(np.float32)


def constants():
    c = {}
    c["c_ident"] = np.eye(P, dtype=np.float32)
    q = np.arange(P)
    c["c_mask"] = np.where(q[None, :] > q[:, None], np.float32(PAD), np.float32(0))
    c["c_maskT"] = c["c_mask"].T.copy()
    unit = np.arange(NR * EF) // EF
    sel = (unit[None, :] == np.arange(NR)[:, None]).astype(np.float32)
    sel = np.concatenate([sel, sel])
    c["c_sel"] = sel
    place = np.zeros((P, 4, HEADS // 4, P), np.float32)
    for cc in range(4):
        for half in range(2):
            for d in range(HD):
                src, dst = HD * (2 * cc + half) + d, 64 * half + d
                place[src, 0, cc, dst] = place[src, 0, cc, dst + 2 * HD] = 1
                place[src, 1, cc, dst + HD] = 1
                place[src, 2, cc, dst] = place[src, 2, cc, dst + HD] = 1
                place[src, 3, cc, dst + 2 * HD] = 1
    c["c_place"] = place.reshape(P, 16 * P)
    c["c_pick"] = np.kron(np.eye(4), np.eye(2 * HD)[:, HD:HD + 1]).astype(np.float32)
    m = np.arange(1, HEADS + 1, dtype=np.float32) * np.float32(8.0 / HEADS)
    slopes = (np.float32(1.0) / np.float32(2.0) ** m).astype(np.float32)
    s_hi, s_lo = hi_lo(slopes * np.float32(4.0))
    qx = np.zeros((P, HEADS), np.float32)
    kx = np.zeros((P, SEQ), np.float32)
    for half in range(2):
        qx[64 * half + 48], qx[64 * half + 49] = s_hi, s_lo
        kx[64 * half + 48] = kx[64 * half + 49] = np.arange(1 - SEQ, 1)
        kx[64 * half + 50] = 1
    c["c_qx"], c["c_kx"] = qx, kx
    inv = (1.0 / np.float32(10000.0) ** (np.arange(0, HD, 2, dtype=np.float32) / np.float32(HD))).astype(np.float32)
    ang = np.arange(SEQ, dtype=np.float32)[:, None] * inv[None, :]
    ang = np.concatenate([ang, ang], -1).T
    c["c_cos"] = np.tile(np.cos(ang), (P // HD, 1)).astype(np.float32)
    sign = np.where(np.arange(HD) < HD // 2, np.float32(-1), np.float32(1))[:, None]
    c["c_sin"] = np.tile(sign * np.sin(ang), (P // HD, 1)).astype(np.float32)
    return c


def kernel_program(nc, t, out):
    with ExitStack() as top:
        def sb(ctx, name, shape, dt=F32):
            return ctx.enter_context(nc.sbuf_tensor(name, shape, dt))

        def sem(name):
            return top.enter_context(nc.semaphore(name))

        PS = top.enter_context(nc.psum_tensor("PS", [P, 8, 512], F32))

        X = sb(top, "X", [P, TILES, D])
        XN = sb(top, "XN", [P, 2, TT, D])
        XH = sb(top, "XH", [P, 2, DH, SEQ], F32R)
        XL = sb(top, "XL", [P, 2, DH, SEQ], F32R)
        LST = sb(top, "LST", [P, TT, 6])
        LTMP = sb(top, "LTMP", [P, 5, TT])
        LMEAN = sb(top, "LMEAN", [P, TT])
        LVE = sb(top, "LVE", [P, TT])
        LRS = sb(top, "LRS", [P, TT])
        MHALF = sb(top, "MHALF", [P, TT])
        IDENT = sb(top, "IDENT", [P, P])
        YS = sb(top, "YS", [P, DH, SEQ])

        ln_stats = sem("ln_stats")
        ln_parts = sem("ln_parts")
        ln_var = sem("ln_var")
        ln_rstd = sem("ln_rstd")
        xn_ready = sem("xn_ready")
        xt_done = sem("xt_done")
        xh_ready = sem("xh_ready")
        xl_ready = sem("xl_ready")
        ins = sem("ins")
        ident_in = sem("ident_in")
        ready = sem("ready")
        stored = sem("stored")
        y_done = sem("y_done")
        y_copied = sem("y_copied")
        yt_done = sem("yt_done")
        x_updated = sem("x_updated")

        def ln_stats_dve(dve, b, g):
            for j in range(TT):
                dve.bn_stats(LST[:, j, :], X[:, bass.ds(b * TT + j, 1), :]).then_inc(ln_stats, 1)
            m_even, v_even, m_odd, v_odd = (LST[:, :, k] for k in (1, 2, 4, 5))
            dve.wait_ge(ln_stats, g * TT + TT)
            dve.tensor_tensor(LTMP[:, 0, :], m_even, m_odd, ALU.subtract).then_inc(ln_parts, 1)
            dve.tensor_tensor(LTMP[:, 1, :], v_even, v_odd, ALU.add).then_inc(ln_parts, 1)
            dve.tensor_tensor(LTMP[:, 2, :], m_even, m_odd, ALU.add).then_inc(ln_parts, 1)
            dve.wait_ge(ln_parts, g * 6 + 3)
            dve.tensor_tensor(LTMP[:, 3, :], LTMP[:, 0, :], LTMP[:, 0, :], ALU.mult).then_inc(ln_parts, 1)
            dve.tensor_scalar(LMEAN[:], LTMP[:, 2, :], 0.5, None, ALU.mult).then_inc(ln_parts, 1)
            dve.wait_ge(ln_parts, g * 6 + 5)
            dve.scalar_tensor_tensor(out=LTMP[:, 4, :], in0=LTMP[:, 3, :], scalar=float(D // 4), in1=LTMP[:, 1, :],
                                     op0=ALU.mult, op1=ALU.add).then_inc(ln_parts, 1)
            dve.wait_ge(ln_parts, g * 6 + 6)
            dve.tensor_scalar(LVE[:], LTMP[:, 4, :], 1.0 / D, EPS, ALU.mult, ALU.add).then_inc(ln_var, 1)

        def ln_rstd_pool(pool, g):
            pool.wait_ge(ln_var, g + 1)
            pool.tensor_tensor(LRS[:], LVE[:], MHALF[:], ALU.pow).then_inc(ln_rstd, 1)

        def ln_norm_dve(dve, b, g, par):
            dve.wait_ge(ln_rstd, g + 1)
            for j in range(TT):
                dve.tensor_scalar(XN[:, par, j, :], X[:, bass.ds(b * TT + j, 1), :], LMEAN[:, j:j + 1],
                                  LRS[:, j:j + 1], ALU.subtract, ALU.mult).then_inc(xn_ready, 1)

        def ln_transpose_pe(pe, g, par, banks):
            pe.wait_ge(xn_ready, g * TT + TT)
            for f in range(DH):
                for j in range(TT):
                    mm = pe.transpose(PS[:, banks[f], j * P:(j + 1) * P],
                                      XN[:, par, j, f * P:(f + 1) * P], IDENT[:])
                mm.then_inc(xt_done, 1)

        def ln_hi_act(act, g, par, banks):
            for f in range(DH):
                act.wait_ge(xt_done, g * DH + f + 1)
                act.activation(XH[:, par, f, :], PS[:, banks[f], :], ACT.Copy).then_inc(xh_ready, 1)

        def ln_lo_dve(dve, g, par, banks):
            for f in range(DH):
                dve.wait_ge(xh_ready, g * DH + f + 1)
                dve.tensor_tensor(XL[:, par, f, :], PS[:, banks[f], :], XH[:, par, f, :].bitcast(F32),
                                  ALU.subtract).then_inc(xl_ready, 1)

        def three_passes(pe, psum, w_hi, w_lo, x_hi, x_lo, start, stop):
            pe.matmul(psum, w_hi, x_hi, start=start, stop=False)
            pe.matmul(psum, w_lo, x_hi, start=False, stop=False)
            return pe.matmul(psum, w_hi, x_lo, start=False, stop=stop)

        fs = {n: sem("f_" + n) for n in (
            "lut", "idx_first", "idx_gate", "idx_up", "idx_down", "masks_dve", "masks_pool", "sums", "sums_used", "diag_hi", "diag_lo",
            "gate", "up", "silu", "h", "hh", "hl", "h_used")}
        ms = {n: sem("m_" + n) for n in (
            "raw0", "raw1", "raw2", "raw3", "w_hi", "w_lo", "const", "bs_sum", "sel", "zero", "ct_hi", "ct_lo",
            "b2_hi", "b2_lo", "logits", "scores", "gate_steps", "g2", "gt", "gt_ready",
            "hid", "gbc", "relu", "h", "hh", "hl", "h_used", "xn_added")}
        a0 = {n: sem("a0_" + n) for n in ATT_SEMS}
        a1 = {n: sem("a1_" + n) for n in ATT_SEMS}

        def start_sync(sp):
            for q in (a0["row"], a1["row"]):
                sp.sem_inc(q, ONE)
            sp.dma_start(IDENT[:], t["c_ident"]).then_inc(ident_in, 16)

        def start_pool(pool):
            for q in (fs["hl"], ms["hl"], a0["ctx_lo"], a1["ctx_lo"]):
                pool.sem_inc(q, ONE)
            pool.memset(MHALF[:], -0.5).then_inc(ready, 1)
            pool.wait_ge(ready, 1)

        def start_dve(dve):
            for q in (x_updated, fs["h"], ms["h"], a0["smax"], a0["x"], a1["smax"], a1["x"]):
                dve.sem_inc(q, ONE)

        def first_stats_dve(dve):
            dve.wait_ge(ins, 16 * BATCHES)
            ln_stats_dve(dve, 0, 0)

        def start_pe(pe):
            for q in (y_done, fs["h_used"], ms["h_used"], a0["pv"], a1["pv"]):
                pe.sem_inc(q, ONE)
            pe.wait_ge(ident_in, 16)

        def start_act(act):
            for q in (y_copied, fs["silu"], ms["relu"], a0["exp"], a1["exp"], a0["pv_copied"], a1["pv_copied"]):
                act.sem_inc(q, ONE)

        def load_x(act):
            for b in range(BATCHES):
                act.dma_start(X[:, b * TT:(b + 1) * TT, :],
                              t["L0_attn_x"][b].rearrange("(j p) d -> p j d", p=P)).then_inc(ins, 16)

        def ring(s, n, k, depth):
            return ONE + s * n + max(k - depth + 1, 0)

        def next_batch(i, u):
            return 2 * i + 1 if u == 0 else 2 - 2 * i

        def epilogue_copy_act(act, e, bias):
            act.wait_ge(y_done, ONE + e * DH + 1)
            if bias is None:
                act.activation(YS[:, 0, :], PS[:, 6, :], ACT.Copy).then_inc(y_copied, 1)
            else:
                act.activation(YS[:, 0, :], PS[:, 6, :], ACT.Identity, bias=bias[:, 0:1]).then_inc(y_copied, 1)

        def epilogue_copy_dve(dve, e, bias):
            dve.wait_ge(y_done, ONE + e * DH + 2)
            if bias is None:
                dve.tensor_copy(YS[:, 1, :], PS[:, 7, :]).then_inc(y_copied, 1)
            else:
                dve.tensor_scalar(YS[:, 1, :], PS[:, 7, :], bias[:, 1:2], None, ALU.add).then_inc(y_copied, 1)

        def epilogue_transpose_pe(pe, e, g, follows=True):
            pe.wait_ge(y_copied, ONE + e * DH + DH)
            if follows:
                pe.wait_ge(xl_ready, (g + 1) * DH + DH)
            for jj in range(2):
                for j in range(2):
                    for f in range(DH):
                        mm = pe.transpose(PS[:, jj, j * D + f * P:j * D + (f + 1) * P],
                                          YS[:, f, (2 * jj + j) * P:(2 * jj + j + 1) * P], IDENT[:])
                mm.then_inc(yt_done, 1)

        def epilogue_add_dve(dve, e, b):
            for jj in range(2):
                dve.wait_ge(yt_done, e * 2 + jj + 1)
                xs = X[:, bass.ds(b * TT + 2 * jj, 2), :]
                dve.scalar_tensor_tensor(out=xs, in0=PS[:, jj, :].rearrange("p (j d) -> p j d", j=2), scalar=0.5,
                                         in1=xs, op0=ALU.mult, op1=ALU.add).then_inc(x_updated, 1)

        def ffn_weights(keep):
            WG = sb(keep, "WGU", [P, 2, 2, DH, FF], F32R)
            WD = sb(keep, "WD", [P, 2, FT, D], F32R)
            with ExitStack() as ctx:
                LB = sb(ctx, "LUTB", [P, LUT])
                DHL = sb(ctx, "DIAGHL", [P, LUT, 2, P], F32R)
                IX = sb(ctx, "IDX", [P, 2, FT, D], I32)
                IXD = sb(ctx, "IDXD", [P, DH, FF], I32)
                MK = sb(ctx, "MASKS", [P, 2, LUT, D], F32R)
                POOL_FROM = 12
                units = [("gu", gu, o) for gu in range(2) for o in range(FT)]
                units += [("d", dh, m0) for dh in range(DH) for m0 in range(0, FT, 2)]

                def sums(n):
                    kind, a, c = units[n]
                    if kind == "gu":
                        return [(slice(f * P, (f + 1) * P), FW[c], P, WG[:, a, :, f, c * P:c * P + FW[c]])
                                for f in range(DH)]
                    return [(slice(i * P, i * P + FW[c + i]), P, FW[c + i],
                             WD[0:FW[c + i], :, c + i, a * P:(a + 1) * P]) for i in range(2)]

                with nc.Block() as block:
                    @block.sync
                    def _(sp):
                        sp.dma_start(LB[:], t["L0_ffn_lut"].partition_broadcast(P)).then_inc(fs["lut"], 16)
                        sp.dma_start(IX[:, 0, 0, :], t["L0_ffn_gate_idx"][0:P, :]).then_inc(fs["idx_first"], 16)
                        start_sync(sp)
                        full = (FT - 1) * P
                        for gu, (name, s_) in enumerate((("L0_ffn_gate_idx", "idx_gate"), ("L0_ffn_up_idx", "idx_up"))):
                            o = 1 - gu
                            sp.dma_start(IX[:, gu, o:FT - 1, :],
                                         t[name][o * P:full, :].rearrange("(o p) d -> p o d", p=P)).then_inc(fs[s_], 16)
                            sp.dma_start(IX[0:FF - full, gu, FT - 1, :], t[name][full:FF, :]).then_inc(fs[s_], 16)
                        sp.dma_start(IXD[:], t["L0_ffn_down_idx"].rearrange("(h p) f -> p h f", p=P)).then_inc(fs["idx_down"], 16)

                    def make_masks(eng, n, ks, done):
                        kind, a, c = units[n]
                        if n >= 2:
                            eng.wait_ge(fs["sums"], 2 * (n - 1))
                        if kind == "gu":
                            if n == 0:
                                eng.wait_ge(fs["idx_first"], 16)
                            else:
                                eng.wait_ge(fs["idx_up" if a else "idx_gate"], 32)
                            rows, w = FW[c], D
                            src = IX[0:rows, a, c, :]
                        else:
                            eng.wait_ge(fs["idx_down"], 16)
                            rows, w = P, min(2 * P, FF - c * P)
                            src = IXD[:, a, c * P:c * P + w]
                        for k in ks:
                            last = eng.tensor_scalar(MK[0:rows, n % 2, k, 0:w], src, float(k), None, ALU.is_equal)
                        last.then_inc(done, 1)

                    @block.gpsimd
                    def _(pool):
                        start_pool(pool)
                        for n in range(len(units)):
                            make_masks(pool, n, range(POOL_FROM, LUT), fs["masks_pool"])
                            if n == 4:
                                ln_rstd_pool(pool, 0)

                    @block.vector
                    def _(dve):
                        start_dve(dve)
                        for n in range(len(units)):
                            make_masks(dve, n, range(POOL_FROM), fs["masks_dve"])
                            if n == 0:
                                for k in range(LUT):
                                    dve.wait_ge(fs["diag_hi"], k + 1)
                                    dve.scalar_tensor_tensor(out=DHL[:, k, 1, :], in0=IDENT[:], scalar=LB[:, k:k + 1],
                                                             in1=DHL[:, k, 0, :].bitcast(F32), op0=ALU.mult,
                                                             op1=ALU.subtract).then_inc(fs["diag_lo"], 1)
                            if n == 4:
                                first_stats_dve(dve)
                            if n == 6:
                                ln_norm_dve(dve, 0, 0, 0)
                            if n == 10:
                                ln_lo_dve(dve, 0, 0, (0, 1))

                    @block.tensor
                    def _(pe):
                        start_pe(pe)
                        pe.wait_ge(fs["diag_lo"], LUT)
                        for n, (kind, a, c) in enumerate(units):
                            rows = FW[c] if kind == "gu" else P
                            pe.wait_ge(fs["masks_dve"], n + 1)
                            pe.wait_ge(fs["masks_pool"], n + 1)
                            for i, (cols, w, orows, _) in enumerate(sums(n)):
                                q = 2 * n + i
                                if q >= 4:
                                    pe.wait_ge(fs["sums_used"], q - 3)
                                dst = PS[0:orows, 2 + q % 4, 0:2 * w].rearrange("p (a n) -> p a n", a=2)
                                for k in range(LUT):
                                    mm = pe.matmul(dst, MK[0:rows, n % 2, k, cols], DHL[0:rows, k, :, 0:w],
                                                   start=k == 0, stop=k == LUT - 1)
                                mm.then_inc(fs["sums"], 1)
                            if n == 8:
                                ln_transpose_pe(pe, 0, 0, (0, 1))

                    @block.scalar
                    def _(act):
                        start_act(act)
                        load_x(act)
                        act.wait_ge(fs["lut"], 16)
                        act.wait_ge(ident_in, 16)
                        for k in range(LUT):
                            act.activation(DHL[:, k, 0, :], IDENT[:], ACT.Copy,
                                           scale=LB[:, k:k + 1]).then_inc(fs["diag_hi"], 1)
                        for n in range(len(units)):
                            for i, (cols, w, orows, dst) in enumerate(sums(n)):
                                q = 2 * n + i
                                act.wait_ge(fs["sums"], q + 1)
                                act.activation(dst, PS[0:orows, 2 + q % 4, 0:2 * w].rearrange("p (a n) -> p a n", a=2),
                                               ACT.Copy).then_inc(fs["sums_used"], 1)
                            if n == 9:
                                ln_hi_act(act, 0, 0, (0, 1))
            return WG, WD

        def ffn_phase(phase, occ, WG, WD, e0):
            with ExitStack() as ctx:
                SG = sb(ctx, f"SG{phase}", [P, 2, SEQ])
                HF = sb(ctx, f"HF{phase}", [P, 3, SEQ])
                HH = sb(ctx, f"HH{phase}", [P, 3, SEQ], F32R)
                HL = sb(ctx, f"HL{phase}", [P, 3, SEQ], F32R)
                LAG = 2
                block = ctx.enter_context(nc.Block())

                def steps(eng):
                    with eng.Fori(0, BATCHES // 2) as i:
                        for u in range(2):
                            b = 2 * i + u
                            yield i, u, b, 4 * occ + b, e0 + b, 4 * phase + b

                @block.tensor
                def _(pe):
                    for i, u, b, s, e, g in steps(pe):
                        def up(m):
                            w = FW[m]
                            for gu, (done, freed) in enumerate((("gate", "silu"), ("up", "h"))):
                                pe.wait_ge(fs[freed], ring(s, FT, m, 2))
                                dst = PS[0:w, 2 + 2 * gu + m % 2, :]
                                cols = slice(m * P, m * P + w)
                                for f in range(DH):
                                    mm = three_passes(pe, dst, WG[:, gu, 0, f, cols], WG[:, gu, 1, f, cols],
                                                      XH[:, u, f, :], XL[:, u, f, :], f == 0, f == DH - 1)
                                mm.then_inc(fs[done], 1)

                        def down(m):
                            w = FW[m]
                            pe.wait_ge(fs["hl"], ONE + s * FT + m + 1)
                            for f in range(DH):
                                cols = slice(f * P, (f + 1) * P)
                                mm = three_passes(pe, PS[:, 6 + f, :], WD[0:w, 0, m, cols], WD[0:w, 1, m, cols],
                                                  HH[0:w, m % 3, :], HL[0:w, m % 3, :], m == 0, m == FT - 1)
                                if m == FT - 1:
                                    mm.then_inc(y_done, 1)
                            mm.then_inc(fs["h_used"], 1) if m < FT - 1 else None

                        pe.wait_ge(xl_ready, g * DH + DH)
                        pe.wait_ge(y_copied, ONE + e * DH)
                        for m in range(FT):
                            up(m)
                            if m >= LAG:
                                down(m - LAG)
                        pe.wait_ge(x_updated, ONE + e * 2)
                        ln_transpose_pe(pe, g + 1, 1 - u, (0, 1))
                        for m in range(FT - LAG, FT):
                            down(m)
                        epilogue_transpose_pe(pe, e, g)

                @block.scalar
                def _(act):
                    for i, u, b, s, e, g in steps(act):
                        def silu(m):
                            act.wait_ge(fs["gate"], s * FT + m + 1)
                            act.wait_ge(fs["h"], ring(s, FT, m, 2))
                            act.activation(SG[0:FW[m], m % 2, :], PS[0:FW[m], 2 + m % 2, :],
                                           ACT.Silu).then_inc(fs["silu"], 1)

                        def hi(m):
                            act.wait_ge(fs["h"], ONE + s * FT + m + 1)
                            if m >= 3:
                                act.wait_ge(fs["h_used"], ring(s, FT - 1, m, 3))
                            else:
                                act.wait_ge(y_done, ONE + e * DH)
                            act.activation(HH[0:FW[m], m % 3, :], HF[0:FW[m], m % 3, :], ACT.Copy).then_inc(fs["hh"], 1)

                        for m in range(FT):
                            if m >= 1:
                                hi(m - 1)
                            silu(m)
                        hi(FT - 1)
                        ln_hi_act(act, g + 1, 1 - u, (0, 1))
                        epilogue_copy_act(act, e, None)

                @block.vector
                def _(dve):
                    for i, u, b, s, e, g in steps(dve):
                        nb = next_batch(i, u)
                        for m in range(FT):
                            w = FW[m]
                            dve.wait_ge(fs["silu"], ONE + s * FT + m + 1)
                            dve.wait_ge(fs["up"], s * FT + m + 1)
                            dve.wait_ge(fs["hl"], ring(s, FT, m, 3))
                            dve.tensor_tensor(HF[0:w, m % 3, :], SG[0:w, m % 2, :], PS[0:w, 4 + m % 2, :],
                                              ALU.mult).then_inc(fs["h"], 1)
                            if m == 0:
                                ln_stats_dve(dve, nb, g + 1)
                            if m == 1:
                                ln_norm_dve(dve, nb, g + 1, 1 - u)
                        ln_lo_dve(dve, g + 1, 1 - u, (0, 1))
                        epilogue_copy_dve(dve, e, None)
                        epilogue_add_dve(dve, e, b)

                @block.gpsimd
                def _(pool):
                    for i, u, b, s, e, g in steps(pool):
                        for m in range(FT):
                            w = FW[m]
                            pool.wait_ge(fs["hh"], s * FT + m + 1)
                            pool.tensor_tensor(HL[0:w, m % 3, :], HF[0:w, m % 3, :], HH[0:w, m % 3, :].bitcast(F32),
                                               ALU.subtract).then_inc(fs["hl"], 1)
                            if m == 0:
                                ln_rstd_pool(pool, g + 1)


        def moe_phase(phase, occ, e0):
            with ExitStack() as ctx:
                def mb(name, shape, dt=F32):
                    return sb(ctx, f"{name}_{phase}", shape, dt)

                RING = 4
                WRAW = mb("WRAW", [P, RING, DH * P + D])
                W = mb("W", [P, MT, 2, DH * P + D], F32R)
                B1 = mb("B1", [P, MT])
                SEL = mb("SEL", [P, RT, P], F32R)
                B2R = mb("B2R", [P, D])
                B2 = mb("B2", [P, 2, D], F32R)
                BS2 = mb("BS2", [P, NS, DH])
                BS = mb("BS", [P, DH])
                CR = mb("CR", [P, DH, NR])
                CT = mb("CT", [P, 2, DH, NR], F32R)
                RB = mb("RB", [P, NR])
                SC = mb("SC", [P, TT, NR + 8])
                V8 = mb("V8", [P, TT, 8])
                MR = mb("MR", [P, TT, NR + 8])
                GK = mb("GK", [P, TT, NR])
                GS = mb("GS", [P, 3, TT])
                G2 = mb("G2", [P, TT, P], F32R)
                GT = mb("GT", [P, 2, SEQ], F32R)
                HR = mb("HR", [P, 2, SEQ])
                HF = mb("HFM", [P, 2, SEQ])
                HH = mb("HHM", [P, 2, SEQ], F32R)
                HL = mb("HLM", [P, 2, SEQ], F32R)
                block = ctx.enter_context(nc.Block())
                LAG = 2

                STEPS = [(b, b % 2, 4 * occ + b, e0 + b, 4 * phase + b) for b in range(BATCHES)]
                LAST = 4 * len(PHASES) - 1
                CONST = 5 * 16

                @block.sync
                def _(sp):
                    for k in range(MT):
                        if k >= RING:
                            sp.wait_ge(ms["w_lo"], occ * MT + k - RING + 1)
                        sp.dma_start(WRAW[:, k % RING, :], t["m_w"][k]).then_inc(ms[f"raw{k % RING}"], 16)

                def raw_loads(k):
                    before = occ * len(range(k % RING, MT, RING))
                    return 16 * (before + k // RING + 1)

                @block.scalar
                def _(act):
                    for dst, name in ((CR, "m_centroids"), (B1, "m_b1"), (B2R, "m_b2"), (BS2, "m_bs2")):
                        act.dma_start(dst[:], t[name]).then_inc(ms["const"], 16)
                    act.dma_start(RB[:], t["L1_ffn_bias"].partition_broadcast(P)).then_inc(ms["const"], 16)

                    def router(r):
                        act.wait_ge(ms["logits"], r + 1)
                        act.activation(SC[:, :, 0:NR], PS[:, 0, 0:TT * NR].rearrange("p (j n) -> p j n", j=TT),
                                       ACT.Sigmoid).then_inc(ms["scores"], 1)

                    def gates_in(r):
                        act.wait_ge(ms["gt"], r + 1)
                        act.activation(GT[:, r % 2, :], PS[:, 1, :], ACT.Copy).then_inc(ms["gt_ready"], 1)

                    def split_hi(k):
                        m = MORDER[k]
                        act.wait_ge(ms[f"raw{k % RING}"], raw_loads(k))
                        act.activation(W[:, m, 0, :], WRAW[:, k % RING, :], ACT.Copy).then_inc(ms["w_hi"], 1)

                    for b, par, s, e, g in STEPS:
                        def relu(k):
                            m, w = MORDER[k], MW[MORDER[k]]
                            act.wait_ge(ms["hid"], s * MT + k + 1)
                            if m >= RT:
                                act.wait_ge(ms["hl"], ring(s, MT, k, 2))
                                dst = HF
                            else:
                                act.wait_ge(ms["h"], ring(s, RT, k - ST, 2))
                                dst = HR
                            act.activation(dst[0:w, k % 2, :], PS[0:w, 2 + k % 2, :], ACT.Relu,
                                           bias=B1[0:w, m:m + 1]).then_inc(ms["relu"], 1)

                        def hi(k):
                            m, w = MORDER[k], MW[MORDER[k]]
                            if m >= RT:
                                act.wait_ge(ms["relu"], ONE + s * MT + k + 1)
                            else:
                                act.wait_ge(ms["h"], ONE + s * RT + k - ST + 1)
                            if k >= 2:
                                act.wait_ge(ms["h_used"], ring(s, MT - 1, k, 2))
                            else:
                                act.wait_ge(y_done, ONE + e * DH)
                            act.activation(HH[0:w, k % 2, :], HF[0:w, k % 2, :], ACT.Copy).then_inc(ms["hh"], 1)

                        if b == 0:
                            split_hi(0)
                            act.wait_ge(ms["const"], occ * CONST + CONST)
                            act.activation(CT[:, 0, :, :], CR[:], ACT.Copy).then_inc(ms["ct_hi"], 1)
                            split_hi(1)
                            act.activation(B2[:, 0, :], B2R[:], ACT.Copy).then_inc(ms["b2_hi"], 1)
                        for k in range(MT):
                            if b == 0 and k + 2 < MT:
                                split_hi(k + 2)
                            if k == 1 and b == 0:
                                router(s)
                            if k >= 1:
                                hi(k - 1)
                            relu(k)
                            if k == ST and b == 0:
                                gates_in(s)
                            if k == 13 and g < LAST:
                                ln_hi_act(act, g + 1, 1 - par, (0, 1))
                            if k == 16 and b < BATCHES - 1:
                                router(s + 1)
                            if k == 21 and b < BATCHES - 1:
                                gates_in(s + 1)
                        hi(MT - 1)
                        epilogue_copy_act(act, e, BS)

                @block.gpsimd
                def _(pool):
                    pool.wait_ge(ms["zero"], 3 * occ + 3)
                    pool.dma_start(SEL[0:2 * NR, :, :].rearrange("p m c -> p (m c)"), t["c_sel"]).then_inc(ms["sel"], 16)
                    for b, par, s, e, g in STEPS:
                        def split_lo(k):
                            m = MORDER[k]
                            pool.wait_ge(ms["w_hi"], occ * MT + k + 1)
                            pool.tensor_tensor(W[:, m, 1, :], WRAW[:, k % RING, :], W[:, m, 0, :].bitcast(F32),
                                               ALU.subtract).then_inc(ms["w_lo"], 1)

                        if b == 0:
                            split_lo(0)
                            split_lo(1)
                        for k in range(MT):
                            w = MW[MORDER[k]]
                            if b == 0 and k + 2 < MT:
                                split_lo(k + 2)
                            pool.wait_ge(ms["hh"], s * MT + k + 1)
                            pool.tensor_tensor(HL[0:w, k % 2, :], HF[0:w, k % 2, :], HH[0:w, k % 2, :].bitcast(F32),
                                               ALU.subtract).then_inc(ms["hl"], 1)
                            if k == 5 and g < LAST:
                                ln_rstd_pool(pool, g + 1)

                @block.vector
                def _(dve):
                    for dst, v in ((SEL[:].bitcast(F32), 0.0), (SC[:, :, NR:], PAD), (G2[:].bitcast(F32), 0.0)):
                        dve.memset(dst, v).then_inc(ms["zero"], 1)
                    dve.wait_ge(ms["ct_hi"], occ + 1)
                    dve.tensor_tensor(CT[:, 1, :, :], CR[:], CT[:, 0, :, :].bitcast(F32), ALU.subtract).then_inc(ms["ct_lo"], 1)
                    dve.wait_ge(ms["const"], CONST * (occ + 1))
                    dve.tensor_tensor(BS[:], BS2[:, 0, :], BS2[:, 1, :], ALU.add).then_inc(ms["bs_sum"], 1)
                    dve.wait_ge(ms["b2_hi"], occ + 1)
                    dve.tensor_tensor(B2[:, 1, :], B2R[:], B2[:, 0, :].bitcast(F32), ALU.subtract).then_inc(ms["b2_lo"], 1)
                    dve.wait_ge(ms["zero"], 3 * occ + 3)

                    def best_scores(r):
                        n = [11 * r]

                        def link(ins_):
                            n[0] += 1
                            ins_.then_inc(ms["gate_steps"], 1)
                            dve.wait_ge(ms["gate_steps"], n[0])

                        dve.wait_ge(ms["scores"], r + 1)
                        best = SC[:, :, 0:NR]
                        link(dve.tensor_tensor(best, best, RB[:].unsqueeze(1).broadcast_to([P, TT, NR]), ALU.add))
                        for j in range(TT):
                            last = dve.max(V8[:, j, :], SC[:, j, :])
                        link(last)
                        link(dve.memset(V8[:, :, TOPK:], PAD))
                        for j in range(TT):
                            last = dve.match_replace(MR[:, j, :], V8[:, j, :], SC[:, j, :], 2 * PAD)
                        link(last)

                    def gate_values(r):
                        n = [11 * r + 4]

                        def link(ins_):
                            n[0] += 1
                            ins_.then_inc(ms["gate_steps"], 1)
                            dve.wait_ge(ms["gate_steps"], n[0])

                        best = SC[:, :, 0:NR]
                        link(dve.tensor_tensor(GK[:], best, MR[:, :, 0:NR], ALU.not_equal))
                        link(dve.tensor_tensor(GK[:], GK[:], best, ALU.mult))
                        link(dve.tensor_reduce(GS[:, 0, :], GK[:], AX.X, ALU.add))
                        link(dve.tensor_scalar(GS[:, 1, :], GS[:, 0, :], 1e-8, None, ALU.max))
                        link(dve.reciprocal(GS[:, 2, :], GS[:, 1, :]))
                        link(dve.tensor_tensor(GK[:], GK[:], GS[:, 2, :].unsqueeze(2).broadcast_to([P, TT, NR]), ALU.mult))
                        if r > 0:
                            dve.wait_ge(ms["gt"], r)
                        link(dve.tensor_copy(G2[:, :, 0:NR], GK[:]))
                        dve.tensor_tensor(G2[:, :, NR:2 * NR], GK[:], G2[:, :, 0:NR].bitcast(F32),
                                          ALU.subtract).then_inc(ms["g2"], 1)

                    for b, par, s, e, g in STEPS:
                        if b == 0:
                            best_scores(s)
                            gate_values(s)
                        else:
                            epilogue_copy_dve(dve, e - 1, BS)
                            epilogue_add_dve(dve, e - 1, b - 1)
                        for r in range(RT):
                            k = ST + r
                            dve.wait_ge(ms["relu"], ONE + s * MT + k + 1)
                            dve.wait_ge(ms["gbc"], s * RT + r + 1)
                            dve.wait_ge(ms["hl"], ring(s, MT, k, 2))
                            dve.tensor_tensor(HF[:, k % 2, :], HR[:, k % 2, :], PS[:, 4 + r % 2, :],
                                              ALU.mult).then_inc(ms["h"], 1)
                            if g < LAST:
                                if r == 2:
                                    ln_stats_dve(dve, (b + 1) % BATCHES, g + 1)
                                if r == 4:
                                    ln_norm_dve(dve, (b + 1) % BATCHES, g + 1, 1 - par)
                                if r == 11:
                                    ln_lo_dve(dve, g + 1, 1 - par, (0, 1))
                            if r == 7:
                                xs = X[:, b * TT:(b + 1) * TT, :]
                                dve.scalar_tensor_tensor(out=xs, in0=XN[:, par, :, :], scalar=0.5, in1=xs,
                                                         op0=ALU.mult, op1=ALU.add).then_inc(ms["xn_added"], 1)
                            if b < BATCHES - 1:
                                if r == 14:
                                    best_scores(s + 1)
                                if r == 15:
                                    gate_values(s + 1)
                        dve.wait_ge(ms["xn_added"], s + 1)
                    epilogue_copy_dve(dve, e, BS)
                    epilogue_add_dve(dve, e, b)

                @block.tensor
                def _(pe):
                    for b, par, s, e, g in STEPS:
                        def gates(k):
                            r = k - ST
                            pe.wait_ge(ms["h"], ring(s, RT, r, 2))
                            pe.matmul(PS[:, 4 + r % 2, :], SEL[:, r, :], GT[:, s % 2, :], start=True,
                                      stop=True).then_inc(ms["gbc"], 1)

                        def router(r, par):
                            for j in range(TT):
                                tok = slice(j * P, (j + 1) * P)
                                for f in range(DH):
                                    dst = PS[:, 0, j * NR:(j + 1) * NR]
                                    for n, (x_, c_) in enumerate(((XH, 0), (XL, 0), (XH, 1))):
                                        mm = pe.matmul(dst, x_[:, par, f, tok], CT[:, c_, f, :],
                                                       start=f == 0 and n == 0, stop=f == DH - 1 and n == 2)
                            mm.then_inc(ms["logits"], 1)

                        def gates_transposed(r):
                            pe.wait_ge(ms["g2"], r + 1)
                            for j in range(TT):
                                mm = pe.transpose(PS[:, 1, j * P:(j + 1) * P], G2[:, j, :].bitcast(F32), IDENT[:])
                            mm.then_inc(ms["gt"], 1)

                        def up(k):
                            m, w = MORDER[k], MW[MORDER[k]]
                            if b == 0:
                                pe.wait_ge(ms["w_lo"], occ * MT + k + 1)
                            pe.wait_ge(ms["relu"], ring(s, MT, k, 2))
                            for f in range(DH):
                                cols = slice(f * P, f * P + w)
                                mm = three_passes(pe, PS[0:w, 2 + k % 2, :], W[:, m, 0, cols], W[:, m, 1, cols],
                                                  XH[:, par, f, :], XL[:, par, f, :], f == 0, f == DH - 1)
                            mm.then_inc(ms["hid"], 1)

                        def down(k):
                            m, w = MORDER[k], MW[MORDER[k]]
                            pe.wait_ge(ms["hl"], ONE + s * MT + k + 1)
                            for f in range(DH):
                                cols = slice(DH * P + f * P, DH * P + (f + 1) * P)
                                mm = three_passes(pe, PS[:, 6 + f, :], W[0:w, m, 0, cols], W[0:w, m, 1, cols],
                                                  HH[0:w, k % 2, :], HL[0:w, k % 2, :], k == 0, k == MT - 1)
                                if k == MT - 1:
                                    mm.then_inc(y_done, 1)
                            if k < MT - 1:
                                mm.then_inc(ms["h_used"], 1)

                        pe.wait_ge(xl_ready, g * DH + DH)
                        for k in range(MT):
                            up(k)
                            if k == 0 and b == 0:
                                pe.wait_ge(ms["ct_lo"], occ + 1)
                                pe.wait_ge(x_updated, ONE + e * 2)
                                router(s, par)
                            if k == 1 and b > 0:
                                pe.wait_ge(ms["gt_ready"], s + 1)
                                epilogue_transpose_pe(pe, e - 1, g - 1)
                            if k == ST and b == 0:
                                gates_transposed(s)
                                pe.wait_ge(ms["sel"], 16 * (occ + 1))
                                pe.wait_ge(ms["b2_lo"], occ + 1)
                            if k == ST:
                                pe.wait_ge(ms["gt_ready"], s + 1)
                            if k >= ST:
                                gates(k)
                            if k == 12 and g < LAST:
                                pe.wait_ge(x_updated, ONE + e * 2)
                                ln_transpose_pe(pe, g + 1, 1 - par, (0, 1))
                            if k == 15 and b < BATCHES - 1:
                                pe.wait_ge(xl_ready, (g + 1) * DH + DH)
                                router(s + 1, 1 - par)
                            if k == 20 and b < BATCHES - 1:
                                gates_transposed(s + 1)
                            if k == LAG:
                                pe.wait_ge(y_copied, ONE + e * DH)
                            if k >= LAG:
                                down(k - LAG)
                        for k in range(MT - LAG, MT - 1):
                            down(k)
                        for f in range(DH):
                            cols = slice(f * P, (f + 1) * P)
                            pe.matmul(PS[:, 6 + f, :], B2[:, 0, cols], GT[:, s % 2, :], start=False, stop=False)
                            pe.matmul(PS[:, 6 + f, :], B2[:, 1, cols], GT[:, s % 2, :], start=False, stop=False)
                        down(MT - 1)
                    epilogue_transpose_pe(pe, e, g, g < LAST)


        def attn_phase(phase, first_layer):
            A = a0 if first_layer else a1
            TILE_ORDER = (0, 2, 1, 3) if first_layer else (0, 2, 1)
            NI = len(TILE_ORDER)
            NK = 8 if first_layer else 2
            NV = 2 if first_layer else 1
            VH = HEADS if first_layer else KV
            COLS = 3 * D if first_layer else 2 * D + 3 * KV * HD
            QUADS = HEADS // 4
            O0 = DH * COLS
            K0 = 2 * D
            V0 = 2 * D if first_layer else K0 + 2 * KV * HD
            with ExitStack() as ctx:
                def ab(name, shape, dt=F32):
                    return sb(ctx, f"{name}_{phase}", shape, dt)

                W = ab("W", [P, 2, O0 + QUADS * D], F32R)
                PLACE = ab("PLACE", [P, 4, 4, P], F32R)
                PICK = ab("PICK", [P, 4])
                KX = ab("KX", [P, SEQ])
                IDB = ab("IDB", [P, P], BF16)
                MKB = ab("MKB", [P, P], BF16)
                MTB = ab("MTB", [P, P], BF16)
                QZ = ab("QZ", [P, HEADS, SEQ], F32R)
                KS = ab("KS", [P, NK, SEQ], F32R)
                QKH = ab("QKH", [P, QUADS, SEQ], F32R)
                QKL = ab("QKL", [P, QUADS, SEQ], F32R)
                V = ab("V", [P, TT, VH, 2 * HD])
                NM = ab("NM", [P, TT, HEADS])
                MROW = ab("MROW", [4, 2, SEQ], F32R)
                TRI = [sum(SEQ - P * x for x in range(kt)) for kt in range(TT + 1)]
                PT = ab("PT", [P, 2, 2, TRI[TT]])
                WR = PT[:].rearrange("p a b n -> p (a b n)")[:, 0:O0 + QUADS * D]
                RECIP = ab("RECIP", [P, TT * 4])

                def r_wide(u):
                    return XN[:, u, 0:2, :].rearrange("p j (z r) -> p (j z) r", r=2 * HD)

                if first_layer:
                    QX = ab("QX", [P, HEADS])
                    BQK = ab("BQK", [P, 4])
                    BVB = ab("BVB", [P, D])
                    BOB = ab("BOB", [P, D])
                else:
                    COS = ab("COS", [P, SEQ])
                    SIN = ab("SIN", [P, SEQ])
                    RA = ab("RA", [P, 2, SEQ])
                    RB_ = ab("RB", [P, 2, SEQ])
                    RC = ab("RC", [P, 3, SEQ])
                block = ctx.enter_context(nc.Block())

                def steps(eng):
                    with eng.Fori(0, BATCHES // 2) as i:
                        for u in range(2):
                            b = 2 * i + u
                            yield i, u, b, b, 4 * phase + b

                LEAD = 28
                core = [("PLACE", 0)]
                for k in range(0, 2 * (4 * QUADS * 2 + 8) + LEAD, 2):
                    x = (k - LEAD) // 2
                    if k // 2 + 1 < HEADS // 2:
                        core.append(("PLACE", k // 2 + 1))
                    for kk in (k, k + 1):
                        if kk < 4 * HEADS:
                            core.append(("S", kk))
                        if kk == k + 1 and 0 <= x < 2 * HEADS:
                            core.append(("ST", x))
                        if kk >= 17 and (kk - 17) % 16 == 0 and (kk - 17) // 16 < QUADS:
                            core.append(("NMT", (kk - 17) // 16))
                    if k in (64, 68, 78):
                        core.append(({64: "LN_STATS", 68: "LN_NORM", 78: "LN_T"}[k], 0))
                    if 0 <= x - 2 < 2 * HEADS:
                        core.append(("PV", x - 2))
                    for name, at in (("COPY", 9), ("SUMS", 10), ("SPREAD", 11), ("HI", 12)):
                        if x >= at and (x - at) % 8 == 0 and (x - at) // 8 < QUADS:
                            core.append((name, (x - at) // 8))
                    core += [("OUT", q) for q, at in enumerate((34, 36, 37, 38)) if x == at]
                for name, n in (("PLACE", 8), ("S", 64), ("NMT", 4), ("ST", 32), ("PV", 32), ("COPY", 4),
                                ("SUMS", 4), ("SPREAD", 4), ("HI", 4), ("OUT", 4), ("LN_T", 1)):
                    assert [x for x in core if x[0] == name] == [(name, y) for y in range(n)], name

                def bank7_read(a, event):
                    done = [x for x in core[:core.index(event)] if x[0] in ("NMT", "SUMS", "SPREAD")]
                    if not done:
                        return A["qz"], 16 * a + 16
                    kind, k = done[-1]
                    return A[{"NMT": "mrow", "SUMS": "recip", "SPREAD": "ctx"}[kind]], 4 * a + k + 1

                def nm_column(z):
                    return 4 * (z // 4) + 2 * (z % 2) + z % 4 // 2

                def kidx(z):
                    return z // 2 if first_layer else z // 8

                @block.sync
                def _(sp):
                    w_in = t["a0_w" if first_layer else "a1_w"]
                    sp.dma_start(WR[:, 0:O0], w_in[:, 0:O0]).then_inc(A["load"], 16)
                    consts = [(PICK[:], t["c_pick"]), (KX[:], t["c_kx"])]
                    if first_layer:
                        consts += [(BQK[:], t["a0_bqk"]), (BVB[:], t["a0_bv"].partition_broadcast(P)),
                                   (BOB[:], t["a0_bo"].partition_broadcast(P)), (QX[:], t["c_qx"])]
                    else:
                        consts += [(COS[:], t["c_cos"]), (SIN[:], t["c_sin"])]
                    for dst, src in consts:
                        sp.dma_start(dst, src).then_inc(A["const"], 16)
                    sp.dma_start(WR[:, O0:], w_in[:, O0:]).then_inc(A["load_out"], 16)
                    for i, u, b, a, g in steps(sp):
                        for y in range(QUADS):
                            sp.wait_ge(A["mrow"], 4 * a + y + 1)
                            for par in range(2):
                                row = 64 * par + 50
                                sp.dma_start(QZ[row:row + 1, 4 * y + par:4 * y + par + 3:2, :].bitcast(F32),
                                             MROW[2 * par:2 * par + 2, y % 2, :].bitcast(F32)).then_inc(A["row"], 16)

                N_CONST = 16 * (6 if first_layer else 4)

                @block.gpsimd
                def _(pool):
                    pool.dma_start(PLACE[:].rearrange("p a b c -> p (a b c)"), t["c_place"]).then_inc(A["cast"], 16)
                    pool.dma_start(IDB[:], t["c_ident"]).then_inc(A["cast"], 16)
                    pool.dma_start(MKB[:], t["c_mask"]).then_inc(A["cast"], 16)
                    pool.dma_start(MTB[:], t["c_maskT"]).then_inc(A["cast"], 16)
                    if first_layer:
                        pool.wait_ge(A["const"], N_CONST)
                    for i, u, b, a, g in steps(pool):
                        if first_layer:
                            pool.wait_ge(xn_ready, g * TT + TT)
                            xs = X[:, bass.ds(b * TT, TT), :]
                            pool.tensor_tensor(xs, xs, BOB[:].unsqueeze(1).broadcast_to([P, TT, D]),
                                               ALU.add).then_inc(A["bias"], 1)
                        else:
                            for n, tile in enumerate(TILE_ORDER):
                                w = P if tile < 2 else KV * HD
                                pool.wait_ge(A["rope"], 6 * a + 2 * n + 2)
                                pool.tensor_tensor(RC[0:w, tile, :], RA[0:w, n % 2, :], RB_[0:w, n % 2, :],
                                                   ALU.add).then_inc(A["sum"], 1)
                                pool.wait_ge(A["hi"], NI * a + n + 1)
                                pool.tensor_tensor(QKL[0:w, tile, :], RC[0:w, tile, :], QKH[0:w, tile, :].bitcast(F32),
                                                   ALU.subtract).then_inc(A["lo"], 1)
                        for kind, k in core:
                            if kind == "LN_STATS":
                                ln_rstd_pool(pool, g + 1)
                            if kind == "HI":
                                pool.wait_ge(A["ctx_hi"], 4 * a + k + 1)
                                pool.tensor_tensor(QKL[:, k, :], YS[:, k % 2, :], QKH[:, k, :].bitcast(F32),
                                                   ALU.subtract).then_inc(A["ctx_lo"], 1)

                @block.scalar
                def _(act):
                    act.wait_ge(A["load"], 16)
                    act.activation(W[:, 0, 0:O0], WR[:, 0:O0], ACT.Copy).then_inc(A["w_hi"], 1)
                    act.wait_ge(A["load_out"], 16)
                    act.activation(W[:, 0, O0:], WR[:, O0:], ACT.Copy).then_inc(A["w_hi"], 1)
                    act.wait_ge(A["const"], N_CONST)
                    act.wait_ge(A["zero"], 2)
                    for i, u, b, a, g in steps(act):
                        for n, tile in enumerate(TILE_ORDER):
                            if first_layer:
                                act.wait_ge(A["proj"], NI * a + n + 1)
                                act.activation(QKH[:, tile, :], PS[:, n, :], ACT.Identity,
                                               bias=BQK[:, tile:tile + 1]).then_inc(A["hi"], 1)
                            else:
                                w = P if tile < 2 else KV * HD
                                act.wait_ge(A["sum"], NI * a + n + 1)
                                act.activation(QKH[0:w, tile, :], RC[0:w, tile, :], ACT.Copy).then_inc(A["hi"], 1)
                        for kind, k in core:
                            if kind == "PLACE":
                                act.wait_ge(A["place_q"], 8 * a + k + 1)
                                for half in range(2):
                                    rows = slice(64 * half, 64 * half + 64)
                                    z = 2 * k + half
                                    if first_layer:
                                        act.activation(QZ[rows, z, :], PS[rows, 6 + k % 2, :], ACT.Identity,
                                                       bias=QX[rows, z:z + 1]).then_inc(A["qz"], 1)
                                    else:
                                        act.activation(QZ[rows, z, :], PS[rows, 6 + k % 2, :],
                                                       ACT.Copy).then_inc(A["qz"], 1)
                            if kind == "NMT":
                                act.wait_ge(A["mt"], 4 * a + k + 1)
                                act.wait_ge(A["row"], ONE + 128 * a + 32 * max(k - 1, 0))
                                act.activation(MROW[:, k % 2, :], PS[0:4, 7, :], ACT.Copy).then_inc(A["mrow"], 1)
                            if kind == "ST":
                                p, kt = divmod(k, TT)
                                n = SEQ - P * kt
                                if kt == 0:
                                    act.wait_ge(A["pv"], ring(a, 8, p, 2))
                                for zi in range(2):
                                    v = 2 * k + zi
                                    act.wait_ge(A["st"], 64 * a + v + 1)
                                    act.activation(PT[:, p % 2, zi, TRI[kt]:TRI[kt] + n], PS[:, 3 + v % 3, 0:n],
                                                   ACT.Exp, scale=0.25).then_inc(A["exp"], 1)
                            if kind == "COPY":
                                act.wait_ge(A["pv"], ONE + 8 * a + 2 * k + 2)
                                act.wait_ge(A["ctx_lo"], ring(a, 4, k, 2))
                                act.activation(YS[:, k % 2, :], PS[:, 6, :], ACT.Copy).then_inc(A["pv_copied"], 1)
                            if kind == "HI":
                                act.wait_ge(A["ctx"], 4 * a + k + 1)
                                act.activation(QKH[:, k, :], YS[:, k % 2, :], ACT.Copy).then_inc(A["ctx_hi"], 1)
                            if kind == "LN_T":
                                ln_hi_act(act, g + 1, 1 - u, (0, 1))

                @block.vector
                def _(dve):
                    dve.memset(QZ[:, 0:HEADS // 2, :].bitcast(F32), 0.0).then_inc(A["zero"], 1)
                    dve.wait_ge(A["w_hi"], 1)
                    dve.tensor_tensor(W[:, 1, 0:O0], WR[:, 0:O0], W[:, 0, 0:O0].bitcast(F32),
                                      ALU.subtract).then_inc(A["w_lo"], 1)
                    dve.memset(QZ[:, HEADS // 2:, :].bitcast(F32), 0.0).then_inc(A["zero"], 1)
                    dve.memset(V[:, :, :, HD:], 1.0).then_inc(A["zero"], 1)
                    dve.wait_ge(A["w_hi"], 2)
                    dve.tensor_tensor(W[:, 1, O0:], WR[:, O0:], W[:, 0, O0:].bitcast(F32),
                                      ALU.subtract).then_inc(A["w_lo"], 1)
                    dve.wait_ge(A["const"], N_CONST)
                    for i, u, b, a, g in steps(dve):
                        nb = next_batch(i, u)
                        for n, tile in enumerate(TILE_ORDER):
                            if first_layer:
                                dve.wait_ge(A["hi"], NI * a + n + 1)
                                dve.scalar_tensor_tensor(out=QKL[:, tile, :], in0=PS[:, n, :],
                                                         scalar=BQK[:, tile:tile + 1],
                                                         in1=QKH[:, tile, :].bitcast(F32), op0=ALU.add,
                                                         op1=ALU.subtract).then_inc(A["lo"], 1)
                            else:
                                w = P if tile < 2 else KV * HD
                                dve.wait_ge(A["proj"], NI * a + n + 1)
                                if n == 2:
                                    dve.wait_ge(A["sum"], NI * a + 1)
                                dve.tensor_tensor(RA[0:w, n % 2, :], PS[0:w, 2 * n, :], COS[0:w, :],
                                                  ALU.mult).then_inc(A["rope"], 1)
                                dve.tensor_tensor(RB_[0:w, n % 2, :], PS[0:w, 2 * n + 1, :], SIN[0:w, :],
                                                  ALU.mult).then_inc(A["rope"], 1)
                        for jj in range(NV):
                            dve.wait_ge(A["v"], NV * a + jj + 1)
                            if first_layer:
                                dve.tensor_tensor(V[:, 2 * jj:2 * jj + 2, :, 0:HD],
                                                  PS[:, 4 + jj, :].rearrange("p (j h d) -> p j h d", j=2, h=HEADS),
                                                  BVB[:].rearrange("p (h d) -> p h d", d=HD).unsqueeze(1).broadcast_to([P, 2, HEADS, HD]),
                                                  ALU.add).then_inc(A["v_ready"], 1)
                            else:
                                dve.tensor_copy(V[:, :, :, 0:HD],
                                                PS[:, 6, 0:TT * KV * HD].rearrange("p (j h d) -> p j h d", j=TT, h=KV)).then_inc(A["v_ready"], 1)
                        for kind, k in core:
                            if kind == "PLACE" and k < NK:
                                dve.wait_ge(A["place_k"], NK * a + k + 1)
                                dve.tensor_tensor(KS[:, k, :], PS[:, 4 + k % 2, :], KX[:], ALU.add).then_inc(A["kz"], 1)
                            if kind == "S":
                                z, qt = divmod(k, TT)
                                dve.wait_ge(A["s"], 64 * a + k + 1)
                                dve.tensor_reduce(NM[:, qt, nm_column(z):nm_column(z) + 1], PS[:, k % 3, 0:P * (qt + 1)], AX.X, ALU.max,
                                                  negate=True).then_inc(A["smax"], 1)
                            if kind == "LN_STATS":
                                ln_stats_dve(dve, nb, g + 1)
                            if kind == "LN_NORM":
                                ln_norm_dve(dve, nb, g + 1, 1 - u)
                            if kind == "LN_T":
                                ln_lo_dve(dve, g + 1, 1 - u, (0, 1))
                            if kind == "SUMS":
                                dve.wait_ge(A["sums"], 4 * a + k + 1)
                                if k:
                                    dve.wait_ge(A["spread"], 4 * a + k)
                                dve.reciprocal(RECIP[:], PS[:, 7, 0:16]).then_inc(A["recip"], 1)
                                dve.wait_ge(A["recip"], 4 * a + k + 1)
                                dve.tensor_copy(r_wide(u), RECIP[:].unsqueeze(2).broadcast_to([P, TT * 4, 2 * HD])).then_inc(A["recip_wide"], 1)
                            if kind == "SPREAD":
                                dve.wait_ge(A["spread"], 4 * a + k + 1)
                                dve.tensor_tensor(YS[:, k % 2, :], YS[:, k % 2, :], PS[:, 7, :],
                                                  ALU.mult).then_inc(A["ctx"], 1)
                        if first_layer:
                            dve.wait_ge(A["bias"], a + 1)
                        for jj in range(2):
                            dve.wait_ge(A["o"], 2 * a + jj + 1)
                            xs = X[:, bass.ds(b * TT + 2 * jj, 2), :]
                            dve.tensor_tensor(xs, PS[:, 2 + 2 * jj:4 + 2 * jj, 0:D], xs, ALU.add).then_inc(A["x"], 1)

                @block.tensor
                def _(pe):
                    pe.wait_ge(A["w_lo"], 1)
                    for i, u, b, a, g in steps(pe):
                        xh, xl = XH[:, u, :, :], XL[:, u, :, :]

                        def w_cols(part, f, c0, n):
                            return W[:, part, f * COLS + c0:f * COLS + c0 + n]

                        def project(dst, c0, n):
                            for f in range(DH):
                                mm = three_passes(pe, dst, w_cols(0, f, c0, n), w_cols(1, f, c0, n), xh[:, f, :],
                                                  xl[:, f, :], f == 0, f == DH - 1)
                            return mm

                        pe.wait_ge(xl_ready, g * DH + DH)
                        pe.wait_ge(A["x"], ONE + 2 * a)
                        for n, tile in enumerate(TILE_ORDER):
                            if first_layer:
                                project(PS[:, n, :], tile * P, P).then_inc(A["proj"], 1)
                            else:
                                for sw in range(2):
                                    c0, w = (sw * D + tile * P, P) if tile < 2 else (K0 + sw * KV * HD, KV * HD)
                                    mm = project(PS[0:w, 2 * n + sw, :], c0, w)
                                mm.then_inc(A["proj"], 1)
                        pe.wait_ge(A["pv_copied"], ONE + 4 * a)
                        w = VH * HD
                        for j in range(TT):
                            tok = slice(j * P, (j + 1) * P)
                            dst = PS[:, 4 + j // 2, (j % 2) * w:(j % 2 + 1) * w] if first_layer else PS[:, 6, j * w:(j + 1) * w]
                            for f in range(DH):
                                mm = three_passes(pe, dst, xh[:, f, tok], xl[:, f, tok], w_cols(0, f, V0, w),
                                                  w_cols(1, f, V0, w), f == 0, f == DH - 1)
                            if not first_layer and j == TT - 1 or first_layer and j % 2:
                                mm.then_inc(A["v"], 1)
                        for kind, k in core:
                            if kind == "PLACE":
                                tl, cc = divmod(k, 4)
                                if cc == 0:
                                    pe.wait_ge(A["lo"], NI * a + (2 if tl == 0 else NI))
                                if k == 0:
                                    pe.wait_ge(A["v_ready"], NV * a + NV)
                                    pe.wait_ge(A["cast"], 64)
                                    pe.wait_ge(A["zero"], 3)
                                    pe.wait_ge(A["const"], N_CONST)
                                    pe.wait_ge(A["w_lo"], 2)
                                if k >= 2:
                                    pe.wait_ge(A["qz"], 16 * a + 2 * (k - 1))
                                pe.matmul(PS[:, 6 + k % 2, :], PLACE[:, 0, cc, :], QKH[:, tl, :], start=True, stop=False)
                                pe.matmul(PS[:, 6 + k % 2, :], PLACE[:, 1, cc, :], QKL[:, tl, :], start=False,
                                          stop=True).then_inc(A["place_q"], 1)
                                if k < NK:
                                    if k >= 2:
                                        pe.wait_ge(A["kz"], NK * a + k - 1)
                                    r, src = (P, 2 + tl) if first_layer else (KV * HD, 2)
                                    pe.matmul(PS[:, 4 + k % 2, :], PLACE[0:r, 2, cc, :], QKH[0:r, src, :], start=True, stop=False)
                                    pe.matmul(PS[:, 4 + k % 2, :], PLACE[0:r, 3, cc, :], QKL[0:r, src, :], start=False,
                                              stop=True).then_inc(A["place_k"], 1)
                            if kind == "S":
                                z, qt = divmod(k, TT)
                                if qt == 0:
                                    pe.wait_ge(A["qz"], 16 * a + z + 1)
                                    pe.wait_ge(A["kz"], NK * a + kidx(z) + 1)
                                if k == 2:
                                    pe.wait_ge(A["lo"], NI * a + NI)
                                tok = slice(qt * P, (qt + 1) * P)
                                if k >= 3:
                                    pe.wait_ge(A["smax"], ring(a, 64, k, 3))
                                pe.matmul(PS[:, k % 3, 0:P * (qt + 1)], QZ[:, z, tok],
                                          KS[:, kidx(z), 0:P * (qt + 1)], start=True, stop=False)
                                pe.matmul(PS[:, k % 3, tok], IDB[:], MKB[:], start=False, stop=True).then_inc(A["s"], 1)
                            if kind == "NMT":
                                pe.wait_ge(A["smax"], ONE + 64 * a + 16 * (k + 1))
                                pe.wait_ge(*bank7_read(a, (kind, k)))
                                for qt in range(TT):
                                    mm = pe.transpose(PS[0:4, 7, qt * P:(qt + 1) * P], NM[:, qt, 4 * k:4 * k + 4], IDENT[:])
                                mm.then_inc(A["mt"], 1)
                            if kind == "ST":
                                n, kt = divmod(k, TT)
                                if k == 0:
                                    pe.wait_ge(A["kz"], NK * a + NK)
                                if k % 8 == 0:
                                    pe.wait_ge(A["row"], ONE + 128 * a + 32 * (k // 8 + 1))
                                for zi in range(2):
                                    z, v = 2 * n + zi, 2 * k + zi
                                    if v >= 3:
                                        pe.wait_ge(A["exp"], ring(a, 64, v, 3))
                                    pe.matmul(PS[:, 3 + v % 3, 0:SEQ - P * kt], KS[:, kidx(z), kt * P:(kt + 1) * P],
                                              QZ[:, z, kt * P:SEQ], start=True, stop=False)
                                for v in (2 * k, 2 * k + 1):
                                    pe.matmul(PS[:, 3 + v % 3, 0:P], IDB[:], MTB[:], start=False,
                                              stop=True).then_inc(A["st"], 1)
                            if kind == "PV":
                                n, kt = divmod(k, TT)
                                pe.wait_ge(A["exp"], ONE + 64 * a + 2 * k + 2)
                                if k % 8 == 0:
                                    pe.wait_ge(A["pv_copied"], ONE + 4 * a + k // 8)
                                for zi in range(2):
                                    z = 2 * n + zi
                                    vh = z if first_layer else (z // 8) * 2 + z % 2
                                    rows = slice(32 * (z % 4), 32 * (z % 4) + 32)
                                    mm = pe.matmul(PS[rows, 6, kt * P:SEQ], V[:, kt, vh, :],
                                                   PT[:, n % 2, zi, TRI[kt]:TRI[kt + 1]], start=kt == 0,
                                                   stop=kt == TT - 1, tile_position=(0, rows.start))
                                if kt == TT - 1:
                                    mm.then_inc(A["pv"], 1)
                            if kind == "SUMS":
                                pe.wait_ge(A["pv_copied"], ONE + 4 * a + k + 1)
                                pe.wait_ge(*bank7_read(a, (kind, k)))
                                for j in range(TT):
                                    mm = pe.matmul(PS[:, 7, 4 * j:4 * j + 4], YS[:, k % 2, j * P:(j + 1) * P], PICK[:],
                                                   start=True, stop=True)
                                mm.then_inc(A["sums"], 1)
                            if kind == "SPREAD":
                                pe.wait_ge(*bank7_read(a, (kind, k)))
                                pe.wait_ge(A["recip_wide"], 4 * a + k + 1)
                                for j in range(TT):
                                    mm = pe.matmul(PS[:, 7, j * P:(j + 1) * P],
                                                   r_wide(u)[:, 4 * j:4 * j + 4, :].rearrange("p z r -> p (z r)"), IDENT[:],
                                                   start=True, stop=True)
                                mm.then_inc(A["spread"], 1)
                            if kind == "LN_T":
                                pe.wait_ge(A["smax"], ONE + 64 * a + 64)
                                ln_transpose_pe(pe, g + 1, 1 - u, (0, 1))
                            if kind == "OUT":
                                if k == 0:
                                    pe.wait_ge(A["exp"], ONE + 64 * a + 64)
                                pe.wait_ge(A["ctx_lo"], ONE + 4 * a + k + 1)
                                cols = slice(O0 + k * D, O0 + (k + 1) * D)
                                for j in range(TT):
                                    tok = slice(j * P, (j + 1) * P)
                                    mm = three_passes(pe, PS[:, 2 + j, 0:D], QKH[:, k, tok], QKL[:, k, tok],
                                                      W[:, 0, cols], W[:, 1, cols], k == 0, k == QUADS - 1)
                                    if k == QUADS - 1 and j % 2:
                                        mm.then_inc(A["o"], 1)

        def run(kinds, first_phase, WG=None, WD=None):
            for phase, kind in enumerate(kinds, first_phase):
                seen = PHASES[:phase].count(kind)
                e0 = BATCHES * sum(x in ("ffn", "moe") for x in PHASES[:phase])
                if kind == "ffn":
                    ffn_phase(phase, seen, WG, WD, e0)
                elif kind == "moe":
                    moe_phase(phase, seen, e0)
                else:
                    attn_phase(phase, kind == "attn0")

        lut_phases = max([n + 1 for n, x in enumerate(PHASES) if x == "ffn"], default=0)
        if not lut_phases:
            with nc.Block() as block:
                block.sync(start_sync)

                @block.gpsimd
                def _(pool):
                    start_pool(pool)
                    ln_rstd_pool(pool, 0)

                @block.vector
                def _(dve):
                    start_dve(dve)
                    first_stats_dve(dve)
                    ln_norm_dve(dve, 0, 0, 0)
                    ln_lo_dve(dve, 0, 0, (0, 1))

                @block.tensor
                def _(pe):
                    start_pe(pe)
                    ln_transpose_pe(pe, 0, 0, (0, 1))

                @block.scalar
                def _(act):
                    start_act(act)
                    load_x(act)
                    ln_hi_act(act, 0, 0, (0, 1))
        with ExitStack() as keep:
            if lut_phases:
                WG, WD = ffn_weights(keep)
                run(PHASES[:lut_phases], 0, WG, WD)
        run(PHASES[lut_phases:], lut_phases)

        with nc.Block() as block:
            @block.sync
            def _(sp):
                for b in range(BATCHES):
                    sp.dma_start(out[b].rearrange("(j p) d -> p j d", p=P),
                                 X[:, b * TT:(b + 1) * TT, :]).then_inc(stored, 16)
                sp.wait_ge(stored, 16 * BATCHES)


_INS = ["L0_attn_x", "L0_attn_Wqkv", "L0_attn_b_qkv", "L0_attn_Wout", "L0_attn_b_out", "L0_ffn_lut",
        "L0_ffn_gate_idx", "L0_ffn_up_idx", "L0_ffn_down_idx", "L1_attn_Wq", "L1_attn_Wk", "L1_attn_Wv",
        "L1_attn_Wproj", "L1_ffn_shared_w1", "L1_ffn_shared_b1", "L1_ffn_shared_w2", "L1_ffn_shared_b2",
        "L1_ffn_routed_w1", "L1_ffn_routed_b1", "L1_ffn_routed_w2", "L1_ffn_routed_b2", "L1_ffn_centroids",
        "L1_ffn_bias"]


def layouts(x):
    a = {}
    w1 = np.zeros((D, MT * P), np.float32)
    w2 = np.zeros((MT * P, D), np.float32)
    b1 = np.zeros(MT * P, np.float32)
    n_routed, n_shared = NR * EF, NS * EF
    w1[:, :n_routed] = x["L1_ffn_routed_w1"].transpose(1, 0, 2).reshape(D, -1)
    w1[:, n_routed:n_routed + n_shared] = x["L1_ffn_shared_w1"].transpose(1, 0, 2).reshape(D, -1)
    w2[:n_routed] = x["L1_ffn_routed_w2"].reshape(-1, D)
    w2[n_routed:n_routed + n_shared] = x["L1_ffn_shared_w2"].reshape(-1, D)
    b1[:n_routed] = x["L1_ffn_routed_b1"].reshape(-1)
    b1[n_routed:n_routed + n_shared] = x["L1_ffn_shared_b1"].reshape(-1)
    up = w1.reshape(DH, P, MT, P).transpose(2, 1, 0, 3).reshape(MT, P, DH * P)
    down = w2.reshape(MT, P, D)
    a["m_w"] = np.concatenate([up, down], -1)[MORDER]
    a["m_b1"] = b1.reshape(MT, P).T
    a["m_centroids"] = x["L1_ffn_centroids"].T.reshape(DH, P, NR).transpose(1, 0, 2)
    b2 = np.zeros((P, D), np.float32)
    b2[:NR] = b2[NR:2 * NR] = x["L1_ffn_routed_b2"]
    a["m_b2"] = b2
    a["m_bs2"] = x["L1_ffn_shared_b2"].reshape(NS, DH, P).transpose(2, 0, 1)
    a["L1_ffn_bias"] = x["L1_ffn_bias"]
    def out_rows(w_out, head):
        rows = np.zeros((4, 4, 2 * HD, D), np.float32)
        for z in range(HEADS):
            rows[z // 4, z % 4, :HD] = w_out[HD * head(z):HD * (head(z) + 1)]
        return rows.reshape(4, P, D).transpose(1, 0, 2).reshape(P, 4 * D)

    def qkv_columns(w):
        return w.reshape(DH, P, -1).transpose(1, 0, 2).reshape(P, -1)

    a["a0_w"] = np.concatenate([qkv_columns(x["L0_attn_Wqkv"].T), out_rows(x["L0_attn_Wout"].T, lambda z: z)], 1)
    a["a0_bqk"] = x["L0_attn_b_qkv"][:2 * D].reshape(4, P).T
    a["a0_bv"], a["a0_bo"] = x["L0_attn_b_qkv"][2 * D:], x["L0_attn_b_out"]
    wq = x["L1_attn_Wq"].reshape(D, 2, 2, 4, 2, HD // 2).transpose(0, 1, 3, 2, 4, 5)
    wk = x["L1_attn_Wk"].reshape(D, KV, 2, HD // 2)
    w = np.concatenate([wq.reshape(D, D), wq[..., ::-1, :].reshape(D, D), wk.reshape(D, -1),
                        wk[..., ::-1, :].reshape(D, -1), x["L1_attn_Wv"]], 1)
    a["a1_w"] = np.concatenate([qkv_columns(w), out_rows(x["L1_attn_Wproj"],
                                                         lambda z: 8 * (z // 8) + 4 * (z % 2) + z % 8 // 2)], 1)
    for n in ("L0_attn_x", "L0_ffn_lut", "L0_ffn_gate_idx", "L0_ffn_up_idx", "L0_ffn_down_idx"):
        a[n] = x[n]
    return {n: np.ascontiguousarray(v) for n, v in a.items()}


def kernel(**inputs):
    import concourse.bacc as bacc
    from concourse.bass_utils import run_bass_kernel_spmd

    nc = bacc.Bacc("TRN2", target_bir_lowering=False, num_devices=1)
    arrays = layouts({n: np.asarray(inputs[n]) for n in _INS})
    arrays.update(constants())
    t = {n: nc.dram_tensor("in_" + n, a.shape, mybir.dt.from_np(a.dtype), kind="ExternalInput").ap()
         for n, a in arrays.items()}
    shape = (BATCHES, SEQ, D)
    out = nc.dram_tensor("out_x", shape, F32, kind="ExternalOutput").ap()
    kernel_program(nc, t, out)
    r = run_bass_kernel_spmd(nc, [{"in_" + n: a for n, a in arrays.items()}], core_ids=[0])
    return r.results[0]["out_x"]
```
